# Optimizing a Trainium2 kernel written in Bass

```python
import numpy as np
import jax
import jax.numpy as jnp

def _softmax(x, axis=-1):
    return jax.nn.softmax(x, axis=axis)

def _gelu(x):
    return jax.nn.gelu(x, approximate=True)

def _silu(x):
    return jax.nn.silu(x)

def _sigmoid(x):
    return jax.nn.sigmoid(x)

def _layernorm(x, axis=-1, eps=1e-05):
    m = jnp.mean(x, axis=axis, keepdims=True)
    v = jnp.var(x, axis=axis, keepdims=True)
    return (x - m) / jnp.sqrt(v + eps)

def _scatter_add(tgt, idx, src, axis=0):
    return tgt.at[idx].add(src)

def _segment_sum(src, seg, n):
    return jax.ops.segment_sum(src, seg, n)
kernel_name = 'mk_flamingo_gated_d4_seqx_r4_967770'

def setup_inputs(seed: int=0):
    np.random.seed(seed)
    _w = jnp.asarray

    def _rec_inputs():
        import jax
        import jax.numpy as jnp
        _rk = jax.random.key(seed)
        x = -0.0005847 + 1 * jax.random.normal(jax.random.fold_in(_rk, 1), (16, 256, 256), jnp.float32)
        _lenS = 256 - jax.random.randint(jax.random.fold_in(_rk, 7), (16,), 0, max(1, 256 // 4) + 1, jnp.int32)
        _lenS2 = 77 - jax.random.randint(jax.random.fold_in(_rk, 8), (16,), 0, max(1, 77 // 4) + 1, jnp.int32)
        _ctx_1024P = jax.random.normal(jax.random.fold_in(_rk, 11), (16, 16, 256), jnp.float32)
        _ctx_1024c = jax.random.dirichlet(jax.random.fold_in(_rk, 511), 0.3 * jnp.ones((16,), jnp.float32), (16, 77))
        _ctx_1024t = jnp.einsum('bsk,bkd->bsd', _ctx_1024c, _ctx_1024P)
        _ctx_1024t = _ctx_1024t * jax.lax.rsqrt(jnp.mean(jnp.square(_ctx_1024t)) + 1e-12) * 0.953939
        ctx_1024 = 2.81802e-05 + 1.00001 * (_ctx_1024t + 0.3 * jax.random.normal(jax.random.fold_in(_rk, 611), (16, 77, 256), jnp.float32))
        _validS = jnp.arange(256)[None, :] < _lenS[:, None]
        _validS2 = jnp.arange(77)[None, :] < _lenS2[:, None]
        _causal = jnp.tril(jnp.ones((256, 256), dtype=bool))
        mask_BxS2_ik1 = jnp.where(jnp.broadcast_to(_validS2[:, :], (16, 77)), 1, 0).astype(jnp.int32)
        mask_Bx1xSxS2_ik1 = jnp.where(jnp.broadcast_to(_validS2[:, None, None, :], (16, 1, 256, 77)), 1, 0).astype(jnp.int32)
        _g = jax.random.normal(jax.random.fold_in(_rk, 9001), (2, 4), jnp.float32)
        _g = jnp.sign(_g) * jnp.maximum(jnp.abs(_g), 1.0) + (_g == 0) * 1.0
        g_xattn = _g[0]
        g_ffn = _g[1]
        return (x, ctx_1024, mask_BxS2_ik1, mask_Bx1xSxS2_ik1, g_xattn, g_ffn)
    x, ctx_1024, mask_BxS2_ik1, mask_Bx1xSxS2_ik1, g_xattn, g_ffn = _rec_inputs()

    def _L0_xattn_setup():
        import jax, jax.numpy as jnp
        import numpy as np
        DIM = 256
        NUM_HEADS = 16
        HEAD_DIM = DIM // NUM_HEADS
        SCALE = HEAD_DIM ** (-0.5)

        def _split_heads(x):
            B, L, _ = x.shape
            return x.reshape(B, L, NUM_HEADS, HEAD_DIM).transpose(0, 2, 1, 3)
        key = jax.random.key(seed)
        ks = jax.random.split(key, 12)
        B, Q, S = (4, 225, 1024)
        inp = {'query_vectors': jax.random.normal(ks[0], (B, Q, DIM), jnp.float32), 'key_input_flatten': jax.random.normal(ks[1], (B, S, DIM), jnp.float32), 'value_input_flatten': jax.random.normal(ks[2], (B, S, DIM), jnp.float32), 'attention_mask': jax.random.randint(ks[3], (B, S), 0, 2, jnp.int32), 'Wq': jax.random.normal(ks[4], (DIM, DIM), jnp.float32) * 0.02, 'bq': jnp.zeros((DIM,), jnp.float32), 'Wk': jax.random.normal(ks[5], (DIM, DIM), jnp.float32) * 0.02, 'bk': jnp.zeros((DIM,), jnp.float32), 'Wv': jax.random.normal(ks[6], (DIM, DIM), jnp.float32) * 0.02, 'bv': jnp.zeros((DIM,), jnp.float32), 'Wo': jax.random.normal(ks[7], (DIM, DIM), jnp.float32) * 0.02, 'bo': jnp.zeros((DIM,), jnp.float32)}
        return inp
    _L0_xattn_all = _L0_xattn_setup()
    _L0_xattn_in = {k: v for k, v in _L0_xattn_all.items() if k in ('Wq', 'bq', 'Wk', 'bk', 'Wv', 'bv', 'Wo', 'bo')}
    del _L0_xattn_all

    def _L0_ffn_setup():
        import jax, jax.numpy as jnp
        import numpy as np
        EMBED = 256
        HEADS = 16
        HEAD_DIM = EMBED // HEADS
        NUM_EXPERTS = 8
        TOP_K = 2
        HIDDEN = (int(2 * (4 * EMBED) / 3) + 63) // 64 * 64
        SEQ = 512
        BATCH = 2
        ROPE_BASE = 10000.0
        EPS = 1e-06

        def _rope_tables(seq_len, dim):
            inv_freq = 1.0 / ROPE_BASE ** (np.arange(0, dim, 2, dtype=np.float32) / dim)
            t = np.arange(seq_len, dtype=np.float32)
            freqs = np.einsum('i,j->ij', t, inv_freq)
            emb = np.concatenate([freqs, freqs], axis=-1)
            return (jnp.asarray(np.cos(emb)), jnp.asarray(np.sin(emb)))

        def _rotate_half(x):
            x1, x2 = jnp.split(x, 2, axis=-1)
            return jnp.concatenate([-x2, x1], axis=-1)

        def _rmsnorm(x, w):
            return x * jax.lax.rsqrt(jnp.mean(x * x, axis=-1, keepdims=True) + EPS) * w

        def _attention(x, wq, wk, wv, wo):
            B, S, _ = x.shape
            q = (x @ wq).reshape(B, S, HEADS, HEAD_DIM).transpose(0, 2, 1, 3)
            k = (x @ wk).reshape(B, S, HEADS, HEAD_DIM).transpose(0, 2, 1, 3)
            v = (x @ wv).reshape(B, S, HEADS, HEAD_DIM).transpose(0, 2, 1, 3)
            cos, sin = _rope_tables(S, HEAD_DIM)
            cos = cos[None, None]
            sin = sin[None, None]
            q = q * cos + _rotate_half(q) * sin
            k = k * cos + _rotate_half(k) * sin
            scale = HEAD_DIM ** (-0.5)
            scores = jnp.einsum('bhqd,bhkd->bhqk', q, k) * scale
            causal = jnp.triu(jnp.ones((S, S), bool), k=1)
            scores = jnp.where(causal, -jnp.inf, scores)
            attn = jax.nn.softmax(scores, axis=-1)
            out = jnp.einsum('bhqk,bhkd->bhqd', attn, v)
            out = out.transpose(0, 2, 1, 3).reshape(B, S, EMBED)
            return out @ wo

        def _moe(x, w_router, wg, wu, wd):
            B, S, E = x.shape
            xf = x.reshape(-1, E)
            logits = xf @ w_router
            probs = jax.nn.softmax(logits, axis=-1)
            topw, topi = jax.lax.top_k(probs, TOP_K)
            topw = topw / jnp.sum(topw, axis=-1, keepdims=True)
            combine = jnp.sum(jax.nn.one_hot(topi, NUM_EXPERTS, dtype=xf.dtype) * topw[..., None], axis=1)
            g = jax.nn.silu(jnp.einsum('td,xdh->txh', xf, wg))
            u = jnp.einsum('td,xdh->txh', xf, wu)
            eo = jnp.einsum('txh,xhd->txd', g * u, wd)
            out = jnp.einsum('txd,tx->td', eo, combine)
            return out.reshape(B, S, E)
        key = jax.random.key(seed)
        ks = jax.random.split(key, 12)
        s = 0.02
        return {'x': jax.random.normal(ks[0], (BATCH, SEQ, EMBED), jnp.float32), 'wq': jax.random.normal(ks[1], (EMBED, EMBED), jnp.float32) * s, 'wk': jax.random.normal(ks[2], (EMBED, EMBED), jnp.float32) * s, 'wv': jax.random.normal(ks[3], (EMBED, EMBED), jnp.float32) * s, 'wo': jax.random.normal(ks[4], (EMBED, EMBED), jnp.float32) * s, 'w_router': jax.random.normal(ks[5], (EMBED, NUM_EXPERTS), jnp.float32) * s, 'wg': jax.random.normal(ks[6], (NUM_EXPERTS, EMBED, HIDDEN), jnp.float32) * s, 'wu': jax.random.normal(ks[7], (NUM_EXPERTS, EMBED, HIDDEN), jnp.float32) * s, 'wd': jax.random.normal(ks[8], (NUM_EXPERTS, HIDDEN, EMBED), jnp.float32) * s, 'g1': jnp.ones((EMBED,), jnp.float32), 'g2': jnp.ones((EMBED,), jnp.float32)}
    _L0_ffn_all = _L0_ffn_setup()
    _L0_ffn_in = {k: v for k, v in _L0_ffn_all.items() if k in ('wq', 'wk', 'wv', 'wo', 'w_router', 'wg', 'wu', 'wd', 'g1', 'g2')}
    del _L0_ffn_all

    def _L1_xattn_setup():
        import jax, jax.numpy as jnp
        import numpy as np
        HEADS = 16
        DIM_HEAD = 64
        QUERY_DIM = 256
        CTX_DIM = 256
        INNER = HEADS * DIM_HEAD
        key = jax.random.key(seed)
        ks = jax.random.split(key, 7)
        B, N, M = (2, 512, 512)
        s = 0.02
        return {'x': jax.random.normal(ks[0], (B, N, QUERY_DIM), dtype=jnp.float32), 'context': jax.random.normal(ks[1], (B, M, CTX_DIM), dtype=jnp.float32), 'Wq': jax.random.normal(ks[2], (QUERY_DIM, INNER), dtype=jnp.float32) * s, 'Wk': jax.random.normal(ks[3], (CTX_DIM, INNER), dtype=jnp.float32) * s, 'Wv': jax.random.normal(ks[4], (CTX_DIM, INNER), dtype=jnp.float32) * s, 'Wo': jax.random.normal(ks[5], (INNER, QUERY_DIM), dtype=jnp.float32) * s, 'bo': jnp.zeros((QUERY_DIM,), dtype=jnp.float32)}
    _L1_xattn_all = _L1_xattn_setup()
    _L1_xattn_in = {k: v for k, v in _L1_xattn_all.items() if k in ('Wq', 'Wk', 'Wv', 'Wo', 'bo')}
    del _L1_xattn_all

    def _L1_ffn_setup():
        import jax, jax.numpy as jnp
        import numpy as np
        B, S, IN, OUT = (4, 2048, 256, 256)
        EPS = 1e-06

        def _xla_quantized_matmul(x2d, weight_q, weight_scale):
            amax = jnp.max(jnp.abs(x2d), axis=-1, keepdims=True)
            x_scale = jnp.maximum(amax, EPS) / 127.0
            x_q = jnp.clip(jnp.round(x2d / x_scale), -128, 127).astype(jnp.int8)
            acc = jax.lax.dot_general(x_q, weight_q, (((1,), (1,)), ((), ())), preferred_element_type=jnp.int32)
            return acc.astype(jnp.float32) * x_scale * weight_scale[None, :]
        key = jax.random.key(seed)
        k1, k2, k3, k4 = jax.random.split(key, 4)
        x = jax.random.normal(k1, (B, S, IN), dtype=jnp.float32)
        weight_q = jax.random.randint(k2, (OUT, IN), -128, 128, dtype=jnp.int32).astype(jnp.int8)
        weight_scale = jax.random.uniform(k3, (OUT,), dtype=jnp.float32, minval=0.001, maxval=0.01)
        bias = jax.random.normal(k4, (OUT,), dtype=jnp.float32) * 0.01
        return {'x': x, 'weight_q': weight_q, 'weight_scale': weight_scale, 'bias': bias}
    _L1_ffn_all = _L1_ffn_setup()
    _L1_ffn_in = {k: v for k, v in _L1_ffn_all.items() if k in ('weight_q', 'weight_scale', 'bias')}
    del _L1_ffn_all

    def _L2_xattn_setup():
        import jax, jax.numpy as jnp
        import numpy as np
        DIM = 256
        HEADS = 16
        HEAD_DIM = DIM // HEADS
        key = jax.random.key(seed)
        ks = jax.random.split(key, 12)
        B, Tq, Tk = (2, 512, 512)
        inp = {'query': jax.random.normal(ks[0], (B, Tq, DIM), jnp.float32), 'key': jax.random.normal(ks[1], (B, Tk, DIM), jnp.float32), 'value': jax.random.normal(ks[2], (B, Tk, DIM), jnp.float32), 'mask': jax.random.randint(ks[3], (B, 1, Tq, Tk), 0, 2, jnp.int32), 'wq': jax.random.uniform(ks[4], (DIM, DIM), jnp.float32, -1.0, 1.0) * np.sqrt(6.0 / (2 * DIM)), 'wk': jax.random.uniform(ks[5], (DIM, DIM), jnp.float32, -1.0, 1.0) * np.sqrt(6.0 / (2 * DIM)), 'wv': jax.random.uniform(ks[6], (DIM, DIM), jnp.float32, -1.0, 1.0) * np.sqrt(6.0 / (2 * DIM)), 'wo': jax.random.uniform(ks[7], (DIM, DIM), jnp.float32, -1.0, 1.0) * np.sqrt(6.0 / (2 * DIM)), 'bq': jnp.zeros((DIM,), jnp.float32), 'bk': jnp.zeros((DIM,), jnp.float32), 'bv': jnp.zeros((DIM,), jnp.float32), 'bo': jnp.zeros((DIM,), jnp.float32)}
        return inp
    _L2_xattn_all = _L2_xattn_setup()
    _L2_xattn_in = {k: v for k, v in _L2_xattn_all.items() if k in ('wq', 'wk', 'wv', 'wo', 'bq', 'bk', 'bv', 'bo')}
    del _L2_xattn_all

    def _L2_ffn_setup():
        import jax, jax.numpy as jnp
        import numpy as np
        B, T, C, H, E = (4, 512, 256, 512, 8)
        CAPACITY_FACTOR = 1.0
        key = jax.random.key(seed)
        ks = jax.random.split(key, 5)
        scale = 0.02
        return {'x': jax.random.normal(ks[0], (B, T, C), dtype=jnp.float32), 'Wg': jax.random.normal(ks[1], (E, C), dtype=jnp.float32) * scale, 'W1': jax.random.normal(ks[2], (E, H, C), dtype=jnp.float32) * scale, 'W2': jax.random.normal(ks[3], (E, C, H), dtype=jnp.float32) * scale, 'W3': jax.random.normal(ks[4], (E, H, C), dtype=jnp.float32) * scale}
    _L2_ffn_all = _L2_ffn_setup()
    _L2_ffn_in = {k: v for k, v in _L2_ffn_all.items() if k in ('Wg', 'W1', 'W2', 'W3')}
    del _L2_ffn_all

    def _L3_xattn_setup():
        import jax, jax.numpy as jnp
        import numpy as np
        DIM = 256
        CTX_DIM = 256
        HEADS = 16
        DIM_HEAD = 64
        INNER = HEADS * DIM_HEAD
        FF_INNER = 4 * DIM
        EPS = 1e-05

        def layer_norm(x, g, b):
            mu = jnp.mean(x, axis=-1, keepdims=True)
            var = jnp.var(x, axis=-1, keepdims=True)
            return (x - mu) * jax.lax.rsqrt(var + EPS) * g + b
        key = jax.random.key(seed)
        ks = jax.random.split(key, 9)
        b, n, j = (4, 512, 256)
        inp = {'x': jax.random.normal(ks[0], (b, n, DIM), dtype=jnp.float32), 'context': jax.random.normal(ks[1], (b, j, CTX_DIM), dtype=jnp.float32), 'ln_g': jnp.ones((DIM,), jnp.float32), 'ln_b': jnp.zeros((DIM,), jnp.float32), 'cln_g': jnp.ones((CTX_DIM,), jnp.float32), 'cln_b': jnp.zeros((CTX_DIM,), jnp.float32), 'Wq': jax.random.normal(ks[2], (DIM, INNER), dtype=jnp.float32) * DIM ** (-0.5), 'Wkv': jax.random.normal(ks[3], (CTX_DIM, 2 * DIM_HEAD), dtype=jnp.float32) * CTX_DIM ** (-0.5), 'Wo': jax.random.normal(ks[4], (INNER, DIM), dtype=jnp.float32) * INNER ** (-0.5), 'Wff1': jax.random.normal(ks[5], (DIM, 2 * FF_INNER), dtype=jnp.float32) * DIM ** (-0.5), 'Wff2': jax.random.normal(ks[6], (FF_INNER, DIM), dtype=jnp.float32) * FF_INNER ** (-0.5)}
        return inp
    _L3_xattn_all = _L3_xattn_setup()
    _L3_xattn_in = {k: v for k, v in _L3_xattn_all.items() if k in ('ln_g', 'ln_b', 'cln_g', 'cln_b', 'Wq', 'Wkv', 'Wo', 'Wff1', 'Wff2')}
    del _L3_xattn_all

    def _L3_ffn_setup():
        import jax, jax.numpy as jnp
        import numpy as np
        B, S, K, N = (8, 2048, 256, 256)
        key = jax.random.key(seed)
        k1, k2, k3, k4 = jax.random.split(key, 4)
        x = jax.random.normal(k1, (B, S, K), dtype=jnp.float32)
        CB = jnp.clip(jnp.round(jax.random.normal(k2, (N, K), dtype=jnp.float32) * 42.0), -127.0, 127.0)
        SCB = jax.random.uniform(k3, (N,), dtype=jnp.float32, minval=0.5, maxval=2.0)
        bias = jax.random.normal(k4, (N,), dtype=jnp.float32) * 0.02
        return {'x': x, 'CB': CB, 'SCB': SCB, 'bias': bias}
    _L3_ffn_all = _L3_ffn_setup()
    _L3_ffn_in = {k: v for k, v in _L3_ffn_all.items() if k in ('CB', 'SCB', 'bias')}
    del _L3_ffn_all
    return {'x': x, 'ctx_1024': ctx_1024, 'mask_BxS2_ik1': mask_BxS2_ik1, 'mask_Bx1xSxS2_ik1': mask_Bx1xSxS2_ik1, 'g_xattn': g_xattn, 'g_ffn': g_ffn, 'L0_xattn_Wq': _L0_xattn_in['Wq'], 'L0_xattn_bq': _L0_xattn_in['bq'], 'L0_xattn_Wk': _L0_xattn_in['Wk'], 'L0_xattn_bk': _L0_xattn_in['bk'], 'L0_xattn_Wv': _L0_xattn_in['Wv'], 'L0_xattn_bv': _L0_xattn_in['bv'], 'L0_xattn_Wo': _L0_xattn_in['Wo'], 'L0_xattn_bo': _L0_xattn_in['bo'], 'L0_ffn_wq': _L0_ffn_in['wq'], 'L0_ffn_wk': _L0_ffn_in['wk'], 'L0_ffn_wv': _L0_ffn_in['wv'], 'L0_ffn_wo': _L0_ffn_in['wo'], 'L0_ffn_w_router': _L0_ffn_in['w_router'], 'L0_ffn_wg': _L0_ffn_in['wg'], 'L0_ffn_wu': _L0_ffn_in['wu'], 'L0_ffn_wd': _L0_ffn_in['wd'], 'L0_ffn_g1': _L0_ffn_in['g1'], 'L0_ffn_g2': _L0_ffn_in['g2'], 'L1_xattn_Wq': _L1_xattn_in['Wq'], 'L1_xattn_Wk': _L1_xattn_in['Wk'], 'L1_xattn_Wv': _L1_xattn_in['Wv'], 'L1_xattn_Wo': _L1_xattn_in['Wo'], 'L1_xattn_bo': _L1_xattn_in['bo'], 'L1_ffn_weight_q': _L1_ffn_in['weight_q'], 'L1_ffn_weight_scale': _L1_ffn_in['weight_scale'], 'L1_ffn_bias': _L1_ffn_in['bias'], 'L2_xattn_wq': _L2_xattn_in['wq'], 'L2_xattn_wk': _L2_xattn_in['wk'], 'L2_xattn_wv': _L2_xattn_in['wv'], 'L2_xattn_wo': _L2_xattn_in['wo'], 'L2_xattn_bq': _L2_xattn_in['bq'], 'L2_xattn_bk': _L2_xattn_in['bk'], 'L2_xattn_bv': _L2_xattn_in['bv'], 'L2_xattn_bo': _L2_xattn_in['bo'], 'L2_ffn_Wg': _L2_ffn_in['Wg'], 'L2_ffn_W1': _L2_ffn_in['W1'], 'L2_ffn_W2': _L2_ffn_in['W2'], 'L2_ffn_W3': _L2_ffn_in['W3'], 'L3_xattn_ln_g': _L3_xattn_in['ln_g'], 'L3_xattn_ln_b': _L3_xattn_in['ln_b'], 'L3_xattn_cln_g': _L3_xattn_in['cln_g'], 'L3_xattn_cln_b': _L3_xattn_in['cln_b'], 'L3_xattn_Wq': _L3_xattn_in['Wq'], 'L3_xattn_Wkv': _L3_xattn_in['Wkv'], 'L3_xattn_Wo': _L3_xattn_in['Wo'], 'L3_xattn_Wff1': _L3_xattn_in['Wff1'], 'L3_xattn_Wff2': _L3_xattn_in['Wff2'], 'L3_ffn_CB': _L3_ffn_in['CB'], 'L3_ffn_SCB': _L3_ffn_in['SCB'], 'L3_ffn_bias': _L3_ffn_in['bias']}

def reference(x, ctx_1024, mask_BxS2_ik1, mask_Bx1xSxS2_ik1, g_xattn, g_ffn, L0_xattn_Wq, L0_xattn_bq, L0_xattn_Wk, L0_xattn_bk, L0_xattn_Wv, L0_xattn_bv, L0_xattn_Wo, L0_xattn_bo, L0_ffn_wq, L0_ffn_wk, L0_ffn_wv, L0_ffn_wo, L0_ffn_w_router, L0_ffn_wg, L0_ffn_wu, L0_ffn_wd, L0_ffn_g1, L0_ffn_g2, L1_xattn_Wq, L1_xattn_Wk, L1_xattn_Wv, L1_xattn_Wo, L1_xattn_bo, L1_ffn_weight_q, L1_ffn_weight_scale, L1_ffn_bias, L2_xattn_wq, L2_xattn_wk, L2_xattn_wv, L2_xattn_wo, L2_xattn_bq, L2_xattn_bk, L2_xattn_bv, L2_xattn_bo, L2_ffn_Wg, L2_ffn_W1, L2_ffn_W2, L2_ffn_W3, L3_xattn_ln_g, L3_xattn_ln_b, L3_xattn_cln_g, L3_xattn_cln_b, L3_xattn_Wq, L3_xattn_Wkv, L3_xattn_Wo, L3_xattn_Wff1, L3_xattn_Wff2, L3_ffn_CB, L3_ffn_SCB, L3_ffn_bias):
    import jax
    import jax.numpy as jnp

    def _L0_xattn_ref(query_vectors, key_input_flatten, value_input_flatten, attention_mask, Wq, bq, Wk, bk, Wv, bv, Wo, bo):
        import jax, jax.numpy as jnp
        import numpy as np
        DIM = 256
        NUM_HEADS = 16
        HEAD_DIM = DIM // NUM_HEADS
        SCALE = HEAD_DIM ** (-0.5)

        def _split_heads(x):
            B, L, _ = x.shape
            return x.reshape(B, L, NUM_HEADS, HEAD_DIM).transpose(0, 2, 1, 3)
        B, Q, D = query_vectors.shape
        q = _split_heads(query_vectors @ Wq.T + bq) * SCALE
        k = _split_heads(key_input_flatten @ Wk.T + bk)
        v = _split_heads(value_input_flatten @ Wv.T + bv)
        scores = jnp.einsum('bhqd,bhsd->bhqs', q, k)
        scores = scores + attention_mask.astype(scores.dtype)[:, None, None, :] * -100.0
        probs = jax.nn.softmax(scores, axis=-1)
        ctx = jnp.einsum('bhqs,bhsd->bhqd', probs, v)
        ctx = ctx.transpose(0, 2, 1, 3).reshape(B, Q, D)
        return ctx @ Wo.T + bo

    def _L0_ffn_ref(x, wq, wk, wv, wo, w_router, wg, wu, wd, g1, g2):
        import jax, jax.numpy as jnp
        import numpy as np
        EMBED = 256
        HEADS = 16
        HEAD_DIM = EMBED // HEADS
        NUM_EXPERTS = 8
        TOP_K = 2
        HIDDEN = (int(2 * (4 * EMBED) / 3) + 63) // 64 * 64
        SEQ = 512
        BATCH = 2
        ROPE_BASE = 10000.0
        EPS = 1e-06

        def _rope_tables(seq_len, dim):
            inv_freq = 1.0 / ROPE_BASE ** (np.arange(0, dim, 2, dtype=np.float32) / dim)
            t = np.arange(seq_len, dtype=np.float32)
            freqs = np.einsum('i,j->ij', t, inv_freq)
            emb = np.concatenate([freqs, freqs], axis=-1)
            return (jnp.asarray(np.cos(emb)), jnp.asarray(np.sin(emb)))

        def _rotate_half(x):
            x1, x2 = jnp.split(x, 2, axis=-1)
            return jnp.concatenate([-x2, x1], axis=-1)

        def _rmsnorm(x, w):
            return x * jax.lax.rsqrt(jnp.mean(x * x, axis=-1, keepdims=True) + EPS) * w

        def _attention(x, wq, wk, wv, wo):
            B, S, _ = x.shape
            q = (x @ wq).reshape(B, S, HEADS, HEAD_DIM).transpose(0, 2, 1, 3)
            k = (x @ wk).reshape(B, S, HEADS, HEAD_DIM).transpose(0, 2, 1, 3)
            v = (x @ wv).reshape(B, S, HEADS, HEAD_DIM).transpose(0, 2, 1, 3)
            cos, sin = _rope_tables(S, HEAD_DIM)
            cos = cos[None, None]
            sin = sin[None, None]
            q = q * cos + _rotate_half(q) * sin
            k = k * cos + _rotate_half(k) * sin
            scale = HEAD_DIM ** (-0.5)
            scores = jnp.einsum('bhqd,bhkd->bhqk', q, k) * scale
            causal = jnp.triu(jnp.ones((S, S), bool), k=1)
            scores = jnp.where(causal, -jnp.inf, scores)
            attn = jax.nn.softmax(scores, axis=-1)
            out = jnp.einsum('bhqk,bhkd->bhqd', attn, v)
            out = out.transpose(0, 2, 1, 3).reshape(B, S, EMBED)
            return out @ wo

        def _moe(x, w_router, wg, wu, wd):
            B, S, E = x.shape
            xf = x.reshape(-1, E)
            logits = xf @ w_router
            probs = jax.nn.softmax(logits, axis=-1)
            topw, topi = jax.lax.top_k(probs, TOP_K)
            topw = topw / jnp.sum(topw, axis=-1, keepdims=True)
            combine = jnp.sum(jax.nn.one_hot(topi, NUM_EXPERTS, dtype=xf.dtype) * topw[..., None], axis=1)
            g = jax.nn.silu(jnp.einsum('td,xdh->txh', xf, wg))
            u = jnp.einsum('td,xdh->txh', xf, wu)
            eo = jnp.einsum('txh,xhd->txd', g * u, wd)
            out = jnp.einsum('txd,tx->td', eo, combine)
            return out.reshape(B, S, E)
        h = x + _attention(_rmsnorm(x, g1), wq, wk, wv, wo)
        y = h + _moe(_rmsnorm(h, g2), w_router, wg, wu, wd)
        return y

    def _L1_xattn_ref(x, context, Wq, Wk, Wv, Wo, bo):
        import jax, jax.numpy as jnp
        import numpy as np
        HEADS = 16
        DIM_HEAD = 64
        QUERY_DIM = 256
        CTX_DIM = 256
        INNER = HEADS * DIM_HEAD
        B, N, _ = x.shape
        M = context.shape[1]
        scale = DIM_HEAD ** (-0.5)
        q = (x @ Wq).reshape(B, N, HEADS, DIM_HEAD).transpose(0, 2, 1, 3)
        k = (context @ Wk).reshape(B, M, HEADS, DIM_HEAD).transpose(0, 2, 1, 3)
        v = (context @ Wv).reshape(B, M, HEADS, DIM_HEAD).transpose(0, 2, 1, 3)
        sim = jnp.einsum('bhid,bhjd->bhij', q, k) * scale
        attn = jax.nn.softmax(sim, axis=-1)
        out = jnp.einsum('bhij,bhjd->bhid', attn, v)
        out = out.transpose(0, 2, 1, 3).reshape(B, N, INNER)
        return out @ Wo + bo

    def _L1_ffn_ref(x, weight_q, weight_scale, bias):
        import jax, jax.numpy as jnp
        import numpy as np
        B, S, IN, OUT = (4, 2048, 256, 256)
        EPS = 1e-06

        def _xla_quantized_matmul(x2d, weight_q, weight_scale):
            amax = jnp.max(jnp.abs(x2d), axis=-1, keepdims=True)
            x_scale = jnp.maximum(amax, EPS) / 127.0
            x_q = jnp.clip(jnp.round(x2d / x_scale), -128, 127).astype(jnp.int8)
            acc = jax.lax.dot_general(x_q, weight_q, (((1,), (1,)), ((), ())), preferred_element_type=jnp.int32)
            return acc.astype(jnp.float32) * x_scale * weight_scale[None, :]
        orig_shape = x.shape
        x2d = x.reshape(-1, orig_shape[-1])
        out = _xla_quantized_matmul(x2d, weight_q, weight_scale)
        out = out.reshape(*orig_shape[:-1], out.shape[-1])
        out = out + bias
        return out

    def _L2_xattn_ref(query, key, value, mask, wq, wk, wv, wo, bq, bk, bv, bo):
        import jax, jax.numpy as jnp
        import numpy as np
        DIM = 256
        HEADS = 16
        HEAD_DIM = DIM // HEADS
        B, Tq, C = query.shape
        Tk = key.shape[1]
        scale = 1.0 / np.sqrt(HEAD_DIM)
        q = (query @ wq.T + bq).reshape(B, Tq, HEADS, HEAD_DIM).transpose(0, 2, 1, 3)
        k = (key @ wk.T + bk).reshape(B, Tk, HEADS, HEAD_DIM).transpose(0, 2, 1, 3)
        v = (value @ wv.T + bv).reshape(B, Tk, HEADS, HEAD_DIM).transpose(0, 2, 1, 3)
        scores = jnp.einsum('bhqd,bhkd->bhqk', q, k) * scale
        scores = jnp.clip(scores, -100.0, 100.0)
        scores = jnp.where(mask == 0, -jnp.inf, scores)
        attn = jax.nn.softmax(scores, axis=-1)
        out = jnp.einsum('bhqk,bhkd->bhqd', attn, v)
        out = out.transpose(0, 2, 1, 3).reshape(B, Tq, HEADS * HEAD_DIM)
        return out @ wo.T + bo

    def _L2_ffn_ref(x, Wg, W1, W2, W3):
        import jax, jax.numpy as jnp
        import numpy as np
        B, T, C, H, E = (4, 512, 256, 512, 8)
        CAPACITY_FACTOR = 1.0
        b, t, c = x.shape
        e = Wg.shape[0]
        n = b * t
        capacity = max(1, int(CAPACITY_FACTOR * n / e))
        x_flat = x.reshape(n, c)
        scores = (x_flat @ Wg.T).T
        top_vals, token_idx = jax.lax.top_k(scores, capacity)
        token_w = jax.nn.softmax(top_vals, axis=-1)
        xg = x_flat[token_idx]
        h = jax.nn.silu(jnp.einsum('eic,ehc->eih', xg, W1)) * jnp.einsum('eic,ehc->eih', xg, W3)
        y = jnp.einsum('eih,ech->eic', h, W2) * token_w[..., None]
        out = jnp.zeros_like(x_flat).at[token_idx.reshape(-1)].add(y.reshape(-1, c))
        return out.reshape(b, t, c)

    def _L3_xattn_ref(x, context, ln_g, ln_b, cln_g, cln_b, Wq, Wkv, Wo, Wff1, Wff2):
        import jax, jax.numpy as jnp
        import numpy as np
        DIM = 256
        CTX_DIM = 256
        HEADS = 16
        DIM_HEAD = 64
        INNER = HEADS * DIM_HEAD
        FF_INNER = 4 * DIM
        EPS = 1e-05

        def layer_norm(x, g, b):
            mu = jnp.mean(x, axis=-1, keepdims=True)
            var = jnp.var(x, axis=-1, keepdims=True)
            return (x - mu) * jax.lax.rsqrt(var + EPS) * g + b
        scale = DIM_HEAD ** (-0.5)
        xn = layer_norm(x, ln_g, ln_b)
        cn = layer_norm(context, cln_g, cln_b)
        b, n, _ = xn.shape
        q = (xn @ Wq).reshape(b, n, HEADS, DIM_HEAD).transpose(0, 2, 1, 3) * scale
        kv = cn @ Wkv
        k, v = (kv[..., :DIM_HEAD], kv[..., DIM_HEAD:])
        sim = jnp.einsum('bhid,bjd->bhij', q, k)
        attn = jax.nn.softmax(sim, axis=-1)
        out = jnp.einsum('bhij,bjd->bhid', attn, v)
        out = out.transpose(0, 2, 1, 3).reshape(b, n, INNER) @ Wo
        ff = xn @ Wff1
        h, gate = (ff[..., :FF_INNER], ff[..., FF_INNER:])
        out = out + jax.nn.silu(gate) * h @ Wff2
        return out

    def _L3_ffn_ref(x, CB, SCB, bias):
        import jax, jax.numpy as jnp
        import numpy as np
        B, S, K, N = (8, 2048, 256, 256)
        out = jnp.einsum('bsk,nk->bsn', x, CB)
        out = out * (SCB * (1.0 / 127.0)) + bias
        return out
    x = x + jnp.tanh(g_xattn[0]) * _L0_xattn_ref(_layernorm(x, axis=-1), ctx_1024, ctx_1024, mask_BxS2_ik1, L0_xattn_Wq, L0_xattn_bq, L0_xattn_Wk, L0_xattn_bk, L0_xattn_Wv, L0_xattn_bv, L0_xattn_Wo, L0_xattn_bo)
    x = x + jnp.tanh(g_ffn[0]) * _L0_ffn_ref(_layernorm(x, axis=-1), L0_ffn_wq, L0_ffn_wk, L0_ffn_wv, L0_ffn_wo, L0_ffn_w_router, L0_ffn_wg, L0_ffn_wu, L0_ffn_wd, L0_ffn_g1, L0_ffn_g2)
    x = x + jnp.tanh(g_xattn[1]) * _L1_xattn_ref(_layernorm(x, axis=-1), ctx_1024, L1_xattn_Wq, L1_xattn_Wk, L1_xattn_Wv, L1_xattn_Wo, L1_xattn_bo)
    x = x + jnp.tanh(g_ffn[1]) * _L1_ffn_ref(_layernorm(x, axis=-1), L1_ffn_weight_q, L1_ffn_weight_scale, L1_ffn_bias)
    x = x + jnp.tanh(g_xattn[2]) * _L2_xattn_ref(_layernorm(x, axis=-1), ctx_1024, ctx_1024, mask_Bx1xSxS2_ik1, L2_xattn_wq, L2_xattn_wk, L2_xattn_wv, L2_xattn_wo, L2_xattn_bq, L2_xattn_bk, L2_xattn_bv, L2_xattn_bo)
    x = x + jnp.tanh(g_ffn[2]) * _L2_ffn_ref(_layernorm(x, axis=-1), L2_ffn_Wg, L2_ffn_W1, L2_ffn_W2, L2_ffn_W3)
    x = x + jnp.tanh(g_xattn[3]) * _L3_xattn_ref(_layernorm(x, axis=-1), ctx_1024, L3_xattn_ln_g, L3_xattn_ln_b, L3_xattn_cln_g, L3_xattn_cln_b, L3_xattn_Wq, L3_xattn_Wkv, L3_xattn_Wo, L3_xattn_Wff1, L3_xattn_Wff2)
    x = x + jnp.tanh(g_ffn[3]) * _L3_ffn_ref(_layernorm(x, axis=-1), L3_ffn_CB, L3_ffn_SCB, L3_ffn_bias)
    return x

_drawn_inputs = setup_inputs


def setup_inputs(seed=0):
    import zlib

    import numpy as np

    out = dict(_drawn_inputs(seed))
    spreads = {'L0_xattn_bq': (0.0, 0.8),
     'L0_xattn_bk': (0.0, 2.0),
     'L0_xattn_bv': (0.0, 0.278),
     'L0_xattn_bo': (0.0, 0.1),
     'L0_ffn_g1': (1.0, 0.6),
     'L0_ffn_g2': (1.0, 0.2),
     'L1_xattn_bo': (0.0, 0.1),
     'L2_xattn_bq': (0.0, 2.0),
     'L2_xattn_bk': (0.0, 2.0),
     'L2_xattn_bv': (0.0, 0.703),
     'L2_xattn_bo': (0.0, 0.668),
     'L3_xattn_ln_g': (1.0, 0.6),
     'L3_xattn_ln_b': (0.0, 2.0),
     'L3_xattn_cln_g': (1.0, 0.6),
     'L3_xattn_cln_b': (0.0, 2.0)}
    factors = {'L0_xattn_Wq': 8.0,
     'L0_xattn_Wk': 8.0,
     'L0_ffn_wq': 7.204,
     'L0_ffn_wk': 7.15,
     'L1_xattn_Wq': 3.525,
     'L1_xattn_Wk': 3.531,
     'L1_ffn_bias': 46.096,
     'L2_ffn_Wg': 33.181,
     'L2_ffn_W1': 42.482,
     'L2_ffn_W2': 36.91,
     'L2_ffn_W3': 38.061,
     'L3_ffn_bias': 200.0,
     'g_ffn': 3.816,
     'L3_xattn_Wq': 5.122,
     'L3_xattn_Wkv': 2.777,
     'L3_xattn_Wo': 2.702}
    for name, (base, spread) in spreads.items():
        noise = np.random.default_rng([zlib.crc32(name.encode()), seed]).standard_normal(out[name].shape)
        drawn = base * np.exp(spread * noise) if base else spread * noise
        out[name] = jnp.asarray(drawn.astype(out[name].dtype))
    for name, factor in factors.items():
        out[name] = (out[name] * factor).astype(out[name].dtype)
    return out
```

```python
from contextlib import ExitStack, contextmanager

import numpy as np

import concourse.bass as bass
from concourse import mybir

F32 = mybir.dt.float32
F16 = mybir.dt.float16
I32 = mybir.dt.int32
U32 = mybir.dt.uint32
ALU = mybir.AluOpType
ACT = mybir.ActivationFunctionType
AX = mybir.AxisListType

P = 128
BATCH, SEQ, DIM = 16, 256, 256
KEYS = 77
TOKENS = BATCH * SEQ
TILES = TOKENS // P
DC = DIM // P
HEADS = 16
W_SCALE = 16.0
ARENAS = (8192, 4624)
STAGED = 512
CLIP = 100.0
NEG_BIG = -1.0e30
LN_EPS = 1e-5
RMS_EPS = 1e-6


class At:

    def __init__(self, i, off, n):
        self.i, self.off, self.n = i, off, n

    def __add__(self, k):
        return At(self.i, self.off + k, self.n)

    def valid(self):
        return self.i is not None or 0 <= self.off < self.n

    def count(self, per, plus):
        if self.i is None:
            return per * self.off + plus
        assert per * (2 + self.off) + plus > 0, (per, self.off, plus)
        return self.i * (2 * per) + (per * self.off + plus)


def wait(eng, sem, value):
    if isinstance(value, int) and value <= 0:
        return
    eng.wait_ge(sem, value)


@contextmanager
def stage_semaphores(nc, tag):
    sems = []

    def new(name):
        sems.append(nc.alloc_semaphore(f"{tag}_{name}"))
        return sems[-1]

    yield new
    nc.clear_and_free_semaphores(sems)
    nc.all_engine_barrier()


def over_steps(eng, nu, fns, n=BATCH):
    def body(b):
        for j in range(nu):
            for fn in fns:
                for db in (-1, 0, 1, 2):
                    if (b + db).valid():
                        fn(b + db, j - db * nu)

    for b in (-2, -1, 0, 1):
        body(At(None, b, n))
    with eng.Fori(1, n // 2 - 1) as i:
        body(At(i, 0, n))
        body(At(i, 1, n))
    for b in (n - 2, n - 1, n):
        body(At(None, b, n))


class Core:
    pass


def setup_core(nc, ctx, dram):
    c = Core()
    c.nc, c.dram = nc, dram

    def sb(name, shape, dt):
        return ctx.enter_context(nc.sbuf_tensor(name, shape, dt))

    c.x = sb("x_resident", [P, TILES, DIM], F32)
    c.h = sb("h_resident", [P, TILES, DIM], F32)
    c.ct = [sb(f"ctx_T_{p}", [P, DC, BATCH * KEYS], F16) for p in ("hi", "lo")]
    c.arena = [sb(f"weights_{i}", [P, 2, n], F16) for i, n in enumerate(ARENAS)]
    c.rows = [sb(f"bias_rows_{i}", [2, 4 * DIM], F16) for i in range(2)]
    c.ident = sb("ident", [P, P], F32)
    c.ident_h = sb("ident_h", [P, P], F16)
    c.ones_rows = sb("ones_rows", [2, P], F16)
    c.w_scale = sb("w_scale", [P, 1], F32)
    c.gates = sb("gates", [P, 8], F32)
    c.gates_w = sb("gates_w", [P, 8], F32)
    c.rstd1 = sb("rstd_first", [P, TILES], F32)
    c.tmp_a = sb("norm_tmp", [P, TILES], F32)
    c.w_stage = sb("w_stage", [P, 2, STAGED], F32)
    c.w_scaled = sb("w_scaled", [P, STAGED], F32)
    c.row_raw = sb("row_raw", [1, 4 * DIM], F32)
    c.row_lo = sb("row_lo", [1, 4 * DIM], F16)
    c.ct_now = c.ct
    c.stats = sb("stats", [P, TILES, 6], F32)
    c.mv = sb("mean_var", [P, TILES, 2], F32)
    c.rstd = sb("rstd", [P, TILES], F32)
    c.consts = sb("consts", [P, 8], F32)
    c.bank = [ctx.enter_context(nc.psum_tensor(f"bank{i}", [P, 512], F32)) for i in range(8)]
    return c


def prepare(nc, c, names):
    with ExitStack() as ctx:
        cx = ctx.enter_context(nc.sbuf_tensor("ctx_rows", [KEYS, BATCH, DIM], F32))
        graw = ctx.enter_context(nc.sbuf_tensor("gates_raw", [P, 8], F32))
        sem = ctx.enter_context(stage_semaphores(nc, "prepare"))
        loaded_x, loaded_ctx, loaded_g = sem("loaded_x"), sem("loaded_ctx"), sem("loaded_g")
        const, selected = sem("const"), sem("selected")
        full, hi_done, free = sem("full"), sem("hi_done"), sem("free")
        block = ctx.enter_context(nc.Block())
        groups = DC * BATCH // 4

        @block.sync
        def _(sp):
            sp.dma_start(cx[:], c.dram["ctx_1024"].rearrange("b k d -> k b d")).then_inc(loaded_ctx, 16)
            sp.dma_start(graw[:, 0:4], c.dram["g_xattn"].partition_broadcast(P)).then_inc(loaded_g, 16)
            sp.dma_start(graw[:, 4:8], c.dram["g_ffn"].partition_broadcast(P)).then_inc(loaded_g, 16)
            sp.dma_start(c.x[:], c.dram["x"].rearrange("b (t p) d -> p (b t) d", p=P)).then_inc(loaded_x, 16)
            sp.wait_ge(loaded_x, 16)

        @block.gpsimd
        def _(pool):
            nc.gpsimd.memset(c.ident[:], 0.0).then_inc(const, 1)
            nc.gpsimd.memset(c.ident_h[:], 0.0).then_inc(const, 1)
            pool.wait_ge(const, 2)
            for m in (c.ident, c.ident_h):
                nc.gpsimd.affine_select(out=m[:], in_=m[:], compare_op=ALU.not_equal, fill=1.0, base=0,
                                        pattern=[[-1, P]], channel_multiplier=1).then_inc(selected, 1)
            nc.gpsimd.memset(c.ones_rows[:], 1.0).then_inc(const, 1)
            nc.gpsimd.memset(c.w_scale[:], W_SCALE).then_inc(const, 1)
            for i, v in enumerate((LN_EPS, -0.5, RMS_EPS, 1.0)):
                nc.gpsimd.memset(c.consts[:, i:i + 1], v).then_inc(const, 1)
            pool.wait_ge(const, 8)
            prep_weights(nc, c, pool, c.first_weights)

        @block.tensor
        def _(pe):
            pe.wait_ge(selected, 2)
            pe.wait_ge(loaded_ctx, 16)
            for g in range(groups):
                d, b0 = g % DC, g // DC * 4
                wait(pe, free, g - 1)
                for j in range(4):
                    last = nc.tensor.transpose(c.bank[g % 2][:, j * KEYS:(j + 1) * KEYS],
                                               cx[:, b0 + j, d * P:(d + 1) * P], c.ident[0:KEYS, 0:KEYS])
                last.then_inc(full, 1)

        @block.scalar
        def _(act):
            for g in range(groups):
                d, b0 = g % DC, g // DC * 4
                act.wait_ge(full, g + 1)
                nc.scalar.copy(c.ct[0][:, d, b0 * KEYS:(b0 + 4) * KEYS],
                               c.bank[g % 2][:, 0:4 * KEYS]).then_inc(hi_done, 1)
            act.wait_ge(loaded_g, 32)
            nc.scalar.activation(c.gates[:], graw[:], ACT.Tanh).then_inc(hi_done, 1)
            act.wait_ge(hi_done, groups + 1)
            nc.scalar.mul(c.gates_w[:], c.gates[:], 1.0 / W_SCALE ** 2)

        @block.vector
        def _(dve):
            for g in range(groups):
                d, b0 = g % DC, g // DC * 4
                dve.wait_ge(hi_done, g + 1)
                cols = slice(b0 * KEYS, (b0 + 4) * KEYS)
                nc.vector.tensor_tensor(c.ct[1][:, d, cols], c.bank[g % 2][:, 0:4 * KEYS],
                                        c.ct[0][:, d, cols], ALU.subtract).then_inc(free, 1)


class Weights:

    def __init__(self, nc, ctx, c, tag, slot, w_dram, rows_dram=None, rows_scale=()):
        self.cols = w_dram.shape[1]
        self.tag, self.slot, self.w, self.rows, self.rows_scale = tag, slot, w_dram, rows_dram, rows_scale
        self.landed = [ctx.enter_context(nc.semaphore(f"{tag}_w_landed{i}")) for i in range(2)]
        self.step = ctx.enter_context(nc.semaphore(f"{tag}_w_step"))
        self.row_step = ctx.enter_context(nc.semaphore(f"{tag}_row_step"))
        self.row_dma = ctx.enter_context(nc.semaphore(f"{tag}_row_dma"))


def prep_weights(nc, c, pool, w):
    if w is None:
        return
    stage, scaled = c.w_stage, c.w_scaled
    chunks = [(o, min(STAGED, w.cols - o)) for o in range(0, w.cols, STAGED)]
    for k, (o, n) in enumerate(chunks):
        wait(pool, w.step, 3 * (k - 1))
        pool.dma_start(stage[:, k % 2, 0:n], w.w[:, o:o + n]).then_inc(w.landed[k % 2], 16)
        if k >= 1:
            split_chunk(nc, c, pool, w, k - 1, chunks)
    split_chunk(nc, c, pool, w, len(chunks) - 1, chunks)
    if w.rows is not None:
        n = w.rows.shape[1]
        raw, lo = c.row_raw, c.row_lo
        pool.dma_start(raw[0:1, 0:n], w.rows).then_inc(w.row_dma, 16)
        pool.wait_ge(w.row_dma, 16)
        for j, s in enumerate(w.rows_scale):
            nc.gpsimd.tensor_scalar(raw[0:1, j * DIM:(j + 1) * DIM], raw[0:1, j * DIM:(j + 1) * DIM],
                                    s, 1.0, ALU.mult, ALU.mult).then_inc(w.row_step, 1)
        m = len(w.rows_scale)
        pool.wait_ge(w.row_step, m)
        nc.gpsimd.tensor_copy(c.rows[w.slot][0:1, 0:n], raw[0:1, 0:n]).then_inc(w.row_step, 1)
        pool.wait_ge(w.row_step, m + 1)
        nc.gpsimd.tensor_tensor(lo[0:1, 0:n], raw[0:1, 0:n], c.rows[w.slot][0:1, 0:n],
                                ALU.subtract).then_inc(w.row_step, 1)
        pool.wait_ge(w.row_step, m + 2)
        pool.dma_start(c.rows[w.slot][1:2, 0:n], lo[0:1, 0:n]).then_inc(w.row_dma, 16)
        pool.wait_ge(w.row_dma, 32)


def split_chunk(nc, c, pool, w, k, chunks):
    o, n = chunks[k]
    src, scaled = c.w_stage[:, k % 2, 0:n], c.w_scaled[:, 0:n]
    hi, lo = (c.arena[w.slot][:, i, o:o + n] for i in range(2))
    factor = c.w_scale[:, 0:1].broadcast_to([P, n])
    pool.wait_ge(w.landed[k % 2], 16 * (k // 2 + 1))
    nc.gpsimd.tensor_tensor(hi, src, factor, ALU.mult).then_inc(w.step, 1)
    nc.gpsimd.tensor_tensor(scaled, src, factor, ALU.mult).then_inc(w.step, 1)
    pool.wait_ge(w.step, 3 * k + 2)
    nc.gpsimd.tensor_tensor(lo, scaled, hi, ALU.subtract).then_inc(w.step, 1)
    pool.wait_ge(w.step, 3 * k + 3)


def norm_stats(nc, c, tag, second=None):
    with ExitStack() as ctx:
        sem = ctx.enter_context(stage_semaphores(nc, tag))
        stat_done, var_done, pow_done = sem("stat_done"), sem("var_done"), sem("pow_done")
        block = ctx.enter_context(nc.Block())

        @block.vector
        def _(dve):
            for t in range(TILES):
                nc.vector.bn_stats(c.stats[:, t, :], c.x[:, t, :]).then_inc(stat_done, 1)
            for t in range(TILES):
                dve.wait_ge(stat_done, t + 1)
                nc.vector.bn_aggr(c.mv[:, t, :], c.stats[:, t, :]).then_inc(var_done, 1)

        @block.gpsimd
        def _(pool):
            def col(i):
                return c.consts[:, i:i + 1].broadcast_to([P, TILES])
            pool.wait_ge(var_done, TILES)
            var = c.mv[:, :, 1]
            out = c.rstd1 if second is not None else c.rstd
            nc.gpsimd.tensor_tensor(c.tmp_a[:], var, col(0), ALU.add).then_inc(pow_done, 1)
            pool.wait_ge(pow_done, 1)
            nc.gpsimd.tensor_tensor(out[:], c.tmp_a[:], col(1), ALU.pow).then_inc(pow_done, 1)
            if second is not None:
                pool.wait_ge(pow_done, 2)
                nc.gpsimd.tensor_tensor(c.tmp_a[:], out[:], out[:], ALU.mult).then_inc(pow_done, 1)
                pool.wait_ge(pow_done, 3)
                nc.gpsimd.tensor_tensor(c.tmp_a[:], c.tmp_a[:], var, ALU.mult).then_inc(pow_done, 1)
                pool.wait_ge(pow_done, 4)
                nc.gpsimd.tensor_tensor(c.tmp_a[:], c.tmp_a[:], col(second), ALU.add).then_inc(pow_done, 1)
                pool.wait_ge(pow_done, 5)
                nc.gpsimd.tensor_tensor(c.tmp_a[:], c.tmp_a[:], col(1), ALU.pow).then_inc(pow_done, 1)
                pool.wait_ge(pow_done, 6)
                nc.gpsimd.tensor_tensor(c.rstd[:], c.tmp_a[:], out[:], ALU.mult).then_inc(pow_done, 1)


def three_products(nc, out, stationary, moving, first=True, last=True):
    (ah, al), (bh, bl) = stationary, moving
    nc.tensor.matmul(out, ah, bh, start=first, stop=False)
    nc.tensor.matmul(out, ah, bl, start=False, stop=False)
    return nc.tensor.matmul(out, al, bh, start=False, stop=last)


class Attention:

    def __init__(self, tag, kind, weights, gate=None, shared_kv=False, add_mask=None, clip_mask=None,
                 affine=False, biased=False, store="x"):
        self.tag, self.kind, self.weights = tag, kind, weights
        self.gate, self.shared_kv, self.add_mask, self.clip_mask = gate, shared_kv, add_mask, clip_mask
        self.affine, self.biased, self.store = affine, biased, store
        self.dh = 64 if kind == "cross64" else 16
        self.causal = kind == "self16"
        self.kw = P if self.causal else KEYS
        self.key_tiles = SEQ // P if self.causal else 1
        self.scale = self.dh ** -0.5 / (W_SCALE * W_SCALE)
        if self.causal:
            self.units = [(0, h, 4, [0]) for h in (0, 1, 8, 9)]
            self.units += [(1, h, 2, [0, 1]) for h in (0, 1, 4, 5, 8, 9, 12, 13)]
            self.fronts = [("xT", -12), ("q", -11), ("k", -10), ("v", -9),
                           ("qT0", -6), ("qT1", -5), ("kT0", -3), ("kT1", -2)]
        else:
            self.units = [(t, h, 4, [0]) for t in range(2) for h in (0, 1, 8, 9)]
            if self.dh == 16:
                self.fronts = [("xT", -8), ("q", -7), ("kv", -6), ("qT0", -5), ("qT1", -4), ("kT", -3)]
            elif self.shared_kv:
                self.fronts = [("xT", -8), ("q0", -7), ("q1", -6), ("q2", -5), ("q3", -4), ("kv", -3)]
            else:
                self.fronts = [("xT", -8), ("q0", -7), ("q1", -7), ("q2", -6), ("q3", -5), ("k0", -4),
                               ("k1", -4), ("v0", -3), ("v1", -2)]
        self.nu = len(self.units)
        self.nf = len(self.fronts)
        self.o_chunks = HEADS * self.dh // P
        parts = max(1, self.o_chunks // 4)
        self.outs = []
        for t in range(2):
            last = max(i for i, u in enumerate(self.units) if u[0] == t)
            self.outs += [("turn", t, k, last + 3 + k) for k in range(parts)]
            self.outs += [("project", t, 0, last + 3 + parts)]
        self.no = len(self.outs)


def attention(nc, c, a, next_weights):
    dh, kw, nu, nf, no, units = a.dh, a.kw, a.nu, a.nf, a.no, a.units
    nkt = a.key_tiles
    wide = a.kind == "cross64"
    v_heads = 1 if a.shared_kv else HEADS
    with ExitStack() as ctx:
        def sb(name, shape, dt):
            return ctx.enter_context(nc.sbuf_tensor(f"{a.tag}_{name}", shape, dt))

        sem = ctx.enter_context(stage_semaphores(nc, a.tag))

        xn = sb("xn", [P, 2, DIM], F32)
        xt = [sb(f"xT_{p}", [P, DC, SEQ], F16) for p in ("hi", "lo")]
        q_parts = ("hi", "lo") if wide else ("stack",)
        k_chunks = 1 if a.shared_kv else HEADS // 2
        qt = [[sb(f"qT_{p}{i}", [P, HEADS // 2, SEQ], F16) for p in q_parts] for i in range(2)]
        kt = [[sb(f"kT_{p}{i}", [P, k_chunks, kw * nkt], F16) for p in q_parts] for i in range(2)]
        v = [[sb(f"v_{p}{i}", [P, nkt, v_heads, dh + 1], F16) for p in ("hi", "lo")] for i in range(2)]
        e = [sb(f"exp{i}", [P, 512], F32) for i in range(2)]
        pt = [[sb(f"pT_{p}{i}", [P, 512], F16) for p in ("hi", "lo")] for i in range(2)]
        top = sb("top", [P, 2, 4], F32)
        shift = sb("shift", [P, 2, 4], F32)
        rden = sb("rden", [P, 2, 4], F32)
        o = [sb(f"o{i}", [P, HEADS * dh], F32) for i in range(2)]
        ot = [sb(f"oT_{p}", [P, a.o_chunks, P], F16) for p in ("hi", "lo")]
        if a.affine:
            norm_g = sb("norm_g", [P, DC], F32)
            norm_b = sb("norm_b", [P, DC], F32)
            xf = sb("xT_f32", [P, DC, SEQ], F32)
        if not wide:
            qs = sb("q_stack", [P, 2, HEADS, 4, 16], F16)
            ks = sb("k_stack", [P, nkt, HEADS, 4, 16], F16)
        if a.add_mask is not None:
            mask_i = sb("mask_i", [KEYS, BATCH], I32)
            mask_f = sb("mask_f", [KEYS, BATCH], F32)
            mask_h = sb("mask_h", [KEYS, BATCH], F16)
        if a.clip_mask is not None:
            cm_i = sb("clip_mask_i", [P, 2, 2, KEYS], I32)
            cm_t = sb("clip_mask_t", [P, 2, 2, KEYS], F32)
            cm_u = sb("clip_mask_u", [P, 2, 2, KEYS], F32)
            clipped = sb("clipped", [P, 2, 4 * KEYS], F32)
        if a.causal:
            cos_t = sb("cos", [P, 2, 16], F32)
            sin_t = sb("sin", [P, 2, 16], F32)
            raw = [sb(f"raw{i}", [P, 2, HEADS, 16], F32) for i in range(2)]
            rot = [sb(f"rot{i}", [P, 2, HEADS, 16], F32) for i in range(2)]
            half = sb("rot_half", [P, 2, HEADS, 16], F32)
            future = sb("future", [P, P], F16)
            big_id = sb("big_id", [P, P], F16)

        loaded, const_ready, setup_step = sem("loaded"), sem("const_ready"), sem("setup_step")
        xn_ready = sem("xn_ready")
        f_full, f_hi, f_free = sem("f_full"), sem("f_hi"), sem("f_free")
        s_full = sem("scores_full")
        clip_done = sem("clip_done")
        top_done, shift_done, exp_done = sem("top_done"), sem("shift_done"), sem("exp_done")
        t_full, p_hi, p_lo = sem("pT_full"), sem("hi"), sem("lo")
        pv_full, rden_done, norm_done = sem("pv_full"), sem("rden_done"), sem("norm_done")
        o_full, o_hi, o_free = sem("o_full"), sem("o_hi"), sem("o_free")
        rot_step, stack_hi, stack_lo = sem("rot_step"), sem("stack_hi"), sem("stack_lo")
        cm_landed, cm_step, cm_ready = [sem("cm_landed0"), sem("cm_landed1")], sem("cm_step"), sem("cm_ready")
        block = ctx.enter_context(nc.Block())

        w_hi, w_lo = (c.arena[a.weights.slot][:, i, :] for i in range(2))
        rows = c.rows[a.weights.slot]

        def weight(off, n):
            return w_hi[:, off:off + n], w_lo[:, off:off + n]

        if wide and a.shared_kv:
            k_off, v_off, o_off, kn, vn = 2048, 2048 + 256, 2048 + 256 + 128, P, 64
        elif wide:
            k_off, v_off, o_off, kn, vn = 2048, 4096, 6144, 1024, 1024
        else:
            k_off, v_off, o_off, kn, vn = 512, 1024, 1536, 256, 256
        qn = 1024 if wide else 256
        f_bank, o_bank = c.bank[6], c.bank[7]
        f_bank_h = f_bank[:].bitcast(F16)
        both = [n for n, _ in a.fronts if n in ("xT", "q", "kv", "v", "q0", "q1", "q2", "q3", "k0", "k1", "v0", "v1")]
        if a.causal:
            both = ["xT", "v"]
        turns = [x for x in a.outs if x[0] == "turn"]

        def blocks(u):
            t, h0, nh, kts = units[u]
            return [(i * len(kts) + j, h0 + 2 * i, k) for i in range(nh) for j, k in enumerate(kts)]

        def turned_w(m):
            return (m + 7) // 8 * 8

        def head_rows(x, h, cols, shared=False):
            return x[64 * (h % 2):64 * (h % 2) + 64, 0 if shared else h // 2, cols]

        a.consts = 0
        a.tables = 2 if a.causal else 0
        a.loads = a.tables + (1 if a.add_mask is not None else 0) + (2 if a.affine else 0)

        @block.gpsimd
        def _(pool):
            def const(ins):
                ins.then_inc(const_ready, 1)
                a.consts += 1
                pool.wait_ge(const_ready, a.consts)

            if a.causal:
                const(nc.gpsimd.memset(future[:], 0.0))
                const(nc.gpsimd.affine_select(out=future[:], in_=future[:], compare_op=ALU.is_ge, fill=-60000.0,
                                              base=0, pattern=[[-1, P]], channel_multiplier=1))
                const(nc.gpsimd.memset(big_id[:], 0.0))
                const(nc.gpsimd.affine_select(out=big_id[:], in_=big_id[:], compare_op=ALU.not_equal, fill=1024.0,
                                              base=0, pattern=[[-1, P]], channel_multiplier=1))
            if not wide:
                const(nc.gpsimd.memset(qs[:, :, :, 3, :], 0.0))
                const(nc.gpsimd.memset(ks[:, :, :, 3, :], 0.0))
                if a.add_mask is not None:
                    const(nc.gpsimd.memset(qs[:, :, :, 3, 0:1], W_SCALE * W_SCALE))
            for i in range(2):
                const(nc.gpsimd.memset(v[i][0][:, :, :, dh:dh + 1], 1.0))
                const(nc.gpsimd.memset(v[i][1][:, :, :, dh:dh + 1], 0.0))
            if a.add_mask is not None:
                pool.wait_ge(loaded, 16 * a.loads)
                factor = -CLIP / (a.scale * W_SCALE * W_SCALE)
                const(nc.gpsimd.tensor_scalar(mask_f[:], mask_i[:], factor, 1.0, ALU.mult, ALU.mult))
                const(nc.gpsimd.tensor_scalar(mask_h[:], mask_f[:], 1.0, 0.0, ALU.mult, ALU.add))

            def rotate(b, s):
                for i, at in enumerate((-11, -10)):
                    if at != s:
                        continue
                    n = lambda k: b.count(8, 4 * i + k)
                    pool.wait_ge(f_free, b.count(nf, i + 2))
                    wait(pool, stack_hi, b.count(2, i - 1))
                    table = lambda x, r: x[:, :, r].unsqueeze(2).broadcast_to([P, 2, HEADS, 16 if r == slice(0, 16) else 8])
                    nc.gpsimd.tensor_tensor(rot[i][:], raw[i][:], table(cos_t, slice(0, 16)), ALU.mult).then_inc(rot_step, 1)
                    nc.gpsimd.tensor_tensor(half[:, :, :, 0:8], raw[i][:, :, :, 8:16], table(sin_t, slice(0, 8)),
                                            ALU.mult).then_inc(rot_step, 1)
                    nc.gpsimd.tensor_tensor(half[:, :, :, 8:16], raw[i][:, :, :, 0:8], table(sin_t, slice(8, 16)),
                                            ALU.mult).then_inc(rot_step, 1)
                    pool.wait_ge(rot_step, n(3))
                    nc.gpsimd.tensor_tensor(rot[i][:], rot[i][:], half[:], ALU.add).then_inc(rot_step, 1)
                    pool.wait_ge(rot_step, n(4))
                for i, at in enumerate((-8, -6)):
                    if at == s:
                        st, blk = ((qs, 1), (ks, 2))[i]
                        pool.wait_ge(stack_hi, b.count(2, i + 1))
                        nc.gpsimd.tensor_tensor(st[:, :, :, blk, :], rot[i][:], st[:, :, :, 0, :],
                                                ALU.subtract).then_inc(stack_lo, 1)

            if a.causal:
                pool.wait_ge(loaded, 16 * a.loads)
                over_steps(pool, nu, (rotate,))
            prep_weights(nc, c, pool, next_weights)

        @block.sync
        def _(sp):
            n = 0
            def load(dst, src):
                nonlocal n
                n += 1
                sp.dma_start(dst, src).then_inc(loaded, 16)
            if a.add_mask is not None:
                load(mask_i[:], a.add_mask)
            if a.causal:
                load(cos_t[:], c.dram["rope_cos"])
                load(sin_t[:], c.dram["rope_sin"])
            if a.affine:
                load(norm_g[:], a.norm_g)
                load(norm_b[:], a.norm_b)
            if n:
                sp.wait_ge(loaded, 16 * n)
            if a.clip_mask is not None:
                def masks(b, s):
                    if s != -nu - 1:
                        return
                    row = b.off if b.i is None else b.count(1, 0)
                    wait(sp, cm_step, b.count(1, -1))
                    sp.dma_start(cm_i[:, b.off % 2], a.clip_mask[row]).then_inc(cm_landed[b.off % 2], 16)
                over_steps(sp, nu, (masks,))

        @block.tensor
        def _(pe):
            if a.causal:
                pe.wait_ge(const_ready, 4)

            def scores(b, s):
                if not 0 <= s < nu:
                    return
                t, h0, nh, kts = units[s]
                wait(pe, clip_done if a.clip_mask is not None else exp_done, b.count(nu, s - 1))
                if s == 0:
                    wait(pe, f_free, b.count(nf, nf))
                for blk, h, k in blocks(s):
                    out = c.bank[s % 2][:, blk * kw:(blk + 1) * kw]
                    q_cols, k_cols = slice(t * P, (t + 1) * P), slice(k * kw, (k + 1) * kw)
                    qp = [head_rows(x, h, q_cols) for x in qt[b.off % 2]]
                    kp = [head_rows(x, h, k_cols, a.shared_kv) for x in kt[b.off % 2]]
                    if wide:
                        last = three_products(nc, out, qp, kp)
                    else:
                        diagonal = a.causal and k == t
                        last = nc.tensor.matmul(out, qp[0], kp[0], start=True, stop=not diagonal)
                        if diagonal:
                            last = nc.tensor.matmul(out, big_id[:], future[:], start=False, stop=True)
                last.then_inc(s_full, 1)

            def turn_probs(b, s):
                u = s - 1
                if not 0 <= u < nu:
                    return
                wait(pe, exp_done, b.count(nu, u + 1))
                wait(pe, p_lo, b.count(nu, u - 1))
                for blk in range(4):
                    last = nc.tensor.transpose(c.bank[2 + u % 2][0:kw, blk * P:(blk + 1) * P],
                                               e[u % 2][:, blk * kw:(blk + 1) * kw], c.ident[:])
                last.then_inc(t_full, 1)

            def times_v(b, s):
                u = s - 2
                if not 0 <= u < nu:
                    return
                t, h0, nh, kts = units[u]
                wait(pe, p_lo, b.count(nu, u + 1))
                wait(pe, norm_done, b.count(nu, u - 1))
                ph, pl = pt[u % 2]
                for blk, h, k in blocks(u):
                    i = (h - h0) // 2
                    vh, vl = (x[0:kw, k, 0 if a.shared_kv else h, :] for x in v[b.off % 2])
                    pp = (ph[0:kw, blk * P:(blk + 1) * P], pl[0:kw, blk * P:(blk + 1) * P])
                    last = three_products(nc, c.bank[4 + u % 2][:, i * (dh + 1):(i + 1) * (dh + 1)], pp, (vh, vl),
                                          first=k == kts[0], last=k == kts[-1])
                last.then_inc(pv_full, 1)

            def output(b, s):
                for n, (what, t, k, at) in enumerate(a.outs):
                    if at != s:
                        continue
                    wait(pe, o_free, b.count(no, n))
                    if what == "turn":
                        last_unit = max(i for i, u in enumerate(units) if u[0] == t)
                        wait(pe, norm_done, b.count(nu, last_unit + 1))
                        m = min(4, a.o_chunks)
                        for j in range(m):
                            ch = 4 * k + j
                            last = nc.tensor.transpose(o_bank[:, j * P:(j + 1) * P],
                                                       o[t][:, ch * P:(ch + 1) * P], c.ident[:])
                    else:
                        for ch in range(a.o_chunks):
                            last = three_products(nc, o_bank[:, 0:DIM], [x[:, ch, :] for x in ot],
                                                  weight(o_off + ch * DIM, DIM), first=ch == 0,
                                                  last=ch == a.o_chunks - 1 and not a.biased)
                        if a.biased:
                            last = nc.tensor.matmul(o_bank[:, 0:DIM], c.ones_rows[:], rows[:, 3 * DIM:4 * DIM],
                                                    start=False, stop=True)
                    last.then_inc(o_full, 1)

            def project_rows(out, lhs, off, n, width, bias=None, m=P):
                for d in range(DC):
                    last = three_products(nc, out, [x[d] for x in lhs], weight(off + d * width, n),
                                          first=d == 0, last=d == DC - 1 and bias is None)
                if bias is not None:
                    last = nc.tensor.matmul(out, c.ones_rows[:, 0:m], rows[:, bias * DIM:(bias + 1) * DIM],
                                            start=False, stop=True)
                return last

            def front(b, s):
                for n, (what, at) in enumerate(a.fronts):
                    if at != s:
                        continue
                    wait(pe, f_free, b.count(nf, n))
                    x_tile = [[[x[:, d, t * P:(t + 1) * P] for d in range(DC)] for x in xt] for t in range(2)]
                    keys = lambda: [[x[:, d, bass.ds(b.count(KEYS, 0), KEYS)] for d in range(DC)] for x in c.ct_now]
                    if what == "xT":
                        wait(pe, xn_ready, b.count(1, 1))
                        for d in range(DC):
                            for t in range(2):
                                col = (d * 2 + t) * P
                                last = nc.tensor.transpose(f_bank[:, col:col + P], xn[:, t, d * P:(d + 1) * P],
                                                           c.ident[:])
                    elif what == "q" or (a.causal and what in "kv"):
                        i = "qkv".index(what)
                        for t in range(2):
                            last = project_rows(f_bank[:, t * 256:t * 256 + 256], x_tile[t], i * 512, 256, 256,
                                                bias=i if a.biased else None)
                    elif what == "kv" and not wide:
                        kk = keys()
                        for i in (1, 2):
                            last = project_rows(f_bank[0:KEYS, (i - 1) * 256:i * 256], kk, i * 512, 256, 256,
                                                bias=i if a.biased else None, m=KEYS)
                    elif what == "kv":
                        kk = keys()
                        for d in range(DC):
                            last = three_products(nc, f_bank[:, 0:KEYS], weight(k_off + d * kn, P),
                                                  [x[d] for x in kk], first=d == 0, last=d == DC - 1)
                        last = project_rows(f_bank[0:KEYS, 128:128 + 64], kk, v_off, 64, 64)
                    elif what[:2] in ("qT", "kT"):
                        cross_k = what == "kT"
                        if a.causal:
                            wait(pe, stack_lo, b.count(2, 1 if what[0] == "q" else 2))
                        t = 0 if cross_k else int(what[2])
                        st, m = (ks, kw) if what[0] == "k" else (qs, P)
                        for ch in range(HEADS // 2):
                            last = nc.tensor.transpose(
                                f_bank_h[:, ch * turned_w(m):ch * turned_w(m) + m],
                                st[0:m, t, 2 * ch:2 * ch + 2, :, :].rearrange("p h f d -> p (h f d)"),
                                c.ident_h[0:m, 0:m])
                    elif what[0] == "q":
                        for j in range(2):
                            ch = 2 * int(what[1]) + j
                            for d in range(DC):
                                last = three_products(nc, f_bank[:, j * SEQ:(j + 1) * SEQ],
                                                      weight(d * qn + ch * P, P), [x[:, d, :] for x in xt],
                                                      first=d == 0, last=d == DC - 1)
                    elif what[0] == "k":
                        kk = keys()
                        for j in range(4):
                            ch = 4 * int(what[1]) + j
                            for d in range(DC):
                                last = three_products(nc, f_bank[:, j * KEYS:(j + 1) * KEYS],
                                                      weight(k_off + d * kn + ch * P, P), [x[d] for x in kk],
                                                      first=d == 0, last=d == DC - 1)
                    else:
                        last = project_rows(f_bank[0:KEYS, :], keys(), v_off + 512 * int(what[1]), 512, vn)
                    last.then_inc(f_full, 1)

            over_steps(pe, nu, (scores, turn_probs, times_v, output, front,))

        @block.scalar
        def _(act):
            if a.affine:
                act.wait_ge(loaded, 16 * a.loads)

            def probs_hi(b, s):
                u = s - 1
                if not 0 <= u < nu:
                    return
                wait(act, t_full, b.count(nu, u + 1))
                wait(act, pv_full, b.count(nu, u - 1))
                nc.scalar.copy(pt[u % 2][0][0:kw, :], c.bank[2 + u % 2][0:kw, :]).then_inc(p_hi, 1)

            def exps(b, s):
                if not 0 <= s < nu:
                    return
                t, h0, nh, kts = units[s]
                wait(act, shift_done, b.count(nu, s + 1))
                wait(act, t_full, b.count(nu, s - 1))
                w = kw * len(kts)
                src = clipped[:, s % 2, :] if a.clip_mask is not None else c.bank[s % 2]
                for i in range(nh):
                    last = nc.scalar.activation(e[s % 2][:, i * w:(i + 1) * w], src[:, i * w:(i + 1) * w], ACT.Exp,
                                                bias=shift[:, s % 2, i:i + 1], scale=a.scale)
                last.then_inc(exp_done, 1)

            def output(b, s):
                for n, (what, t, k, at) in enumerate(a.outs):
                    if at == s and what == "turn":
                        act.wait_ge(o_full, b.count(no, n + 1))
                        m = min(4, a.o_chunks)
                        nc.scalar.copy(ot[0][:, 4 * k:4 * k + m, :].rearrange("p c n -> p (c n)"),
                                       o_bank[:, 0:m * P]).then_inc(o_hi, 1)

            def front(b, s):
                par = b.off % 2
                for n, (what, at) in enumerate(a.fronts):
                    if at != s or what in ("qT1", "kT1"):
                        continue
                    act.wait_ge(f_full, b.count(nf, n + 1))
                    if what == "xT":
                        if a.affine:
                            for d in range(DC):
                                last = nc.scalar.activation(xf[:, d, :], f_bank[:, d * SEQ:(d + 1) * SEQ], ACT.Identity,
                                                            bias=norm_b[:, d:d + 1], scale=norm_g[:, d:d + 1])
                        else:
                            last = nc.scalar.copy(xt[0][:].rearrange("p d n -> p (d n)"), f_bank[:])
                        last.then_inc(f_hi, 1)
                    elif a.causal and what in ("q", "k"):
                        i = "qk".index(what)
                        nc.scalar.copy(raw[i][:].rearrange("p t h d -> p (t h d)"), f_bank[:]).then_inc(f_free, 1)
                    elif a.causal and what == "v":
                        nc.scalar.copy(v[par][0][:, :, :, 0:dh],
                                       f_bank[:].rearrange("p (t h d) -> p t h d", t=2, h=HEADS)).then_inc(f_hi, 1)
                    elif what == "q":
                        for blk in (0, 2):
                            last = nc.scalar.copy(qs[:, :, :, blk, :],
                                                  f_bank[:].rearrange("p (t h d) -> p t h d", t=2, h=HEADS))
                        last.then_inc(f_hi, 1)
                    elif what == "kv" and not wide:
                        kf = f_bank[0:KEYS, 0:256].rearrange("p (h d) -> p h d", h=HEADS)
                        vf = f_bank[0:KEYS, 256:512].rearrange("p (h d) -> p h d", h=HEADS)
                        nc.scalar.copy(ks[0:KEYS, 0, :, 0, :], kf)
                        nc.scalar.copy(ks[0:KEYS, 0, :, 1, :], kf)
                        nc.scalar.copy(v[par][0][0:KEYS, 0, :, 0:dh], vf).then_inc(f_hi, 1)
                    elif what == "kv":
                        nc.scalar.copy(kt[par][0][:, 0, :], f_bank[:, 0:KEYS])
                        nc.scalar.copy(v[par][0][0:KEYS, 0, 0, 0:dh], f_bank[0:KEYS, 128:192]).then_inc(f_hi, 1)
                    elif what[:2] == "qT":
                        nc.scalar.copy(qt[par][0][:, :, 0:P], f_bank_h.rearrange("p (c n) -> p c n", n=P)).then_inc(f_free, 1)
                    elif what == "kT0":
                        nc.scalar.copy(kt[par][0][:, :, 0:P], f_bank_h.rearrange("p (c n) -> p c n", n=P)).then_inc(f_free, 1)
                    elif what == "kT":
                        nc.scalar.copy(kt[par][0][:, :, :],
                                       f_bank_h[:, 0:8 * turned_w(KEYS)].rearrange("p (c n) -> p c n", c=8)[:, :, 0:KEYS]).then_inc(f_free, 1)
                    elif what[0] == "q":
                        ch = 2 * int(what[1])
                        nc.scalar.copy(qt[par][0][:, ch:ch + 2, :].rearrange("p c n -> p (c n)"), f_bank[:]).then_inc(f_hi, 1)
                    elif what[0] == "k":
                        ch = 4 * int(what[1])
                        nc.scalar.copy(kt[par][0][:, ch:ch + 4, :].rearrange("p c n -> p (c n)"),
                                       f_bank[:, 0:4 * KEYS]).then_inc(f_hi, 1)
                    else:
                        h = 8 * int(what[1])
                        nc.scalar.copy(v[par][0][0:KEYS, 0, h:h + 8, 0:dh],
                                       f_bank[0:KEYS, :].rearrange("p (h d) -> p h d", h=8)).then_inc(f_hi, 1)
                if a.causal:
                    for i, at in enumerate((-8, -6)):
                        if at == s:
                            act.wait_ge(rot_step, b.count(8, 4 * i + 4))
                            st, blks = ((qs, (0, 2)), (ks, (0, 1)))[i]
                            for blk in blks:
                                last = nc.scalar.copy(st[:, :, :, blk, :], rot[i][:])
                            last.then_inc(stack_hi, 1)

            over_steps(act, nu, (probs_hi, exps, output, front,))

        @block.vector
        def _(dve):
            dve.wait_ge(const_ready, a.consts)

            def maxima(b, s):
                if not 0 <= s < nu:
                    return
                t, h0, nh, kts = units[s]
                w = kw * len(kts)
                src = c.bank[s % 2][:, 0:nh * w].rearrange("p (h k) -> p h k", h=nh)
                wait(dve, s_full, b.count(nu, s + 1))
                if a.clip_mask is not None:
                    if s == 0:
                        wait(dve, cm_ready, b.count(1, 1))
                    wait(dve, exp_done, b.count(nu, s - 1))
                    dst = clipped[:, s % 2, :].rearrange("p (h k) -> p h k", h=nh)
                    bound = CLIP / a.scale
                    upper = cm_u[:, b.off % 2, t, :].unsqueeze(1).broadcast_to([P, nh, KEYS])
                    nc.vector.scalar_tensor_tensor(out=dst, in0=src, scalar=-bound, in1=upper,
                                                   op0=ALU.max, op1=ALU.min).then_inc(clip_done, 1)
                    dve.wait_ge(clip_done, b.count(nu, s + 1))
                    src = dst
                nc.vector.tensor_reduce(top[:, s % 2, 0:nh], src, AX.X, ALU.max).then_inc(top_done, 1)

            def reciprocals(b, s):
                u = s - 2
                if not 0 <= u < nu:
                    return
                nh = units[u][2]
                sums = c.bank[4 + u % 2][:, 0:nh * (dh + 1)].rearrange("p (h d) -> p h d", h=nh)[:, :, dh]
                wait(dve, pv_full, b.count(nu, u + 1))
                nc.vector.reciprocal(rden[:, u % 2, 0:nh], sums).then_inc(rden_done, 1)

            def shifts(b, s):
                if not 0 <= s < nu:
                    return
                nh = units[s][2]
                dve.wait_ge(top_done, b.count(nu, s + 1))
                nc.vector.tensor_scalar(shift[:, s % 2, 0:nh], top[:, s % 2, 0:nh], -a.scale, None,
                                        ALU.mult).then_inc(shift_done, 1)

            def normalise(b, s):
                u = s - 2
                if not 0 <= u < nu:
                    return
                t, h0, nh, kts = units[u]
                heads = c.bank[4 + u % 2][:, 0:nh * (dh + 1)].rearrange("p (h d) -> p h d", h=nh)[:, :, 0:dh]
                dve.wait_ge(rden_done, b.count(nu, u + 1))
                nc.vector.tensor_tensor(o[t][:].rearrange("p (h d) -> p h d", d=dh)[:, h0:h0 + 2 * nh - 1:2, :], heads,
                                        rden[:, u % 2, 0:nh].unsqueeze(2).broadcast_to([P, nh, dh]),
                                        ALU.mult).then_inc(norm_done, 1)

            def probs_lo(b, s):
                u = s - 1
                if not 0 <= u < nu:
                    return
                dve.wait_ge(p_hi, b.count(nu, u + 1))
                nc.vector.tensor_tensor(pt[u % 2][1][0:kw, :], c.bank[2 + u % 2][0:kw, :], pt[u % 2][0][0:kw, :],
                                        ALU.subtract).then_inc(p_lo, 1)

            def output(b, s):
                for n, (what, t, k, at) in enumerate(a.outs):
                    if at != s:
                        continue
                    if what == "turn":
                        i = [x for x in turns].index((what, t, k, at))
                        m = min(4, a.o_chunks)
                        dve.wait_ge(o_hi, b.count(len(turns), i + 1))
                        nc.vector.tensor_tensor(ot[1][:, 4 * k:4 * k + m, :].rearrange("p c n -> p (c n)"),
                                                o_bank[:, 0:m * P],
                                                ot[0][:, 4 * k:4 * k + m, :].rearrange("p c n -> p (c n)"),
                                                ALU.subtract).then_inc(o_free, 1)
                        continue
                    tile = b.count(2, t)
                    dve.wait_ge(o_full, b.count(no, n + 1))
                    if a.store == "x":
                        nc.vector.scalar_tensor_tensor(out=c.x[:, tile, :], in0=o_bank[:, 0:DIM],
                                                       scalar=c.gates_w[:, a.gate:a.gate + 1], in1=c.x[:, tile, :],
                                                       op0=ALU.mult, op1=ALU.add).then_inc(o_free, 1)
                    elif a.store == "h+":
                        nc.vector.scalar_tensor_tensor(out=c.h[:, tile, :], in0=o_bank[:, 0:DIM],
                                                       scalar=1.0 / W_SCALE ** 2, in1=c.h[:, tile, :],
                                                       op0=ALU.mult, op1=ALU.add).then_inc(o_free, 1)
                    else:
                        nc.vector.tensor_scalar(c.h[:, tile, :], o_bank[:, 0:DIM], 1.0 / W_SCALE ** 2, None,
                                                ALU.mult).then_inc(o_free, 1)

            def front(b, s):
                par = b.off % 2
                if s == -nu - 1:
                    for t in range(2):
                        tile = b.count(2, t)
                        args = (c.mv[:, tile, 0:1], c.rstd[:, bass.ds(tile, 1)])
                        last = nc.vector.tensor_scalar(xn[:, t, :], c.x[:, tile, :], *args, ALU.subtract, ALU.mult)
                        if t == 1:
                            last.then_inc(xn_ready, 1)
                        if a.store == "h+":
                            r1 = c.rstd1[:, bass.ds(tile, 1)]
                            nc.vector.tensor_scalar(c.h[:, tile, :], c.x[:, tile, :], args[0], r1,
                                                    ALU.subtract, ALU.mult)
                for n, (what, at) in enumerate(a.fronts):
                    if at != s:
                        continue
                    if what in ("qT0", "kT0", "kT") or (a.causal and what in ("q", "k")):
                        continue
                    if what in ("qT1", "kT1"):
                        dve.wait_ge(f_full, b.count(nf, n + 1))
                        dst = (qt if what[0] == "q" else kt)[par][0]
                        nc.vector.tensor_copy(dst[:, :, P:2 * P], f_bank_h.rearrange("p (c n) -> p c n", n=P)).then_inc(f_free, 1)
                        continue
                    dve.wait_ge(f_hi, b.count(len(both), both.index(what) + 1))
                    if what == "xT" and a.affine:
                        flat = xf[:].rearrange("p d n -> p (d n)")
                        nc.vector.tensor_copy(xt[0][:].rearrange("p d n -> p (d n)"), flat).then_inc(setup_step, 1)
                        dve.wait_ge(setup_step, b.count(1, 1))
                        nc.vector.tensor_tensor(xt[1][:].rearrange("p d n -> p (d n)"), flat,
                                                xt[0][:].rearrange("p d n -> p (d n)"), ALU.subtract).then_inc(f_free, 1)
                    elif what == "xT":
                        nc.vector.tensor_tensor(xt[1][:].rearrange("p d n -> p (d n)"), f_bank[:],
                                                xt[0][:].rearrange("p d n -> p (d n)"), ALU.subtract).then_inc(f_free, 1)
                    elif what == "v" and a.causal:
                        nc.vector.tensor_tensor(v[par][1][:, :, :, 0:dh],
                                                f_bank[:].rearrange("p (t h d) -> p t h d", t=2, h=HEADS),
                                                v[par][0][:, :, :, 0:dh], ALU.subtract).then_inc(f_free, 1)
                    elif what == "q":
                        nc.vector.tensor_tensor(qs[:, :, :, 1, :],
                                                f_bank[:].rearrange("p (t h d) -> p t h d", t=2, h=HEADS),
                                                qs[:, :, :, 0, :], ALU.subtract).then_inc(f_free, 1)
                    elif what == "kv" and not wide:
                        kf = f_bank[0:KEYS, 0:256].rearrange("p (h d) -> p h d", h=HEADS)
                        vf = f_bank[0:KEYS, 256:512].rearrange("p (h d) -> p h d", h=HEADS)
                        nc.vector.tensor_tensor(ks[0:KEYS, 0, :, 2, :], kf, ks[0:KEYS, 0, :, 0, :], ALU.subtract)
                        if a.add_mask is not None:
                            col = mask_h[:, bass.ds(b.count(1, 0), 1)]
                            nc.vector.tensor_copy(ks[0:KEYS, 0, :, 3, 0], col.broadcast_to([KEYS, HEADS]))
                        nc.vector.tensor_tensor(v[par][1][0:KEYS, 0, :, 0:dh], vf, v[par][0][0:KEYS, 0, :, 0:dh],
                                                ALU.subtract).then_inc(f_free, 1)
                    elif what == "kv":
                        nc.vector.tensor_tensor(kt[par][1][:, 0, :], f_bank[:, 0:KEYS], kt[par][0][:, 0, :], ALU.subtract)
                        nc.vector.tensor_tensor(v[par][1][0:KEYS, 0, 0, 0:dh], f_bank[0:KEYS, 128:192],
                                                v[par][0][0:KEYS, 0, 0, 0:dh], ALU.subtract).then_inc(f_free, 1)
                    elif what[0] == "q":
                        ch = 2 * int(what[1])
                        hi, lo = (x[:, ch:ch + 2, :].rearrange("p c n -> p (c n)") for x in qt[par])
                        nc.vector.tensor_tensor(lo, f_bank[:], hi, ALU.subtract).then_inc(f_free, 1)
                    elif what[0] == "k":
                        ch = 4 * int(what[1])
                        hi, lo = (x[:, ch:ch + 4, :].rearrange("p c n -> p (c n)") for x in kt[par])
                        nc.vector.tensor_tensor(lo, f_bank[:, 0:4 * KEYS], hi, ALU.subtract).then_inc(f_free, 1)
                    else:
                        h = 8 * int(what[1])
                        hi, lo = (x[0:KEYS, 0, h:h + 8, 0:dh] for x in v[par])
                        nc.vector.tensor_tensor(lo, f_bank[0:KEYS, :].rearrange("p (h d) -> p h d", h=8), hi,
                                                ALU.subtract).then_inc(f_free, 1)

            def clip_bounds(b, s):
                if a.clip_mask is None or s != -nu:
                    return
                i = b.off % 2
                dve.wait_ge(cm_landed[i], b.count(8, 16 - 8 * i))
                nc.vector.tensor_scalar(cm_t[:, i], cm_i[:, i], 0, NEG_BIG, ALU.is_equal, ALU.mult).then_inc(cm_step, 1)
                dve.wait_ge(cm_step, b.count(1, 1))
                nc.vector.tensor_scalar(cm_u[:, i], cm_t[:, i], CLIP / a.scale, None, ALU.add).then_inc(cm_ready, 1)

            over_steps(dve, nu, (maxima, reciprocals, shifts, normalise, probs_lo, output, front, clip_bounds))


def quantized_linear(nc, c, tag, gate, next_weights):
    ROUND = 12582912.0
    with ExitStack() as ctx:
        sb = lambda n, sh, dt: ctx.enter_context(nc.sbuf_tensor(f"{tag}_{n}", sh, dt))
        sem = ctx.enter_context(stage_semaphores(nc, tag))
        w8 = sb("w_int8", [P, DC, DIM // 4], I32)
        w = sb("w_f16", [P, DC, DIM], F16)
        w_row, b_row = sb("w_scale_row", [P, DIM], F32), sb("bias_row", [P, DIM], F32)
        xn = sb("xn", [P, 2, DIM], F32)
        amax, xs, inv = (sb(n, [P, 2, 2], F32) for n in ("amax", "x_scale", "x_inv"))
        qa, qb = sb("q_a", [P, 2, DIM], F32), sb("q_b", [P, 2, DIM], F32)
        xq = [sb(f"xq{i}", [P, 2, DIM], F16) for i in range(2)]
        xqt = [sb(f"xqT{i}", [P, DC, SEQ], F16) for i in range(2)]
        ya, yb = sb("y_a", [P, 2, DIM], F32), sb("y_b", [P, 2, DIM], F32)
        loaded, w_ready = sem("loaded"), sem("w_ready")
        step, quantised = sem("quant_step"), sem("quantised")
        turned, copied, product, out_step, updated = sem("turned"), sem("copied"), sem("product"), sem("out_step"), sem("updated")
        block = ctx.enter_context(nc.Block())

        @block.sync
        def _(sp):
            sp.dma_start(w8[:], c.dram["l1f_w"]).then_inc(loaded, 16)
            sp.dma_start(w_row[:], c.dram["l1f_scale"].partition_broadcast(P)).then_inc(loaded, 16)
            sp.dma_start(b_row[:], c.dram["l1f_bias"].partition_broadcast(P)).then_inc(loaded, 16)
            sp.wait_ge(loaded, 48)

        @block.gpsimd
        def _(pool):
            prep_weights(nc, c, pool, next_weights)

        @block.vector
        def _(dve):
            def quantise(b, s):
                if s != -2:
                    return
                i = b.off % 2
                n = lambda k: b.count(7, k)
                for t in range(2):
                    tile = b.count(2, t)
                    last = nc.vector.tensor_scalar(xn[:, t, :], c.x[:, tile, :], c.mv[:, tile, 0:1],
                                                   c.rstd[:, bass.ds(tile, 1)], ALU.subtract, ALU.mult)
                last.then_inc(step, 1)
                dve.wait_ge(step, n(1))
                nc.vector.tensor_reduce(amax[:, i, :], xn[:], AX.X, ALU.max, apply_absolute_value=True).then_inc(step, 1)
                dve.wait_ge(step, n(2))
                nc.vector.tensor_scalar(xs[:, i, :], amax[:, i, :], 1e-6, 1.0 / 127.0, ALU.max, ALU.mult).then_inc(step, 1)
                dve.wait_ge(step, n(3))
                nc.vector.reciprocal(inv[:, i, :], xs[:, i, :]).then_inc(step, 1)
                dve.wait_ge(step, n(4))
                for t in range(2):
                    last = nc.vector.tensor_scalar(qa[:, t, :], xn[:, t, :], inv[:, i, t:t + 1], 127.0, ALU.mult, ALU.min)
                last.then_inc(step, 1)
                dve.wait_ge(step, n(5))
                nc.vector.tensor_scalar(qb[:], qa[:], -128.0, ROUND, ALU.max, ALU.add).then_inc(step, 1)
                dve.wait_ge(step, n(6))
                wait(dve, turned, b.count(1, -1))
                nc.vector.tensor_scalar(xq[i][:], qb[:], ROUND, None, ALU.subtract).then_inc(step, 1)

            def finish(b, s):
                if s != 0:
                    return
                i = b.off % 2
                dve.wait_ge(product, b.count(1, 1))
                for t in range(2):
                    last = nc.vector.scalar_tensor_tensor(out=ya[:, t, :], in0=c.bank[2 + i][:, t * DIM:(t + 1) * DIM],
                                                          scalar=xs[:, i, t:t + 1], in1=w_row[:],
                                                          op0=ALU.mult, op1=ALU.mult)
                last.then_inc(out_step, 1)
                dve.wait_ge(out_step, b.count(2, 1))
                nc.vector.tensor_tensor(yb[:], ya[:], b_row[:].unsqueeze(1).broadcast_to([P, 2, DIM]),
                                        ALU.add).then_inc(out_step, 1)
                dve.wait_ge(out_step, b.count(2, 2))
                tile = b.count(2, 0)
                rows = c.x[:, bass.ds(tile, 2), :]
                nc.vector.scalar_tensor_tensor(out=rows, in0=yb[:], scalar=c.gates[:, gate:gate + 1], in1=rows,
                                               op0=ALU.mult, op1=ALU.add).then_inc(updated, 1)

            dve.wait_ge(loaded, 48)
            nc.vector.tensor_copy(w[:], w8[:].bitcast(mybir.dt.int8)).then_inc(w_ready, 1)
            over_steps(dve, 1, (finish, quantise))

        @block.tensor
        def _(pe):
            pe.wait_ge(w_ready, 1)

            def multiply(b, s):
                if s != 0:
                    return
                i = b.off % 2
                pe.wait_ge(copied, b.count(1, 1))
                wait(pe, updated, b.count(1, -1))
                for t in range(2):
                    for d in range(DC):
                        last = nc.tensor.matmul(c.bank[2 + i][:, t * DIM:(t + 1) * DIM],
                                                xqt[i][:, d, t * P:(t + 1) * P], w[:, d, :], start=d == 0, stop=d == 1)
                last.then_inc(product, 1)

            def turn(b, s):
                if s != -1:
                    return
                i = b.off % 2
                pe.wait_ge(step, b.count(7, 7))
                wait(pe, copied, b.count(1, -1))
                out = c.bank[i][:].bitcast(F16)
                for d in range(DC):
                    for t in range(2):
                        last = nc.tensor.transpose(out[:, d * SEQ + t * P:d * SEQ + (t + 1) * P],
                                                   xq[i][:, t, d * P:(d + 1) * P], c.ident_h[:])
                last.then_inc(turned, 1)

            over_steps(pe, 1, (multiply, turn))

        @block.scalar
        def _(act):
            def copy(b, s):
                if s != -1:
                    return
                i = b.off % 2
                act.wait_ge(turned, b.count(1, 1))
                wait(act, product, b.count(1, -1))
                nc.scalar.copy(xqt[i][:].rearrange("p d n -> p (d n)"),
                               c.bank[i][:].bitcast(F16)[:, 0:2 * SEQ]).then_inc(copied, 1)

            over_steps(act, 1, (copy,))


def scaled_linear(nc, c, tag, gate, weights):
    with ExitStack() as ctx:
        sb = lambda n, sh, dt: ctx.enter_context(nc.sbuf_tensor(f"{tag}_{n}", sh, dt))
        sem = ctx.enter_context(stage_semaphores(nc, tag))
        s_row, b_row = sb("scale_row", [P, DIM], F32), sb("bias_row", [P, DIM], F32)
        xn = [sb(f"xn{i}", [P, 2, DIM], F32) for i in range(2)]
        xt = [[sb(f"xT_{p}{i}", [P, DC, SEQ], F16) for p in ("hi", "lo")] for i in range(2)]
        ya = sb("y_a", [P, 2, DIM], F32)
        yb = sb("y_b", [P, 2, DIM], F32)
        loaded, rows_ready = sem("loaded"), sem("rows_ready")
        normed, turned, hi_done, lo_done = sem("normed"), sem("turned"), sem("hi_done"), sem("lo_done")
        product, out_step, updated = sem("product"), sem("out_step"), sem("updated")
        block = ctx.enter_context(nc.Block())

        @block.sync
        def _(sp):
            sp.dma_start(s_row[:], c.dram["l3f_scale"].partition_broadcast(P)).then_inc(loaded, 16)
            sp.dma_start(b_row[:], c.dram["l3f_bias"].partition_broadcast(P)).then_inc(loaded, 16)
            sp.wait_ge(loaded, 32)

        @block.vector
        def _(dve):
            def norm(b, s):
                if s != -2:
                    return
                wait(dve, turned, b.count(1, -1))
                for t in range(2):
                    tile = b.count(2, t)
                    last = nc.vector.tensor_scalar(xn[b.off % 2][:, t, :], c.x[:, tile, :], c.mv[:, tile, 0:1],
                                                   c.rstd[:, bass.ds(tile, 1)], ALU.subtract, ALU.mult)
                last.then_inc(normed, 1)

            def split(b, s):
                if s != -1:
                    return
                i = b.off % 2
                hi, lo = (x[:].rearrange("p d n -> p (d n)") for x in xt[i])
                dve.wait_ge(hi_done, b.count(1, 1))
                nc.vector.tensor_tensor(lo, c.bank[i][:], hi, ALU.subtract).then_inc(lo_done, 1)

            def finish(b, s):
                if s != 0:
                    return
                dve.wait_ge(product, b.count(1, 1))
                nc.vector.tensor_tensor(ya[:], c.bank[2 + b.off % 2][:].rearrange("p (t d) -> p t d", t=2),
                                        s_row[:].unsqueeze(1).broadcast_to([P, 2, DIM]), ALU.mult).then_inc(out_step, 1)
                dve.wait_ge(out_step, b.count(2, 1))
                nc.vector.tensor_tensor(yb[:], ya[:], b_row[:].unsqueeze(1).broadcast_to([P, 2, DIM]),
                                        ALU.add).then_inc(out_step, 1)
                dve.wait_ge(out_step, b.count(2, 2))
                rows = c.x[:, bass.ds(b.count(2, 0), 2), :]
                nc.vector.tensor_tensor(rows, yb[:], rows, ALU.add).then_inc(updated, 1)

            dve.wait_ge(loaded, 32)
            g = c.gates[:, gate:gate + 1]
            nc.vector.tensor_scalar(s_row[:], s_row[:], 1.0 / 127.0 / W_SCALE, g, ALU.mult, ALU.mult).then_inc(rows_ready, 1)
            nc.vector.tensor_scalar(b_row[:], b_row[:], g, None, ALU.mult).then_inc(rows_ready, 1)
            dve.wait_ge(rows_ready, 2)
            over_steps(dve, 1, (finish, split, norm))

        @block.scalar
        def _(act):
            def copy(b, s):
                if s != -1:
                    return
                i = b.off % 2
                act.wait_ge(turned, b.count(1, 1))
                nc.scalar.copy(xt[i][0][:].rearrange("p d n -> p (d n)"), c.bank[i][:]).then_inc(hi_done, 1)

            over_steps(act, 1, (copy,))

        @block.tensor
        def _(pe):
            w = lambda d: tuple(c.arena[weights.slot][:, k, d * DIM:(d + 1) * DIM] for k in range(2))

            def multiply(b, s):
                if s != 0:
                    return
                i = b.off % 2
                pe.wait_ge(lo_done, b.count(1, 1))
                wait(pe, updated, b.count(1, -1))
                for t in range(2):
                    for d in range(DC):
                        last = three_products(nc, c.bank[2 + i][:, t * DIM:(t + 1) * DIM],
                                              [x[:, d, t * P:(t + 1) * P] for x in xt[i]], w(d), d == 0, d == DC - 1)
                last.then_inc(product, 1)

            def turn(b, s):
                if s != -1:
                    return
                i = b.off % 2
                pe.wait_ge(normed, b.count(1, 1))
                wait(pe, lo_done, b.count(1, -1))
                for d in range(DC):
                    for t in range(2):
                        last = nc.tensor.transpose(c.bank[i][:, d * SEQ + t * P:d * SEQ + (t + 1) * P],
                                                   xn[i][:, t, d * P:(d + 1) * P], c.ident[:])
                last.then_inc(turned, 1)

            over_steps(pe, 1, (multiply, turn))


def norm_context(nc, c, tag, gain, shift):
    with ExitStack() as ctx:
        sb = lambda n, sh, dt: ctx.enter_context(nc.sbuf_tensor(f"{tag}_{n}", sh, dt))
        sem = ctx.enter_context(stage_semaphores(nc, tag))
        cx = sb("rows", [KEYS, BATCH, DIM], F32)
        stats, mv = sb("stats", [KEYS, BATCH, 6], F32), sb("mv", [KEYS, BATCH, 2], F32)
        var_eps, rstd = sb("var_eps", [KEYS, BATCH], F32), sb("rstd", [KEYS, BATCH], F32)
        g, b = sb("gain", [P, DC], F32), sb("shift", [P, DC], F32)
        scaled = sb("scaled", [P, 2, 4 * KEYS], F32)
        loaded, stat_done, var_done, pow_done = sem("loaded"), sem("stat_done"), sem("var_done"), sem("pow_done")
        normed, full, affine, hi_done, lo_done = (sem(n) for n in ("normed", "full", "affine", "hi_done", "lo_done"))
        block = ctx.enter_context(nc.Block())
        groups = DC * BATCH // 4

        def cut(grp):
            return grp % DC, grp // DC * 4

        @block.sync
        def _(sp):
            sp.dma_start(cx[:], c.dram["ctx_1024"].rearrange("b k d -> k b d")).then_inc(loaded, 16)
            sp.dma_start(g[:], gain).then_inc(loaded, 16)
            sp.dma_start(b[:], shift).then_inc(loaded, 16)

        @block.vector
        def _(dve):
            dve.wait_ge(loaded, 48)
            for k in range(BATCH):
                nc.vector.bn_stats(stats[:, k, :], cx[:, k, :]).then_inc(stat_done, 1)
            for k in range(BATCH):
                dve.wait_ge(stat_done, k + 1)
                nc.vector.bn_aggr(mv[:, k, :], stats[:, k, :]).then_inc(var_done, 1)
            dve.wait_ge(pow_done, 2)
            for k in range(BATCH):
                nc.vector.tensor_scalar(cx[:, k, :], cx[:, k, :], mv[:, k, 0:1], rstd[:, k:k + 1],
                                        ALU.subtract, ALU.mult).then_inc(normed, 1)
            for grp in range(groups):
                d, b0 = cut(grp)
                cols = slice(b0 * KEYS, (b0 + 4) * KEYS)
                dve.wait_ge(affine, grp + 1)
                nc.vector.tensor_copy(c.ct[0][:, d, cols], scaled[:, grp % 2, :]).then_inc(hi_done, 1)
                dve.wait_ge(hi_done, grp + 1)
                nc.vector.tensor_tensor(c.ct[1][:, d, cols], scaled[:, grp % 2, :], c.ct[0][:, d, cols],
                                        ALU.subtract).then_inc(lo_done, 1)

        @block.gpsimd
        def _(pool):
            col = lambda i: c.consts[0:KEYS, i:i + 1].broadcast_to([KEYS, BATCH])
            pool.wait_ge(var_done, BATCH)
            nc.gpsimd.tensor_tensor(var_eps[:], mv[:, :, 1], col(0), ALU.add).then_inc(pow_done, 1)
            pool.wait_ge(pow_done, 1)
            nc.gpsimd.tensor_tensor(rstd[:], var_eps[:], col(1), ALU.pow).then_inc(pow_done, 1)

        @block.tensor
        def _(pe):
            for grp in range(groups):
                d, b0 = cut(grp)
                pe.wait_ge(normed, b0 + 4)
                wait(pe, affine, grp - 1)
                for j in range(4):
                    last = nc.tensor.transpose(c.bank[grp % 2][:, j * KEYS:(j + 1) * KEYS],
                                               cx[:, b0 + j, d * P:(d + 1) * P], c.ident[0:KEYS, 0:KEYS])
                last.then_inc(full, 1)

        @block.scalar
        def _(act):
            act.wait_ge(loaded, 48)
            for grp in range(groups):
                d, b0 = cut(grp)
                wait(act, lo_done, grp - 1)
                act.wait_ge(full, grp + 1)
                nc.scalar.activation(scaled[:, grp % 2, :], c.bank[grp % 2][:, 0:4 * KEYS], ACT.Identity,
                                     bias=b[:, d:d + 1], scale=g[:, d:d + 1]).then_inc(affine, 1)


class GatedFf:

    def __init__(self, tag, weights, hidden, source, finish, gate=None, combine=None, norm_g=None, norm_b=None,
                 gate_first=False):
        self.tag, self.weights, self.nh, self.source, self.finish = tag, weights, hidden, source, finish
        self.gate, self.combine, self.norm_g, self.norm_b, self.gate_first = gate, combine, norm_g, norm_b, gate_first


def gated_ff(nc, c, f, next_weights):
    nh = f.nh
    with ExitStack() as ctx:
        sb = lambda n, sh, dt: ctx.enter_context(nc.sbuf_tensor(f"{f.tag}_{n}", sh, dt))
        sem = ctx.enter_context(stage_semaphores(nc, f.tag))
        xn = sb("rows", [P, 2, DIM], F32)
        xt = [[sb(f"xT_{p}{i}", [P, DC, SEQ], F16) for p in ("hi", "lo")] for i in range(2)]
        silu = [sb(f"silu{i}", [P, SEQ], F32) for i in range(2)]
        prod = [sb(f"prod{i}", [P, SEQ], F32) for i in range(2)]
        g = [[sb(f"g_{p}{i}", [P, nh, SEQ], F16) for p in ("hi", "lo")] for i in range(2)]
        if f.norm_g is not None:
            gain, shift = sb("gain", [P, DC], F32), sb("shift", [P, DC], F32)
            xf = sb("xT_f32", [P, DC, SEQ], F32)
        if f.finish == "pair":
            y = sb("y", [P, 2, DIM], F32)
        loaded = sem("loaded")
        rows_ready, x_full, x_hi, x_split, x_free = (sem(n) for n in ("rows_ready", "x_full", "x_hi", "x_split", "x_free"))
        up_full, silu_done, prod_done, g_hi, g_lo = (sem(n) for n in ("up_full", "silu_done", "prod_done", "g_hi", "g_lo"))
        down_full, y_done, bank_free = sem("down_full"), sem("y_done"), sem("bank_free")
        block = ctx.enter_context(nc.Block())

        w_hi, w_lo = (c.arena[f.weights.slot][:, i, :] for i in range(2))
        weight = lambda off, n: (w_hi[:, off:off + n], w_lo[:, off:off + n])
        hid = nh * P
        up_off, gate_off = (hid, 0) if f.gate_first else (0, hid)
        down_off = DC * 2 * hid

        @block.gpsimd
        def _(pool):
            prep_weights(nc, c, pool, next_weights)

        @block.sync
        def _(sp):
            if f.norm_g is not None:
                sp.dma_start(gain[:], f.norm_g).then_inc(loaded, 16)
                sp.dma_start(shift[:], f.norm_b).then_inc(loaded, 16)
                sp.wait_ge(loaded, 32)

        @block.tensor
        def _(pe):
            def up(b, s):
                if not 0 <= s < nh:
                    return
                if s == 0:
                    pe.wait_ge(x_free, b.count(1, 1))
                wait(pe, g_lo, b.count(nh, s - 1))
                for i, off in enumerate((gate_off, up_off)):
                    for d in range(DC):
                        last = three_products(nc, c.bank[s % 2][:, i * SEQ:(i + 1) * SEQ],
                                              weight(d * 2 * hid + off + s * P, P),
                                              [x[:, d, :] for x in xt[b.off % 2]], d == 0, d == DC - 1)
                last.then_inc(up_full, 1)

            def down(b, s):
                t = s - nh - 1
                if not 0 <= t < 2:
                    return
                if t == 0:
                    pe.wait_ge(g_lo, b.count(nh, nh))
                    wait(pe, bank_free, b.count(1, 0))
                for j in range(nh):
                    last = three_products(nc, c.bank[4 + b.off % 2][:, t * DIM:(t + 1) * DIM],
                                          [x[:, j, t * P:(t + 1) * P] for x in g[b.off % 2]],
                                          weight(down_off + j * DIM, DIM), j == 0, j == nh - 1)
                if t == 1:
                    last.then_inc(down_full, 1)

            def turn(b, s):
                if s != -3:
                    return
                pe.wait_ge(rows_ready, b.count(1, 1))
                wait(pe, x_free, b.count(1, 0))
                for d in range(DC):
                    for t in range(2):
                        last = nc.tensor.transpose(c.bank[6][:, d * SEQ + t * P:d * SEQ + (t + 1) * P],
                                                   xn[:, t, d * P:(d + 1) * P], c.ident[:])
                last.then_inc(x_full, 1)

            over_steps(pe, nh, (up, down, turn))

        @block.scalar
        def _(act):
            if f.norm_g is not None:
                act.wait_ge(loaded, 32)

            def silus(b, s):
                if not 0 <= s < nh:
                    return
                act.wait_ge(up_full, b.count(nh, s + 1))
                nc.scalar.activation(silu[s % 2][:], c.bank[s % 2][:, 0:SEQ], ACT.Silu,
                                     scale=1.0 / W_SCALE).then_inc(silu_done, 1)

            def hi(b, s):
                j = s - 1
                if not 0 <= j < nh:
                    return
                act.wait_ge(prod_done, b.count(nh, j + 1))
                if j == 0:
                    wait(act, down_full, b.count(1, -1))
                nc.scalar.copy(g[b.off % 2][0][:, j, :], prod[j % 2][:]).then_inc(g_hi, 1)

            def rows_hi(b, s):
                if s != -3:
                    return
                act.wait_ge(x_full, b.count(1, 1))
                if f.norm_g is not None:
                    wait(act, x_free, b.count(1, 0))
                    for d in range(DC):
                        last = nc.scalar.activation(xf[:, d, :], c.bank[6][:, d * SEQ:(d + 1) * SEQ], ACT.Identity,
                                                    bias=shift[:, d:d + 1], scale=gain[:, d:d + 1])
                else:
                    last = nc.scalar.copy(xt[b.off % 2][0][:].rearrange("p d n -> p (d n)"), c.bank[6][:])
                last.then_inc(x_hi, 1)

            over_steps(act, nh, (silus, hi, rows_hi))

        @block.vector
        def _(dve):
            def products(b, s):
                if not 0 <= s < nh:
                    return
                dve.wait_ge(silu_done, b.count(nh, s + 1))
                nc.vector.scalar_tensor_tensor(out=prod[s % 2][:], in0=c.bank[s % 2][:, SEQ:2 * SEQ],
                                               scalar=1.0 / W_SCALE, in1=silu[s % 2][:],
                                               op0=ALU.mult, op1=ALU.mult).then_inc(prod_done, 1)

            def lo(b, s):
                j = s - 1
                if not 0 <= j < nh:
                    return
                dve.wait_ge(g_hi, b.count(nh, j + 1))
                hi_part, lo_part = (x[:, j, :] for x in g[b.off % 2])
                nc.vector.tensor_tensor(lo_part, prod[j % 2][:], hi_part, ALU.subtract).then_inc(g_lo, 1)

            def rows(b, s):
                if s != -4:
                    return
                wait(dve, x_full, b.count(1, 0))
                for t in range(2):
                    tile = b.count(2, t)
                    rstd = c.rstd[:, bass.ds(tile, 1)]
                    if f.source == "x":
                        last = nc.vector.tensor_scalar(xn[:, t, :], c.x[:, tile, :], c.mv[:, tile, 0:1], rstd,
                                                       ALU.subtract, ALU.mult)
                    else:
                        last = nc.vector.tensor_scalar(xn[:, t, :], c.h[:, tile, :], rstd, None, ALU.mult)
                last.then_inc(rows_ready, 1)

            def rows_lo(b, s):
                if s != -3:
                    return
                dve.wait_ge(x_hi, b.count(1, 1))
                hi_part, lo_part = (x[:].rearrange("p d n -> p (d n)") for x in xt[b.off % 2])
                src = c.bank[6][:]
                if f.norm_g is not None:
                    src = xf[:].rearrange("p d n -> p (d n)")
                    nc.vector.tensor_copy(hi_part, src).then_inc(x_split, 1)
                    dve.wait_ge(x_split, b.count(1, 1))
                nc.vector.tensor_tensor(lo_part, src, hi_part, ALU.subtract).then_inc(x_free, 1)

            def update(b, s):
                if s != nh + 3:
                    return
                dve.wait_ge(down_full, b.count(1, 1))
                bank = c.bank[4 + b.off % 2]
                two = bass.ds(b.count(2, 0), 2)
                if f.finish == "pair":
                    nc.vector.scalar_tensor_tensor(out=y[:], in0=bank[:].rearrange("p (t d) -> p t d", t=2),
                                                   scalar=1.0 / W_SCALE, in1=c.h[:, two, :],
                                                   op0=ALU.mult, op1=ALU.add).then_inc(y_done, 1)
                    dve.wait_ge(y_done, b.count(1, 1))
                    nc.vector.scalar_tensor_tensor(out=c.x[:, two, :], in0=y[:], scalar=c.gates[:, f.gate:f.gate + 1],
                                                   in1=c.x[:, two, :], op0=ALU.mult, op1=ALU.add).then_inc(bank_free, 1)
                else:
                    for t in range(2):
                        tile = b.count(2, t)
                        last = nc.vector.scalar_tensor_tensor(out=c.x[:, tile, :], in0=bank[:, t * DIM:(t + 1) * DIM],
                                                              scalar=f.combine[:, bass.ds(tile, 1)],
                                                              in1=c.x[:, tile, :], op0=ALU.mult, op1=ALU.add)
                    last.then_inc(bank_free, 1)

            dve.sem_inc(bank_free, 1)
            over_steps(dve, nh, (products, lo, rows_lo, rows, update))


EXPERTS = 8
PICKED = 2
CAPACITY = TOKENS // EXPERTS
FLAGS = TILES * EXPERTS
BISECTIONS = 40


def by_expert(x):
    return x.rearrange("p (t e) -> p e t", e=EXPERTS)


def over_tiles(x):
    return x.unsqueeze(1).broadcast_to([P, TILES, EXPERTS])


def tiled(x):
    return x.rearrange("p (t e) -> p t e", e=EXPERTS)


def over_experts(x):
    return x.unsqueeze(2).broadcast_to([P, TILES, EXPERTS])


def norm_rows_of_h(nc, c, tag):
    with ExitStack() as ctx:
        sem = ctx.enter_context(stage_semaphores(nc, tag))
        stat_done, var_done, pow_done = sem("stat_done"), sem("var_done"), sem("pow_done")
        block = ctx.enter_context(nc.Block())

        @block.vector
        def _(dve):
            for t in range(TILES):
                nc.vector.bn_stats(c.stats[:, t, :], c.h[:, t, :]).then_inc(stat_done, 1)
            for t in range(TILES):
                dve.wait_ge(stat_done, t + 1)
                nc.vector.bn_aggr(c.mv[:, t, :], c.stats[:, t, :]).then_inc(var_done, 1)

        @block.gpsimd
        def _(pool):
            def col(i):
                return c.consts[:, i:i + 1].broadcast_to([P, TILES])
            pool.wait_ge(var_done, TILES)
            mean, var = c.mv[:, :, 0], c.mv[:, :, 1]
            nc.gpsimd.tensor_tensor(c.tmp_a[:], mean, mean, ALU.mult).then_inc(pow_done, 1)
            pool.wait_ge(pow_done, 1)
            nc.gpsimd.tensor_tensor(c.tmp_a[:], c.tmp_a[:], var, ALU.add).then_inc(pow_done, 1)
            pool.wait_ge(pow_done, 2)
            nc.gpsimd.tensor_tensor(c.tmp_a[:], c.tmp_a[:], col(2), ALU.add).then_inc(pow_done, 1)
            pool.wait_ge(pow_done, 3)
            nc.gpsimd.tensor_tensor(c.rstd[:], c.tmp_a[:], col(1), ALU.pow).then_inc(pow_done, 1)


def normalise_into_h(nc, c, tag):
    with ExitStack() as ctx:
        sem = ctx.enter_context(stage_semaphores(nc, tag))
        rows_done, ones_done = sem("rows_done"), sem("ones_done")
        block = ctx.enter_context(nc.Block())

        @block.vector
        def _(dve):
            for t in range(TILES):
                nc.vector.tensor_scalar(c.h[:, t, :], c.x[:, t, :], c.mv[:, t, 0:1], c.rstd[:, t:t + 1],
                                        ALU.subtract, ALU.mult).then_inc(rows_done, 1)

        @block.gpsimd
        def _(pool):
            pool.wait_ge(rows_done, TILES)
            nc.gpsimd.memset(c.rstd[:], 1.0).then_inc(ones_done, 1)


def router_scores(nc, c, r, tag, weight_off, slot, norm_g=None, norm_b=None):
    with ExitStack() as ctx:
        sb = lambda n, sh, dt: ctx.enter_context(nc.sbuf_tensor(f"{tag}_{n}", sh, dt))
        sem = ctx.enter_context(stage_semaphores(nc, tag))
        xn = [sb(f"xn{i}", [P, 2, DIM], F32) for i in range(2)]
        xf = [sb(f"xT_f32{i}", [P, DC, SEQ], F32) for i in range(2)]
        xt = [[sb(f"xT_{p}{i}", [P, DC, SEQ], F16) for p in ("hi", "lo")] for i in range(2)]
        gain, shift = sb("gain", [P, DC], F32), sb("shift", [P, DC], F32)
        loaded, rows_ready, turned, copied = sem("loaded"), sem("rows_ready"), sem("turned"), sem("copied")
        hi_done, lo_done, product, stored = sem("hi_done"), sem("lo_done"), sem("product"), sem("stored")
        block = ctx.enter_context(nc.Block())

        @block.sync
        def _(sp):
            sp.dma_start(gain[:], norm_g).then_inc(loaded, 16)
            sp.dma_start(shift[:], norm_b).then_inc(loaded, 16)
            sp.wait_ge(loaded, 32)

        @block.vector
        def _(dve):
            def rows(b, s):
                if s != -2:
                    return
                wait(dve, turned, b.count(1, -1))
                for t in range(2):
                    tile = b.count(2, t)
                    last = nc.vector.tensor_scalar(xn[b.off % 2][:, t, :], c.h[:, tile, :],
                                                   c.rstd[:, bass.ds(tile, 1)], None, ALU.mult)
                last.then_inc(rows_ready, 1)

            def split(b, s):
                if s != -1:
                    return
                i = b.off % 2
                src = xf[i][:].rearrange("p d n -> p (d n)")
                hi, lo = (x[:].rearrange("p d n -> p (d n)") for x in xt[i])
                dve.wait_ge(copied, b.count(1, 1))
                wait(dve, product, b.count(1, -1))
                nc.vector.tensor_copy(hi, src).then_inc(hi_done, 1)
                dve.wait_ge(hi_done, b.count(1, 1))
                nc.vector.tensor_tensor(lo, src, hi, ALU.subtract).then_inc(lo_done, 1)

            def finish(b, s):
                if s != 0:
                    return
                dve.wait_ge(product, b.count(1, 1))
                nc.vector.tensor_scalar(r.scores[:, bass.ds(b.count(2 * EXPERTS, 0), 2 * EXPERTS)],
                                        c.bank[2 + b.off % 2][:, 0:2 * EXPERTS], 1.0 / W_SCALE, None,
                                        ALU.mult).then_inc(stored, 1)

            over_steps(dve, 1, (finish, split, rows))

        @block.scalar
        def _(act):
            def affine(b, s):
                if s != -1:
                    return
                i = b.off % 2
                act.wait_ge(turned, b.count(1, 1))
                wait(act, lo_done, b.count(1, -1))
                for d in range(DC):
                    last = nc.scalar.activation(xf[i][:, d, :], c.bank[i][:, d * SEQ:(d + 1) * SEQ], ACT.Identity,
                                                bias=shift[:, d:d + 1], scale=gain[:, d:d + 1])
                last.then_inc(copied, 1)

            act.wait_ge(loaded, 32)
            over_steps(act, 1, (affine,))

        @block.tensor
        def _(pe):
            w = lambda d: tuple(c.arena[slot][:, k, weight_off + d * EXPERTS:weight_off + (d + 1) * EXPERTS]
                                for k in range(2))

            def multiply(b, s):
                if s != 0:
                    return
                i = b.off % 2
                pe.wait_ge(lo_done, b.count(1, 1))
                wait(pe, stored, b.count(1, -1))
                for t in range(2):
                    for d in range(DC):
                        last = three_products(nc, c.bank[2 + i][:, t * EXPERTS:(t + 1) * EXPERTS],
                                              [x[:, d, t * P:(t + 1) * P] for x in xt[i]], w(d), d == 0, d == DC - 1)
                last.then_inc(product, 1)

            def turn(b, s):
                if s != -1:
                    return
                i = b.off % 2
                pe.wait_ge(rows_ready, b.count(1, 1))
                wait(pe, copied, b.count(1, -1))
                for d in range(DC):
                    for t in range(2):
                        last = nc.tensor.transpose(c.bank[i][:, d * SEQ + t * P:d * SEQ + (t + 1) * P],
                                                   xn[i][:, t, d * P:(d + 1) * P], c.ident[:])
                last.then_inc(turned, 1)

            over_steps(pe, 1, (multiply, turn))


class Steps:

    def __init__(self, eng, sem):
        self.eng, self.sem, self.n = eng, sem, 0

    def __call__(self, ins):
        ins.then_inc(self.sem, 1)
        self.n += 1
        self.eng.wait_ge(self.sem, self.n)


class Routing:

    def __init__(self, nc, ctx):
        sb = lambda n, sh, dt: ctx.enter_context(nc.sbuf_tensor(n, sh, dt))
        self.scores = sb("scores", [P, FLAGS], F32)
        self.combine = sb("combine", [P, FLAGS], F32)
        self.by_expert = sb("combine_by_expert", [P, FLAGS], F32)
        self.flags = sb("flags", [P, FLAGS], F32)
        self.flags_h = sb("flags_h", [P, FLAGS], F16)
        self.prefix = sb("prefix", [P, FLAGS], F32)
        self.total = sb("total", [P, EXPERTS], F32)
        self.t = [sb(f"route_tmp{i}", [P, FLAGS], F32) for i in range(4)]
        self.s = [sb(f"route_small{i}", [P, TILES], F32) for i in range(4)]
        self.order = sb("order", [P, EXPERTS], F32)
        self.low, self.high, self.top = (sb(n, [P, EXPERTS], F32) for n in ("low", "high", "top_score"))
        self.ones = sb("route_ones", [P, P], F16)
        self.before = sb("before", [P, P], F16)


def make_routing(nc, ctx):
    r = Routing(nc, ctx)
    with ExitStack() as inner:
        step = inner.enter_context(stage_semaphores(nc, "routing"))("step")
        block = inner.enter_context(nc.Block())

        @block.gpsimd
        def _(pool):
            did = Steps(pool, step)
            for e in range(EXPERTS):
                did(nc.gpsimd.memset(r.order[:, e:e + 1], float(EXPERTS - e)))
            did(nc.gpsimd.memset(r.ones[:], 1.0))
            did(nc.gpsimd.memset(r.before[:], 1.0))
            did(nc.gpsimd.affine_select(out=r.before[:], in_=r.before[:], compare_op=ALU.is_ge, fill=0.0,
                                        base=-1, pattern=[[1, P]], channel_multiplier=-1))
    return r


def prefix_counts(nc, r, c, tag):
    with ExitStack() as ctx:
        sem = ctx.enter_context(stage_semaphores(nc, tag))
        halved, counted, step = sem("halved"), sem("counted"), sem("step")
        block = ctx.enter_context(nc.Block())
        within, totals = c.bank[0][:, 0:FLAGS], c.bank[1][:, 0:FLAGS]

        @block.vector
        def _(dve):
            did = Steps(dve, step)
            nc.vector.tensor_copy(r.flags_h[:], r.flags[:]).then_inc(halved, 1)
            dve.wait_ge(counted, 2)
            a, b = r.t[0], r.t[1]
            did(nc.vector.tensor_copy(a[:], totals))
            for k in (1, 2, 4, 8, 16):
                w = k * EXPERTS
                did(nc.vector.tensor_tensor(b[:, w:], a[:, w:], a[:, 0:FLAGS - w], ALU.add))
                did(nc.vector.tensor_copy(b[:, 0:w], a[:, 0:w]))
                a, b = b, a
            did(nc.vector.tensor_copy(r.total[:], a[:, FLAGS - EXPERTS:]))
            did(nc.vector.tensor_tensor(b[:], a[:], totals, ALU.subtract))
            did(nc.vector.tensor_tensor(r.prefix[:], b[:], within, ALU.add))

        @block.tensor
        def _(pe):
            pe.wait_ge(halved, 1)
            nc.tensor.matmul(within, r.before[:], r.flags_h[:], start=True, stop=True).then_inc(counted, 1)
            nc.tensor.matmul(totals, r.ones[:], r.flags_h[:], start=True, stop=True).then_inc(counted, 1)


def pick_two(nc, c, r, tag, gate):
    with ExitStack() as ctx:
        sem = ctx.enter_context(stage_semaphores(nc, tag))
        step, gap_ready, exp_done = sem("step"), sem("gap_ready"), sem("exp_done")
        block = ctx.enter_context(nc.Block())

        @block.vector
        def _(dve):
            did = Steps(dve, step)
            tt = lambda out, a, b, op: did(nc.vector.tensor_tensor(out, a, b, op))
            left, one = r.t[0], r.t[1]
            for k in range(PICKED):
                src, flag, top = (r.scores, left)[k], r.t[2 + k], r.s[k]
                did(nc.vector.tensor_reduce(top[:], tiled(src[:]), AX.X, ALU.max))
                tt(tiled(one[:]), tiled(src[:]), over_experts(top[:]), ALU.is_equal)
                tt(tiled(one[:]), tiled(one[:]), over_tiles(r.order[:]), ALU.mult)
                did(nc.vector.tensor_reduce(r.s[2][:], tiled(one[:]), AX.X, ALU.max))
                tt(tiled(flag[:]), tiled(one[:]), over_experts(r.s[2][:]), ALU.is_equal)
                if k == 0:
                    did(nc.vector.scalar_tensor_tensor(out=left[:], in0=flag[:], scalar=NEG_BIG, in1=r.scores[:],
                                                       op0=ALU.mult, op1=ALU.add))
            nc.vector.tensor_tensor(r.s[2][:], r.s[1][:], r.s[0][:], ALU.subtract).then_inc(gap_ready, 1)
            dve.wait_ge(exp_done, 1)
            did(nc.vector.tensor_scalar(r.s[2][:], r.s[3][:], 1.0, None, ALU.add))
            did(nc.vector.reciprocal(r.s[0][:], r.s[2][:]))
            tt(r.s[1][:], r.s[0][:], r.s[3][:], ALU.mult)
            tt(tiled(r.t[0][:]), tiled(r.t[2][:]), over_experts(r.s[0][:]), ALU.mult)
            tt(tiled(r.t[1][:]), tiled(r.t[3][:]), over_experts(r.s[1][:]), ALU.mult)
            tt(r.combine[:], r.t[0][:], r.t[1][:], ALU.add)
            did(nc.vector.tensor_scalar(r.combine[:], r.combine[:], 1.0 / W_SCALE, c.gates[:, gate:gate + 1],
                                        ALU.mult, ALU.mult))
            did(nc.vector.tensor_copy(r.by_expert[:].rearrange("p (e t) -> p e t", e=EXPERTS),
                                      by_expert(r.combine[:])))

        @block.scalar
        def _(act):
            act.wait_ge(gap_ready, 1)
            nc.scalar.activation(r.s[3][:], r.s[2][:], ACT.Exp).then_inc(exp_done, 1)


def find_thresholds(nc, c, r, tag):
    with ExitStack() as ctx:
        sb = lambda n: ctx.enter_context(nc.sbuf_tensor(f"{tag}_{n}", [P, EXPERTS], F32))
        sem = ctx.enter_context(stage_semaphores(nc, tag))
        bound, middle, stride, over, big = (sb(n) for n in ("bound", "middle", "stride", "over", "big"))
        counts = ctx.enter_context(nc.sbuf_tensor(f"{tag}_counts", [P, EXPERTS], F16))
        step, reduced, prepared, bisect, counted, summed = (
            sem(n) for n in ("step", "reduced", "prepared", "bisect", "counted", "summed"))
        block = ctx.enter_context(nc.Block())
        chain = 9

        @block.gpsimd
        def _(pool):
            nc.gpsimd.partition_all_reduce(r.t[0][:], r.scores[:], P, bass.bass_isa.ReduceOp.absmax).then_inc(reduced, 1)
            nc.gpsimd.partition_all_reduce(r.t[1][:], r.scores[:], P, bass.bass_isa.ReduceOp.max).then_inc(reduced, 1)

        @block.vector
        def _(dve):
            did = Steps(dve, step)
            dve.wait_ge(reduced, 2)
            did(nc.vector.tensor_reduce(bound[:], by_expert(r.t[0][:]), AX.X, ALU.max))
            did(nc.vector.tensor_reduce(r.top[:], by_expert(r.t[1][:]), AX.X, ALU.max))
            did(nc.vector.tensor_scalar(r.low[:], bound[:], -1.0, None, ALU.mult))
            did(nc.vector.tensor_scalar(r.high[:], bound[:], 0.0, -NEG_BIG, ALU.mult, ALU.add))
            did(nc.vector.tensor_scalar(big[:], bound[:], 0.0, -NEG_BIG, ALU.mult, ALU.add))
            did(nc.vector.tensor_copy(stride[:], bound[:]))
            with dve.Fori(0, BISECTIONS) as i:
                n = 0

                def then(ins):
                    nonlocal n
                    n += 1
                    ins.then_inc(bisect, 1)
                    dve.wait_ge(bisect, i * chain + n)

                then(nc.vector.tensor_tensor(middle[:], r.low[:], stride[:], ALU.add))
                then(nc.vector.tensor_tensor(tiled(r.flags[:]), tiled(r.scores[:]), over_tiles(middle[:]), ALU.is_ge))
                then(nc.vector.tensor_reduce(over[:], by_expert(r.flags[:]), AX.X, ALU.add))
                nc.vector.tensor_copy(counts[:], over[:]).then_inc(counted, 1)
                dve.wait_ge(summed, i + 1)
                total = c.bank[0][:, 0:EXPERTS]
                then(nc.vector.scalar_tensor_tensor(out=over[:], in0=total, scalar=float(CAPACITY), in1=stride[:],
                                                    op0=ALU.is_ge, op1=ALU.mult))
                then(nc.vector.tensor_tensor(r.low[:], r.low[:], over[:], ALU.add))
                then(nc.vector.scalar_tensor_tensor(out=over[:], in0=total, scalar=float(CAPACITY), in1=big[:],
                                                    op0=ALU.is_ge, op1=ALU.mult))
                then(nc.vector.tensor_tensor(over[:], over[:], middle[:], ALU.add))
                then(nc.vector.tensor_tensor(r.high[:], r.high[:], over[:], ALU.min))
                then(nc.vector.tensor_scalar(stride[:], stride[:], 0.5, None, ALU.mult))

        @block.tensor
        def _(pe):
            with pe.Fori(0, BISECTIONS) as i:
                pe.wait_ge(counted, i + 1)
                nc.tensor.matmul(c.bank[0][:, 0:EXPERTS], r.ones[:], counts[:], start=True, stop=True).then_inc(summed, 1)


def flag_ties(nc, c, r, tag):
    with ExitStack() as ctx:
        step = ctx.enter_context(stage_semaphores(nc, tag))("step")
        block = ctx.enter_context(nc.Block())

        @block.vector
        def _(dve):
            did = Steps(dve, step)
            did(nc.vector.tensor_tensor(tiled(r.t[0][:]), tiled(r.scores[:]), over_tiles(r.low[:]), ALU.is_ge))
            did(nc.vector.tensor_tensor(tiled(r.t[2][:]), tiled(r.scores[:]), over_tiles(r.high[:]), ALU.is_ge))
            did(nc.vector.tensor_tensor(r.flags[:], r.t[0][:], r.t[2][:], ALU.subtract))


def take_top(nc, c, r, tag, gate):
    with ExitStack() as ctx:
        sb = lambda n: ctx.enter_context(nc.sbuf_tensor(f"{tag}_{n}", [P, EXPERTS], F32))
        sem = ctx.enter_context(stage_semaphores(nc, tag))
        above, room, sums, total = sb("above"), sb("room"), sb("sums"), sb("sums_all")
        above_all = sb("above_all")
        step, above_ready, above_summed = sem("step"), sem("above_ready"), sem("above_summed")
        gap_ready, exp_done, sums_ready, sums_done = sem("gap_ready"), sem("exp_done"), sem("sums_ready"), sem("sums_done")
        block = ctx.enter_context(nc.Block())

        @block.vector
        def _(dve):
            did = Steps(dve, step)
            tt = lambda out, a, b, op: did(nc.vector.tensor_tensor(out, a, b, op))
            nc.vector.tensor_reduce(above[:], by_expert(r.t[2][:]), AX.X, ALU.add).then_inc(above_ready, 1)
            nc.vector.tensor_tensor(tiled(r.t[0][:]), tiled(r.scores[:]), over_tiles(r.top[:]),
                                    ALU.subtract).then_inc(gap_ready, 1)
            dve.wait_ge(above_summed, 1)
            did(nc.vector.tensor_scalar(room[:], above_all[:], -1.0, float(CAPACITY), ALU.mult, ALU.add))
            tt(tiled(r.t[3][:]), tiled(r.prefix[:]), over_tiles(room[:]), ALU.is_lt)
            tt(r.t[3][:], r.t[3][:], r.flags[:], ALU.mult)
            tt(r.flags[:], r.t[3][:], r.t[2][:], ALU.add)
            dve.wait_ge(exp_done, 1)
            tt(r.combine[:], r.t[1][:], r.flags[:], ALU.mult)
            nc.vector.tensor_reduce(sums[:], by_expert(r.combine[:]), AX.X, ALU.add).then_inc(sums_ready, 1)
            dve.wait_ge(sums_done, 1)
            did(nc.vector.reciprocal(room[:], total[:]))
            tt(tiled(r.combine[:]), tiled(r.combine[:]), over_tiles(room[:]), ALU.mult)
            did(nc.vector.tensor_scalar(r.combine[:], r.combine[:], 1.0 / W_SCALE, c.gates[:, gate:gate + 1],
                                        ALU.mult, ALU.mult))
            did(nc.vector.tensor_copy(r.by_expert[:].rearrange("p (e t) -> p e t", e=EXPERTS),
                                      by_expert(r.combine[:])))

        @block.gpsimd
        def _(pool):
            pool.wait_ge(above_ready, 1)
            nc.gpsimd.partition_all_reduce(above_all[:], above[:], P, bass.bass_isa.ReduceOp.add).then_inc(above_summed, 1)
            pool.wait_ge(sums_ready, 1)
            nc.gpsimd.partition_all_reduce(total[:], sums[:], P, bass.bass_isa.ReduceOp.add).then_inc(sums_done, 1)

        @block.scalar
        def _(act):
            act.wait_ge(gap_ready, 1)
            nc.scalar.activation(r.t[1][:], r.t[0][:], ACT.Exp).then_inc(exp_done, 1)


def add_h(nc, c, tag, gate):
    with ExitStack() as ctx:
        added = ctx.enter_context(stage_semaphores(nc, tag))("added")
        block = ctx.enter_context(nc.Block())

        @block.vector
        def _(dve):
            for t in range(0, TILES, 8):
                nc.vector.scalar_tensor_tensor(out=c.x[:, t:t + 8, :], in0=c.h[:, t:t + 8, :],
                                               scalar=c.gates[:, gate:gate + 1], in1=c.x[:, t:t + 8, :],
                                               op0=ALU.mult, op1=ALU.add).then_inc(added, 1)


def store_result(nc, c, out):
    with ExitStack() as ctx:
        stored = ctx.enter_context(nc.semaphore("stored"))
        block = ctx.enter_context(nc.Block())

        @block.sync
        def _(sp):
            sp.dma_start(out.rearrange("b (t p) d -> p (b t) d", p=P), c.x[:]).then_inc(stored, 16)
            sp.wait_ge(stored, 16)


def build_program(nc, dram, out, first=0, last=8):
    with ExitStack() as ctx:
        c = setup_core(nc, ctx, dram)
        w = {}
        for name, slot in (("l0x", 0), ("l0s", 1), ("l1x", 0), ("l2x", 0), ("l3x", 1), ("l3g", 0), ("l3f", 1)):
            rows = dram.get(f"r_{name}")
            w[name] = Weights(nc, ctx, c, name, slot, dram[f"w_{name}"], rows, (W_SCALE,) * 3 + (W_SCALE ** 2,))
        e0 = [Weights(nc, ctx, c, f"l0e{e}", e % 2, dram["w_l0e"][e]) for e in range(EXPERTS)]
        e2 = [Weights(nc, ctx, c, f"l2e{e}", 1 - e % 2, dram["w_l2e"][e]) for e in range(EXPERTS)]
        c.first_weights = {0: w["l0x"], 1: w["l0s"], 2: w["l1x"], 3: None, 4: w["l2x"], 5: e2[0], 6: w["l3x"], 7: w["l3f"]}[first]
        prepare(nc, c, None)
        for stage in range(first, last):
            if stage == 0:
                norm_stats(nc, c, "n0")
                attention(nc, c, Attention("a0", "cross16", w["l0x"], gate=0, add_mask=dram["mask_t"], biased=True), w["l0s"])
            if stage == 1:
                norm_stats(nc, c, "n1", second=2)
                a1 = Attention("a1", "self16", w["l0s"], affine=True, store="h+")
                a1.norm_g, a1.norm_b = dram["l0_g1"], dram["zeros"]
                attention(nc, c, a1, e0[0])
                norm_rows_of_h(nc, c, "m1n")
                r = make_routing(nc, ctx) if not hasattr(c, "r") else c.r
                c.r = r
                router_scores(nc, c, r, "m1s", 4608, 0, dram["l0_g2"], dram["zeros"])
                pick_two(nc, c, r, "m1p", 4)
                add_h(nc, c, "m1a", 4)
                for e in range(EXPERTS):
                    gated_ff(nc, c, GatedFf(f"m1e{e}", e0[e], 6, "h", "expert", combine=r.by_expert[:, e * TILES:(e + 1) * TILES],
                                            norm_g=dram["l0_g2"], norm_b=dram["zeros"], gate_first=False),
                             e0[e + 1] if e < 7 else w["l1x"])
            if stage == 2:
                norm_stats(nc, c, "n2")
                attention(nc, c, Attention("a2", "cross64", w["l1x"], gate=1, biased=True), None)
            if stage == 3:
                norm_stats(nc, c, "n3")
                quantized_linear(nc, c, "q3", 5, w["l2x"])
            if stage == 4:
                norm_stats(nc, c, "n4")
                attention(nc, c, Attention("a4", "cross16", w["l2x"], gate=2, clip_mask=dram["mask_rows"], biased=True), e2[0])
            if stage == 5:
                norm_stats(nc, c, "n5")
                normalise_into_h(nc, c, "m5n")
                r = make_routing(nc, ctx) if not hasattr(c, "r") else c.r
                c.r = r
                router_scores(nc, c, r, "m5s", 3072, 1, dram["ones"], dram["zeros"])
                find_thresholds(nc, c, r, "m5t")
                flag_ties(nc, c, r, "m5f")
                prefix_counts(nc, r, c, "m5c")
                take_top(nc, c, r, "m5p", 6)
                for e in range(EXPERTS):
                    gated_ff(nc, c, GatedFf(f"m5e{e}", e2[e], 4, "h", "expert", combine=r.by_expert[:, e * TILES:(e + 1) * TILES]),
                             e2[e + 1] if e < 7 else w["l3x"])
            if stage == 6:
                l3 = [dram["l3_" + k] for k in ("ln_g", "ln_b", "cln_g", "cln_b")]
                norm_context(nc, c, "c6", l3[2], l3[3])
                norm_stats(nc, c, "n6", second=0)
                a6 = Attention("a6", "cross64", w["l3x"], shared_kv=True, affine=True, store="h")
                a6.norm_g, a6.norm_b = l3[0], l3[1]
                attention(nc, c, a6, w["l3g"])
                gated_ff(nc, c, GatedFf("g6", w["l3g"], 8, "x", "pair", gate=3, norm_g=l3[0], norm_b=l3[1]), w["l3f"])
            if stage == 7:
                norm_stats(nc, c, "n7")
                scaled_linear(nc, c, "f7", 7, w["l3f"])
        store_result(nc, c, out)


def _by_chunk(w):
    k, n = w.shape
    return w.reshape(k // P, P, n).transpose(1, 0, 2).reshape(P, -1)


def _rotary_tables(length, dim):
    inv_freq = 1.0 / 10000.0 ** (np.arange(0, dim, 2, dtype=np.float32) / dim)
    freqs = np.einsum("i,j->ij", np.arange(length, dtype=np.float32), inv_freq)
    cos, sin = np.cos(freqs), np.sin(freqs)
    return np.concatenate([cos, cos], -1).astype(np.float32), np.concatenate([-sin, sin], -1).astype(np.float32)


def _layout(i):
    cat = lambda *w: np.ascontiguousarray(np.concatenate([_by_chunk(x) for x in w], axis=1))
    d = {k: i[k] for k in ("x", "ctx_1024", "g_xattn", "g_ffn")}
    d["w_l0x"] = cat(*(i["L0_xattn_W" + k].T for k in "qkvo"))
    d["r_l0x"] = np.concatenate([i["L0_xattn_b" + k] for k in "qkvo"]).reshape(1, -1)
    d["w_l0s"] = cat(*(i["L0_ffn_w" + k] for k in "qkvo"))
    columns = lambda v: np.ascontiguousarray(v.reshape(DC, P).T)
    d["l0_g1"], d["l0_g2"] = columns(i["L0_ffn_g1"]), columns(i["L0_ffn_g2"])
    for k in ("ln_g", "ln_b", "cln_g", "cln_b"):
        d["l3_" + k] = columns(i["L3_xattn_" + k])
    pad = lambda a, axis: np.concatenate([a, np.zeros([6 * P - a.shape[axis] if k == axis else n for k, n in enumerate(a.shape)],
                                                      a.dtype)], axis=axis)
    d["w_l0e"] = np.stack([cat(np.concatenate([pad(i["L0_ffn_wu"][e], 1), pad(i["L0_ffn_wg"][e], 1)], 1),
                               pad(i["L0_ffn_wd"][e], 0), i["L0_ffn_w_router"]) for e in range(EXPERTS)])
    d["w_l2e"] = np.stack([cat(np.concatenate([i["L2_ffn_W3"][e].T, i["L2_ffn_W1"][e].T], 1),
                               i["L2_ffn_W2"][e].T, i["L2_ffn_Wg"].T) for e in range(EXPERTS)])
    d["ones"] = np.ones((P, DC), np.float32)
    d["zeros"] = np.zeros((P, DC), np.float32)
    cos, sin = _rotary_tables(SEQ, DIM // HEADS)
    rows = lambda t: np.ascontiguousarray(t.reshape(2, P, -1).transpose(1, 0, 2))
    d["rope_cos"], d["rope_sin"] = rows(cos), rows(sin)
    d["w_l1x"] = cat(*(i["L1_xattn_W" + k] for k in "qkvo"))
    d["r_l1x"] = np.concatenate([np.zeros(3 * DIM, np.float32), i["L1_xattn_bo"]]).reshape(1, -1)
    d["l1f_w"] = np.ascontiguousarray(i["L1_ffn_weight_q"].T.reshape(DC, P, DIM).transpose(1, 0, 2)).view(np.int32)
    d["l1f_scale"], d["l1f_bias"] = i["L1_ffn_weight_scale"], i["L1_ffn_bias"]
    d["w_l2x"] = cat(*(i["L2_xattn_w" + k].T for k in "qkvo"))
    d["r_l2x"] = np.concatenate([i["L2_xattn_b" + k] for k in "qkvo"]).reshape(1, -1)
    k_w, v_w = i["L3_xattn_Wkv"][:, :64], i["L3_xattn_Wkv"][:, 64:]
    d["w_l3x"] = cat(i["L3_xattn_Wq"], np.concatenate([k_w, k_w], axis=1), v_w, i["L3_xattn_Wo"])
    d["w_l3g"] = cat(i["L3_xattn_Wff1"], i["L3_xattn_Wff2"])
    d["w_l3f"] = cat(i["L3_ffn_CB"].T)
    d["l3f_scale"], d["l3f_bias"] = i["L3_ffn_SCB"], i["L3_ffn_bias"]
    d["mask_rows"] = np.ascontiguousarray(i["mask_Bx1xSxS2_ik1"].reshape(BATCH, 2, P, KEYS).transpose(0, 2, 1, 3))
    d["mask_t"] = np.ascontiguousarray(i["mask_BxS2_ik1"].T)
    return d


def kernel(**inputs):
    import concourse.bacc as _bacc
    from concourse.bass_utils import run_bass_kernel_spmd as _run

    nc = _bacc.Bacc("TRN2", target_bir_lowering=False, num_devices=1)
    arrays = _layout({k: np.asarray(v) for k, v in inputs.items()})
    dram = {k: nc.dram_tensor(f"in_{k}", a.shape, mybir.dt.from_np(a.dtype), kind="ExternalInput").ap()
            for k, a in arrays.items()}
    out = nc.dram_tensor("out_x", (BATCH, SEQ, DIM), F32, kind="ExternalOutput").ap()
    build_program(nc, dram, out)
    r = _run(nc, [{f"in_{k}": a for k, a in arrays.items()}], core_ids=[0])
    return r.results[0]["out_x"]
```

```python
from contextlib import ExitStack, contextmanager

import numpy as np

import concourse.bass as bass
from concourse import mybir

F32 = mybir.dt.float32
F16 = mybir.dt.float16
I32 = mybir.dt.int32
U32 = mybir.dt.uint32
ALU = mybir.AluOpType
ACT = mybir.ActivationFunctionType
AX = mybir.AxisListType

P = 128
BATCH, SEQ, DIM = 16, 256, 256
KEYS = 77
TOKENS = BATCH * SEQ
TILES = TOKENS // P
DC = DIM // P
HEADS = 16
W_SCALE = 16.0
ARENAS = (8192, 4624)
STAGED = 512
EXPERTS = 8
PICKED = 2
CAPACITY = TOKENS // EXPERTS
FLAGS = TILES * EXPERTS
BISECTIONS = 32
STEP_ROWS = 2 * P
PICK_STEPS = TOKENS * PICKED // STEP_ROWS + EXPERTS
TOP_STEPS = TOKENS // STEP_ROWS
WEIGHT_UP = 2.0 ** 14
UP_BANKS = 4
CLIP = 100.0
NEG_BIG = -1.0e30
LN_EPS = 1e-5
RMS_EPS = 1e-6


class At:

    def __init__(self, i, off, n):
        self.i, self.off, self.n = i, off, n

    def __add__(self, k):
        return At(self.i, self.off + k, self.n)

    def valid(self):
        return self.i is not None or 0 <= self.off < self.n

    def count(self, per, plus):
        if self.i is None:
            return per * self.off + plus
        assert per * (2 + self.off) + plus > 0, (per, self.off, plus)
        return self.i * (2 * per) + (per * self.off + plus)


def wait(eng, sem, value):
    if isinstance(value, int) and value <= 0:
        return
    eng.wait_ge(sem, value)


@contextmanager
def stage_semaphores(nc, tag):
    sems = []

    def new(name):
        sems.append(nc.alloc_semaphore(f"{tag}_{name}"))
        return sems[-1]

    yield new
    nc.clear_and_free_semaphores(sems)
    nc.all_engine_barrier()


def over_steps(eng, nu, fns, n=BATCH):
    def body(b):
        for j in range(nu):
            for fn in fns:
                for db in (-1, 0, 1, 2):
                    if (b + db).valid():
                        fn(b + db, j - db * nu)

    for b in (-2, -1, 0, 1):
        body(At(None, b, n))
    with eng.Fori(1, n // 2 - 1) as i:
        body(At(i, 0, n))
        body(At(i, 1, n))
    for b in (n - 2, n - 1, n):
        body(At(None, b, n))


class Core:
    pass


def setup_core(nc, ctx, dram):
    c = Core()
    c.nc, c.dram = nc, dram

    def sb(name, shape, dt):
        return ctx.enter_context(nc.sbuf_tensor(name, shape, dt))

    c.x = sb("x_resident", [P, TILES, DIM], F32)
    c.h = sb("h_resident", [P, TILES, DIM], F32)
    c.ct = [sb(f"ctx_T_{p}", [P, DC, BATCH * KEYS], F16) for p in ("hi", "lo")]
    c.arena = [sb(f"weights_{i}", [P, 2, n], F16) for i, n in enumerate(ARENAS)]
    c.rows = [sb(f"bias_rows_{i}", [2, 4 * DIM], F16) for i in range(2)]
    c.ident = sb("ident", [P, P], F32)
    c.ident_h = sb("ident_h", [P, P], F16)
    c.ones_rows = sb("ones_rows", [2, P], F16)
    c.w_scale = sb("w_scale", [P, 1], F32)
    c.gates = sb("gates", [P, 8], F32)
    c.gates_w = sb("gates_w", [P, 8], F32)
    c.rstd1 = sb("rstd_first", [P, TILES], F32)
    c.tmp_a = sb("norm_tmp", [P, TILES], F32)
    c.w_stage = sb("w_stage", [P, 2, STAGED], F32)
    c.w_scaled = sb("w_scaled", [P, STAGED], F32)
    c.e_split = sb("expert_split", [P, 2, 2, STAGED], F16)
    c.row_raw = sb("row_raw", [1, 4 * DIM], F32)
    c.row_lo = sb("row_lo", [1, 4 * DIM], F16)
    c.stats = sb("stats", [P, TILES, 6], F32)
    c.mv = sb("mean_var", [P, TILES, 2], F32)
    c.rstd = sb("rstd", [P, TILES], F32)
    c.consts = sb("consts", [P, 8], F32)
    c.bank = [ctx.enter_context(nc.psum_tensor(f"bank{i}", [P, 512], F32)) for i in range(8)]
    return c


def prepare(nc, c):
    with ExitStack() as ctx:
        cx = ctx.enter_context(nc.sbuf_tensor("ctx_rows", [KEYS, BATCH, DIM], F32))
        graw = ctx.enter_context(nc.sbuf_tensor("gates_raw", [P, 8], F32))
        sem = ctx.enter_context(stage_semaphores(nc, "prepare"))
        loaded_x, loaded_ctx, loaded_g = [sem(f"loaded_x{k}") for k in range(X_LOADS)], sem("loaded_ctx"), sem("loaded_g")
        stat_done = sem("stat_done")
        const, selected = sem("const"), sem("selected")
        full, hi_done, free = sem("full"), sem("hi_done"), sem("free")
        block = ctx.enter_context(nc.Block())
        groups = DC * BATCH // 4

        @block.sync
        def _(sp):
            sp.dma_start(cx[:], c.dram["ctx_1024"].rearrange("b k d -> k b d")).then_inc(loaded_ctx, 16)
            sp.dma_start(graw[:, 0:4], c.dram["g_xattn"].partition_broadcast(P)).then_inc(loaded_g, 16)
            sp.dma_start(graw[:, 4:8], c.dram["g_ffn"].partition_broadcast(P)).then_inc(loaded_g, 16)
            load_x(sp, c, c.dram["x"].rearrange("b (t p) d -> p (b t) d", p=P), loaded_x)

        @block.gpsimd
        def _(pool):
            nc.gpsimd.memset(c.ident[:], 0.0).then_inc(const, 1)
            nc.gpsimd.memset(c.ident_h[:], 0.0).then_inc(const, 1)
            pool.wait_ge(const, 2)
            for m in (c.ident, c.ident_h):
                nc.gpsimd.affine_select(out=m[:], in_=m[:], compare_op=ALU.not_equal, fill=1.0, base=0,
                                        pattern=[[-1, P]], channel_multiplier=1).then_inc(selected, 1)
            nc.gpsimd.memset(c.ones_rows[:], 1.0).then_inc(const, 1)
            nc.gpsimd.memset(c.w_scale[:], W_SCALE).then_inc(const, 1)
            for i, v in enumerate((LN_EPS, -0.5, RMS_EPS, 1.0)):
                nc.gpsimd.memset(c.consts[:, i:i + 1], v).then_inc(const, 1)
            pool.wait_ge(const, 8)
            prep_weights(nc, c, pool, c.first_weights)

        @block.tensor
        def _(pe):
            pe.wait_ge(selected, 2)
            pe.wait_ge(loaded_ctx, 16)
            for g in range(groups):
                d, b0 = g % DC, g // DC * 4
                wait(pe, free, g - 1)
                for j in range(4):
                    last = nc.tensor.transpose(c.bank[g % 2][:, j * KEYS:(j + 1) * KEYS],
                                               cx[:, b0 + j, d * P:(d + 1) * P], c.ident[0:KEYS, 0:KEYS])
                last.then_inc(full, 1)

        @block.scalar
        def _(act):
            for g in range(groups):
                d, b0 = g % DC, g // DC * 4
                act.wait_ge(full, g + 1)
                nc.scalar.copy(c.ct[0][:, d, b0 * KEYS:(b0 + 4) * KEYS],
                               c.bank[g % 2][:, 0:4 * KEYS]).then_inc(hi_done, 1)
            act.wait_ge(loaded_g, 32)
            nc.scalar.activation(c.gates[:], graw[:], ACT.Tanh).then_inc(hi_done, 1)
            act.wait_ge(hi_done, groups + 1)
            nc.scalar.mul(c.gates_w[:], c.gates[:], 1.0 / W_SCALE ** 2)

        @block.vector
        def _(dve):
            for g in range(groups):
                d, b0 = g % DC, g // DC * 4
                dve.wait_ge(hi_done, g + 1)
                cols = slice(b0 * KEYS, (b0 + 4) * KEYS)
                nc.vector.tensor_tensor(c.ct[1][:, d, cols], c.bank[g % 2][:, 0:4 * KEYS],
                                        c.ct[0][:, d, cols], ALU.subtract).then_inc(free, 1)
            stats_of_loads(nc, c, dve, loaded_x, stat_done)


class Weights:

    def __init__(self, nc, ctx, c, tag, slot, w_dram, rows_dram=None, rows_scale=()):
        self.cols = w_dram.shape[1]
        self.tag, self.slot, self.w, self.rows, self.rows_scale = tag, slot, w_dram, rows_dram, rows_scale
        self.landed = [ctx.enter_context(nc.semaphore(f"{tag}_w_landed{i}")) for i in range(2)]
        self.step = ctx.enter_context(nc.semaphore(f"{tag}_w_step"))
        self.row_step = ctx.enter_context(nc.semaphore(f"{tag}_row_step"))
        self.row_dma = ctx.enter_context(nc.semaphore(f"{tag}_row_dma"))


def prep_weights(nc, c, pool, w, part=0, parts=1):
    if w is None:
        return
    stage, scaled = c.w_stage, c.w_scaled
    chunks = [(o, min(STAGED, w.cols - o)) for o in range(0, w.cols, STAGED)]
    start, end = (len(chunks) * p // parts for p in (part, part + 1))
    for k in range(start, end):
        o, n = chunks[k]
        wait(pool, w.step, 3 * (k - 1))
        pool.dma_start(stage[:, k % 2, 0:n], w.w[:, o:o + n]).then_inc(w.landed[k % 2], 16)
        if k > start:
            split_chunk(nc, c, pool, w, k - 1, chunks)
    if end > start:
        split_chunk(nc, c, pool, w, end - 1, chunks)
    if w.rows is not None and part == parts - 1:
        n = w.rows.shape[1]
        raw, lo = c.row_raw, c.row_lo
        pool.dma_start(raw[0:1, 0:n], w.rows).then_inc(w.row_dma, 16)
        pool.wait_ge(w.row_dma, 16)
        for j, s in enumerate(w.rows_scale):
            nc.gpsimd.tensor_scalar(raw[0:1, j * DIM:(j + 1) * DIM], raw[0:1, j * DIM:(j + 1) * DIM],
                                    s, 1.0, ALU.mult, ALU.mult).then_inc(w.row_step, 1)
        m = len(w.rows_scale)
        pool.wait_ge(w.row_step, m)
        nc.gpsimd.tensor_copy(c.rows[w.slot][0:1, 0:n], raw[0:1, 0:n]).then_inc(w.row_step, 1)
        pool.wait_ge(w.row_step, m + 1)
        nc.gpsimd.tensor_tensor(lo[0:1, 0:n], raw[0:1, 0:n], c.rows[w.slot][0:1, 0:n],
                                ALU.subtract).then_inc(w.row_step, 1)
        pool.wait_ge(w.row_step, m + 2)
        pool.dma_start(c.rows[w.slot][1:2, 0:n], lo[0:1, 0:n]).then_inc(w.row_dma, 16)
        pool.wait_ge(w.row_dma, 32)


def split_chunk(nc, c, pool, w, k, chunks):
    o, n = chunks[k]
    src, scaled = c.w_stage[:, k % 2, 0:n], c.w_scaled[:, 0:n]
    hi, lo = (c.arena[w.slot][:, i, o:o + n] for i in range(2))
    factor = c.w_scale[:, 0:1].broadcast_to([P, n])
    pool.wait_ge(w.landed[k % 2], 16 * (k // 2 + 1))
    nc.gpsimd.tensor_tensor(hi, src, factor, ALU.mult).then_inc(w.step, 1)
    nc.gpsimd.tensor_tensor(scaled, src, factor, ALU.mult).then_inc(w.step, 1)
    pool.wait_ge(w.step, 3 * k + 2)
    nc.gpsimd.tensor_tensor(lo, scaled, hi, ALU.subtract).then_inc(w.step, 1)
    pool.wait_ge(w.step, 3 * k + 3)


class ExpertWeights:

    def __init__(self, nc, ctx, tag, w_dram, hidden):
        self.tag, self.w, self.cols, self.hidden = tag, w_dram, w_dram.shape[1] // EXPERTS, hidden
        self.split = nc.dram_tensor(f"{tag}_split", (P, 2, w_dram.shape[1]), F16, kind="Internal").ap()
        self.chunks = w_dram.shape[1] // STAGED
        sem = lambda n: ctx.enter_context(nc.semaphore(f"{tag}_{n}"))
        self.landed = [sem("ew_landed0"), sem("ew_landed1")]
        self.stored = [sem("ew_stored0"), sem("ew_stored1")]
        self.step = sem("ew_step")


def load_and_store_split(sp, c, e, after):
    if after is not None:
        sp.wait_ge(after.step, 3 * -(-after.cols // STAGED))
    def load(k, par):
        sp.dma_start(c.w_stage[:, par, :], e.w[:, bass.ds(k * STAGED, STAGED)]).then_inc(e.landed[par], 16)

    def store(k, par):
        wait(sp, e.step, k * 3 + 3)
        sp.dma_start(e.split[:, :, bass.ds(k * STAGED, STAGED)], c.e_split[:, par]).then_inc(e.stored[par], 16)

    load(0, 0)
    load(1, 1)
    with sp.Fori(0, e.chunks // 2 - 1) as i:
        for par in range(2):
            store(i * 2 + par, par)
            load(i * 2 + (par + 2), par)
    for par in range(2):
        store(e.chunks - 2 + par, par)
    for par in range(2):
        sp.wait_ge(e.stored[par], 16 * (e.chunks // 2))


def split_experts(nc, c, pool, e):
    factor = c.w_scale[:, 0:1].broadcast_to([P, STAGED])

    def chunk(k, par, pair, first):
        src, scaled, hi, lo = c.w_stage[:, par, :], c.w_scaled[:], c.e_split[:, par, 0, :], c.e_split[:, par, 1, :]
        pool.wait_ge(e.landed[par], pair * 16 + 16)
        if not first:
            pool.wait_ge(e.stored[par], pair * 16)
        nc.gpsimd.tensor_tensor(hi, src, factor, ALU.mult).then_inc(e.step, 1)
        nc.gpsimd.tensor_tensor(scaled, src, factor, ALU.mult).then_inc(e.step, 1)
        pool.wait_ge(e.step, k * 3 + 2)
        nc.gpsimd.tensor_tensor(lo, scaled, hi, ALU.subtract).then_inc(e.step, 1)
        pool.wait_ge(e.step, k * 3 + 3)

    for par in range(2):
        chunk(par, par, 0, True)
    with pool.Fori(1, e.chunks // 2) as i:
        for par in range(2):
            chunk(i * 2 + par, par, i, False)


X_LOADS = 4


def load_x(sp, c, rows, landed):
    for k, part in enumerate(landed):
        at = slice(k * TILES // X_LOADS, (k + 1) * TILES // X_LOADS)
        sp.dma_start(c.x[:, at, :], rows[:, at, :]).then_inc(part, 16)


def stats_of_loads(nc, c, dve, landed, stat_done):
    for t in range(TILES):
        if t % (TILES // X_LOADS) == 0:
            dve.wait_ge(landed[t * X_LOADS // TILES], 16)
        nc.vector.bn_stats(c.stats[:, t, :], c.x[:, t, :]).then_inc(stat_done, 1)


def norm_stats(nc, c, tag, second=None, have_stats=False):
    with ExitStack() as ctx:
        sem = ctx.enter_context(stage_semaphores(nc, tag))
        stat_done, var_done, pow_done = sem("stat_done"), sem("var_done"), sem("pow_done")
        block = ctx.enter_context(nc.Block())

        @block.vector
        def _(dve):
            for t in range(TILES if not have_stats else 0):
                nc.vector.bn_stats(c.stats[:, t, :], c.x[:, t, :]).then_inc(stat_done, 1)
            for t in range(TILES):
                if not have_stats:
                    dve.wait_ge(stat_done, t + 1)
                nc.vector.bn_aggr(c.mv[:, t, :], c.stats[:, t, :]).then_inc(var_done, 1)

        @block.gpsimd
        def _(pool):
            def col(i):
                return c.consts[:, i:i + 1].broadcast_to([P, TILES])
            pool.wait_ge(var_done, TILES)
            var = c.mv[:, :, 1]
            out = c.rstd1 if second is not None else c.rstd
            nc.gpsimd.tensor_tensor(c.tmp_a[:], var, col(0), ALU.add).then_inc(pow_done, 1)
            pool.wait_ge(pow_done, 1)
            nc.gpsimd.tensor_tensor(out[:], c.tmp_a[:], col(1), ALU.pow).then_inc(pow_done, 1)
            if second is not None:
                pool.wait_ge(pow_done, 2)
                nc.gpsimd.tensor_tensor(c.tmp_a[:], out[:], out[:], ALU.mult).then_inc(pow_done, 1)
                pool.wait_ge(pow_done, 3)
                nc.gpsimd.tensor_tensor(c.tmp_a[:], c.tmp_a[:], var, ALU.mult).then_inc(pow_done, 1)
                pool.wait_ge(pow_done, 4)
                nc.gpsimd.tensor_tensor(c.tmp_a[:], c.tmp_a[:], col(second), ALU.add).then_inc(pow_done, 1)
                pool.wait_ge(pow_done, 5)
                nc.gpsimd.tensor_tensor(c.tmp_a[:], c.tmp_a[:], col(1), ALU.pow).then_inc(pow_done, 1)
                pool.wait_ge(pow_done, 6)
                nc.gpsimd.tensor_tensor(c.rstd[:], c.tmp_a[:], out[:], ALU.mult).then_inc(pow_done, 1)


def three_products(nc, out, stationary, moving, first=True, last=True):
    (ah, al), (bh, bl) = stationary, moving
    nc.tensor.matmul(out, ah, bh, start=first, stop=False)
    nc.tensor.matmul(out, ah, bl, start=False, stop=False)
    return nc.tensor.matmul(out, al, bh, start=False, stop=last)


class Attention:

    def __init__(self, tag, kind, weights, gate=None, shared_kv=False, add_mask=None, clip_mask=None,
                 affine=False, biased=False, store="x"):
        self.tag, self.kind, self.weights = tag, kind, weights
        self.gate, self.shared_kv, self.add_mask, self.clip_mask = gate, shared_kv, add_mask, clip_mask
        self.affine, self.biased, self.store = affine, biased, store
        self.dh = 64 if kind == "cross64" else 16
        self.causal = kind == "self16"
        self.kw = P if self.causal else KEYS
        self.key_tiles = SEQ // P if self.causal else 1
        self.scale = self.dh ** -0.5 / (W_SCALE * W_SCALE)
        if self.causal:
            self.units = [(0, h, 4, [0]) for h in (0, 1, 8, 9)]
            self.units += [(1, h, 2, [0, 1]) for h in (0, 1, 4, 5, 8, 9, 12, 13)]
            self.fronts = [("xT", -12), ("q", -11), ("k", -10), ("v", -9),
                           ("qT0", -6), ("qT1", -5), ("kT0", -4), ("kT1", -3)]
        else:
            self.units = [(t, h, 4, [0]) for t in range(2) for h in (0, 1, 8, 9)]
            if self.dh == 16:
                self.fronts = [("xT", -8), ("q", -6.5), ("kv", -5), ("qT0", -4), ("qT1", -3), ("kT", -2)]
            elif self.shared_kv:
                self.fronts = [("xT", -7), ("q0", -6), ("q1", -5), ("q2", -4), ("q3", -3), ("kv", -2)]
            else:
                self.fronts = [("xT", -8), ("q0", -7), ("q1", -6), ("q2", -5), ("q3", -4), ("k0", -3),
                               ("k1", -2.5), ("v0", -2), ("v1", -1)]
        self.q_and_k = len(self.fronts) - (2 if self.dh == 64 and not self.shared_kv else 0)
        self.nu = len(self.units)
        self.nf = len(self.fronts)
        self.o_chunks = HEADS * self.dh // P
        parts = max(1, self.o_chunks // 4)
        self.outs = []
        for t in range(2):
            last = max(i for i, u in enumerate(self.units) if u[0] == t)
            self.outs += [("turn", t, k, last + 4 + k) for k in range(parts)]
            self.outs += [("project", t, 0, last + 4 + parts)]
        self.no = len(self.outs)


def attention(nc, c, a, next_weights, experts=None):
    dh, kw, nu, nf, no, units = a.dh, a.kw, a.nu, a.nf, a.no, a.units
    nkt = a.key_tiles
    wide = a.kind == "cross64"
    v_heads = 1 if a.shared_kv else HEADS
    with ExitStack() as ctx:
        def sb(name, shape, dt):
            return ctx.enter_context(nc.sbuf_tensor(f"{a.tag}_{name}", shape, dt))

        sem = ctx.enter_context(stage_semaphores(nc, a.tag))

        xn = sb("xn", [P, 2, DIM], F32)
        xt = [sb(f"xT_{p}", [P, DC, SEQ], F16) for p in ("hi", "lo")]
        q_parts = ("hi", "lo") if wide else ("stack",)
        k_chunks = 1 if a.shared_kv else HEADS // 2
        qt = [[sb(f"qT_{p}{i}", [P, HEADS // 2, SEQ], F16) for p in q_parts] for i in range(2)]
        kt = [[sb(f"kT_{p}{i}", [P, k_chunks, kw * nkt], F16) for p in q_parts] for i in range(2)]
        v = [[sb(f"v_{p}{i}", [P, nkt, v_heads, dh + 1], F16) for p in ("hi", "lo")] for i in range(2)]
        e = [sb(f"exp{i}", [P, 512], F32) for i in range(2)]
        pt = [[sb(f"pT_{p}{i}", [P, 512], F16) for p in ("hi", "lo")] for i in range(2)]
        top = sb("top", [P, 2, 4], F32)
        shift = sb("shift", [P, 2, 4], F32)
        rden = sb("rden", [P, 2, 4], F32)
        o = [sb(f"o{i}", [P, HEADS * dh], F32) for i in range(2)]
        ot = [sb(f"oT_{p}", [P, a.o_chunks, P], F16) for p in ("hi", "lo")]
        if a.affine:
            norm_g = sb("norm_g", [P, DC], F32)
            norm_b = sb("norm_b", [P, DC], F32)
            xf = sb("xT_f32", [P, DC, SEQ], F32)
        if not wide:
            qs = sb("q_stack", [P, 2, HEADS, 4, 16], F16)
            ks = sb("k_stack", [P, nkt, HEADS, 4, 16], F16)
        if a.add_mask is not None:
            mask_i = sb("mask_i", [KEYS, BATCH], I32)
            mask_f = sb("mask_f", [KEYS, BATCH], F32)
            mask_h = sb("mask_h", [KEYS, BATCH], F16)
        if a.clip_mask is not None:
            cm_i = sb("clip_mask_i", [P, 2, 2, KEYS], I32)
            cm_t = sb("clip_mask_t", [P, 2, 2, KEYS], F32)
            cm_u = sb("clip_mask_u", [P, 2, 2, KEYS], F32)
            clipped = sb("clipped", [P, 2, 4 * KEYS], F32)
        if a.causal:
            cos_t = sb("cos", [P, 2, 16], F32)
            sin_t = sb("sin", [P, 2, 16], F32)
            raw = [sb(f"raw{i}", [P, 2, HEADS, 16], F32) for i in range(2)]
            rot = [sb(f"rot{i}", [P, 2, HEADS, 16], F32) for i in range(2)]
            half = sb("rot_half", [P, 2, HEADS, 16], F32)
            future = sb("future", [P, P], F16)
            big_id = sb("big_id", [P, P], F16)

        loaded, const_ready, setup_step = sem("loaded"), sem("const_ready"), sem("setup_step")
        xn_ready = sem("xn_ready")
        f_full, f_hi, f_free = sem("f_full"), sem("f_hi"), sem("f_free")
        s_full = sem("scores_full")
        clip_done = sem("clip_done")
        top_done, shift_done, exp_done = sem("top_done"), sem("shift_done"), sem("exp_done")
        t_full, p_hi, p_lo = sem("pT_full"), sem("hi"), sem("lo")
        pv_full, rden_done, norm_done = sem("pv_full"), sem("rden_done"), sem("norm_done")
        o_full, o_hi, o_free = sem("o_full"), sem("o_hi"), sem("o_free")
        rot_step, stack_hi, stack_lo = sem("rot_step"), sem("stack_hi"), sem("stack_lo")
        cm_landed, cm_step, cm_ready = [sem("cm_landed0"), sem("cm_landed1")], sem("cm_step"), sem("cm_ready")
        block = ctx.enter_context(nc.Block())

        w_hi, w_lo = (c.arena[a.weights.slot][:, i, :] for i in range(2))
        rows = c.rows[a.weights.slot]

        def weight(off, n):
            return w_hi[:, off:off + n], w_lo[:, off:off + n]

        if wide and a.shared_kv:
            k_off, v_off, o_off, kn, vn = 2048, 2048 + 256, 2048 + 256 + 128, P, 64
        elif wide:
            k_off, v_off, o_off, kn, vn = 2048, 4096, 6144, 1024, 1024
        else:
            k_off, v_off, o_off, kn, vn = 512, 1024, 1536, 256, 256
        qn = 1024 if wide else 256
        f_bank, o_bank = c.bank[6], c.bank[7]
        f_bank_h = f_bank[:].bitcast(F16)
        both = [n for n, _ in a.fronts if n in ("xT", "q", "kv", "v", "q0", "q1", "q2", "q3", "k0", "k1", "v0", "v1")]
        if a.causal:
            both = ["xT", "v"]
        turns = [x for x in a.outs if x[0] == "turn"]

        def blocks(u):
            t, h0, nh, kts = units[u]
            return [(i * len(kts) + j, h0 + 2 * i, k) for i in range(nh) for j, k in enumerate(kts)]

        def turned_w(m):
            return (m + 7) // 8 * 8

        def head_rows(x, h, cols, shared=False):
            return x[64 * (h % 2):64 * (h % 2) + 64, 0 if shared else h // 2, cols]

        a.consts = 0
        a.tables = 2 if a.causal else 0
        a.loads = a.tables + (1 if a.add_mask is not None else 0) + (2 if a.affine else 0)

        @block.gpsimd
        def _(pool):
            def const(ins):
                ins.then_inc(const_ready, 1)
                a.consts += 1
                pool.wait_ge(const_ready, a.consts)

            if a.causal:
                const(nc.gpsimd.memset(future[:], 0.0))
                const(nc.gpsimd.affine_select(out=future[:], in_=future[:], compare_op=ALU.is_ge, fill=-60000.0,
                                              base=0, pattern=[[-1, P]], channel_multiplier=1))
                const(nc.gpsimd.memset(big_id[:], 0.0))
                const(nc.gpsimd.affine_select(out=big_id[:], in_=big_id[:], compare_op=ALU.not_equal, fill=1024.0,
                                              base=0, pattern=[[-1, P]], channel_multiplier=1))
            if not wide:
                const(nc.gpsimd.memset(qs[:, :, :, 3, :], 0.0))
                const(nc.gpsimd.memset(ks[:, :, :, 3, :], 0.0))
                if a.add_mask is not None:
                    const(nc.gpsimd.memset(qs[:, :, :, 3, 0:1], W_SCALE * W_SCALE))
            for i in range(2):
                const(nc.gpsimd.memset(v[i][0][:, :, :, dh:dh + 1], 1.0))
                const(nc.gpsimd.memset(v[i][1][:, :, :, dh:dh + 1], 0.0))
            if a.add_mask is not None:
                pool.wait_ge(loaded, 16 * a.loads)
                factor = -CLIP / (a.scale * W_SCALE * W_SCALE)
                const(nc.gpsimd.tensor_scalar(mask_f[:], mask_i[:], factor, 1.0, ALU.mult, ALU.mult))
                const(nc.gpsimd.tensor_scalar(mask_h[:], mask_f[:], 1.0, 0.0, ALU.mult, ALU.add))

            def rotate(b, s):
                for i, at in enumerate((-11, -10)):
                    if at != s:
                        continue
                    n = lambda k: b.count(8, 4 * i + k)
                    pool.wait_ge(f_free, b.count(nf, i + 2))
                    wait(pool, stack_hi, b.count(2, i - 1))
                    table = lambda x, r: x[:, :, r].unsqueeze(2).broadcast_to([P, 2, HEADS, 16 if r == slice(0, 16) else 8])
                    nc.gpsimd.tensor_tensor(rot[i][:], raw[i][:], table(cos_t, slice(0, 16)), ALU.mult).then_inc(rot_step, 1)
                    nc.gpsimd.tensor_tensor(half[:, :, :, 0:8], raw[i][:, :, :, 8:16], table(sin_t, slice(0, 8)),
                                            ALU.mult).then_inc(rot_step, 1)
                    nc.gpsimd.tensor_tensor(half[:, :, :, 8:16], raw[i][:, :, :, 0:8], table(sin_t, slice(8, 16)),
                                            ALU.mult).then_inc(rot_step, 1)
                    pool.wait_ge(rot_step, n(3))
                    nc.gpsimd.tensor_tensor(rot[i][:], rot[i][:], half[:], ALU.add).then_inc(rot_step, 1)
                    pool.wait_ge(rot_step, n(4))
                for i, at in enumerate((-8, -6)):
                    if at == s:
                        st, blk = ((qs, 1), (ks, 2))[i]
                        pool.wait_ge(stack_hi, b.count(2, i + 1))
                        nc.gpsimd.tensor_tensor(st[:, :, :, blk, :], rot[i][:], st[:, :, :, 0, :],
                                                ALU.subtract).then_inc(stack_lo, 1)

            if a.causal:
                pool.wait_ge(loaded, 16 * a.loads)
                over_steps(pool, nu, (rotate,))
            prep_weights(nc, c, pool, next_weights)
            if experts is not None:
                split_experts(nc, c, pool, experts)

        @block.sync
        def _(sp):
            n = 0
            def load(dst, src):
                nonlocal n
                n += 1
                sp.dma_start(dst, src).then_inc(loaded, 16)
            if a.add_mask is not None:
                load(mask_i[:], a.add_mask)
            if a.causal:
                load(cos_t[:], c.dram["rope_cos"])
                load(sin_t[:], c.dram["rope_sin"])
            if a.affine:
                load(norm_g[:], a.norm_g)
                load(norm_b[:], a.norm_b)
            if n:
                sp.wait_ge(loaded, 16 * n)
            if experts is not None:
                load_and_store_split(sp, c, experts, next_weights)
            if a.clip_mask is not None:
                def masks(b, s):
                    if s != -nu - 1:
                        return
                    row = b.off if b.i is None else b.count(1, 0)
                    wait(sp, cm_step, b.count(1, -1))
                    sp.dma_start(cm_i[:, b.off % 2], a.clip_mask[row]).then_inc(cm_landed[b.off % 2], 16)
                over_steps(sp, nu, (masks,))

        @block.tensor
        def _(pe):
            if a.causal:
                pe.wait_ge(const_ready, 4)

            def scores(b, s):
                u = s + 1
                if not 0 <= u < nu:
                    return
                t, h0, nh, kts = units[u]
                wait(pe, clip_done if a.clip_mask is not None else exp_done, b.count(nu, u - 1))
                if u == 0:
                    wait(pe, f_free, b.count(nf, a.q_and_k))
                for blk, h, k in blocks(u):
                    out = c.bank[u % 2][:, blk * kw:(blk + 1) * kw]
                    q_cols, k_cols = slice(t * P, (t + 1) * P), slice(k * kw, (k + 1) * kw)
                    qp = [head_rows(x, h, q_cols) for x in qt[b.off % 2]]
                    kp = [head_rows(x, h, k_cols, a.shared_kv) for x in kt[b.off % 2]]
                    if wide:
                        last = three_products(nc, out, qp, kp)
                    else:
                        diagonal = a.causal and k == t
                        last = nc.tensor.matmul(out, qp[0], kp[0], start=True, stop=not diagonal)
                        if diagonal:
                            last = nc.tensor.matmul(out, big_id[:], future[:], start=False, stop=True)
                last.then_inc(s_full, 1)

            def turn_probs(b, s):
                u = s - 1
                if not 0 <= u < nu:
                    return
                wait(pe, exp_done, b.count(nu, u + 1))
                wait(pe, p_lo, b.count(nu, u - 1))
                for blk in range(4):
                    last = nc.tensor.transpose(c.bank[2 + u % 2][0:kw, blk * P:(blk + 1) * P],
                                               e[u % 2][:, blk * kw:(blk + 1) * kw], c.ident[:])
                last.then_inc(t_full, 1)

            def times_v(b, s):
                u = s - 2
                if not 0 <= u < nu:
                    return
                t, h0, nh, kts = units[u]
                wait(pe, p_lo, b.count(nu, u + 1))
                if u == 0:
                    wait(pe, f_free, b.count(nf, nf))
                wait(pe, norm_done, b.count(nu, u - 1))
                ph, pl = pt[u % 2]
                for blk, h, k in blocks(u):
                    i = (h - h0) // 2
                    vh, vl = (x[0:kw, k, 0 if a.shared_kv else h, :] for x in v[b.off % 2])
                    pp = (ph[0:kw, blk * P:(blk + 1) * P], pl[0:kw, blk * P:(blk + 1) * P])
                    last = three_products(nc, c.bank[4 + u % 2][:, i * (dh + 1):(i + 1) * (dh + 1)], pp, (vh, vl),
                                          first=k == kts[0], last=k == kts[-1])
                last.then_inc(pv_full, 1)

            def output(b, s):
                for n, (what, t, k, at) in enumerate(a.outs):
                    if at != s:
                        continue
                    wait(pe, o_free, b.count(no, n))
                    if what == "turn":
                        last_unit = max(i for i, u in enumerate(units) if u[0] == t)
                        wait(pe, norm_done, b.count(nu, last_unit + 1))
                        m = min(4, a.o_chunks)
                        for j in range(m):
                            ch = 4 * k + j
                            last = nc.tensor.transpose(o_bank[:, j * P:(j + 1) * P],
                                                       o[t][:, ch * P:(ch + 1) * P], c.ident[:])
                    else:
                        for ch in range(a.o_chunks):
                            last = three_products(nc, o_bank[:, 0:DIM], [x[:, ch, :] for x in ot],
                                                  weight(o_off + ch * DIM, DIM), first=ch == 0,
                                                  last=ch == a.o_chunks - 1 and not a.biased)
                        if a.biased:
                            last = nc.tensor.matmul(o_bank[:, 0:DIM], c.ones_rows[:], rows[:, 3 * DIM:4 * DIM],
                                                    start=False, stop=True)
                    last.then_inc(o_full, 1)

            def project_rows(out, lhs, off, n, width, bias=None, m=P):
                for d in range(DC):
                    last = three_products(nc, out, [x[d] for x in lhs], weight(off + d * width, n),
                                          first=d == 0, last=d == DC - 1 and bias is None)
                if bias is not None:
                    last = nc.tensor.matmul(out, c.ones_rows[:, 0:m], rows[:, bias * DIM:(bias + 1) * DIM],
                                            start=False, stop=True)
                return last

            def front(b, s, half=0):
                for n, (what, at) in enumerate(a.fronts):
                    if at != s - half:
                        continue
                    wait(pe, f_free, b.count(nf, n))
                    x_tile = [[[x[:, d, t * P:(t + 1) * P] for d in range(DC)] for x in xt] for t in range(2)]
                    keys = lambda: [[x[:, d, bass.ds(b.count(KEYS, 0), KEYS)] for d in range(DC)] for x in c.ct]
                    if what == "xT":
                        wait(pe, xn_ready, b.count(1, 1))
                        for d in range(DC):
                            for t in range(2):
                                col = (d * 2 + t) * P
                                last = nc.tensor.transpose(f_bank[:, col:col + P], xn[:, t, d * P:(d + 1) * P],
                                                           c.ident[:])
                    elif what == "q" or (a.causal and what in "kv"):
                        i = "qkv".index(what)
                        for t in range(2):
                            last = project_rows(f_bank[:, t * 256:t * 256 + 256], x_tile[t], i * 512, 256, 256,
                                                bias=i if a.biased else None)
                    elif what == "kv" and not wide:
                        kk = keys()
                        for i in (1, 2):
                            last = project_rows(f_bank[0:KEYS, (i - 1) * 256:i * 256], kk, i * 512, 256, 256,
                                                bias=i if a.biased else None, m=KEYS)
                    elif what == "kv":
                        kk = keys()
                        for d in range(DC):
                            last = three_products(nc, f_bank[:, 0:KEYS], weight(k_off + d * kn, P),
                                                  [x[d] for x in kk], first=d == 0, last=d == DC - 1)
                        last = project_rows(f_bank[0:KEYS, 128:128 + 64], kk, v_off, 64, 64)
                    elif what[:2] in ("qT", "kT"):
                        cross_k = what == "kT"
                        if a.causal:
                            wait(pe, stack_lo, b.count(2, 1 if what[0] == "q" else 2))
                        t = 0 if cross_k else int(what[2])
                        st, m = (ks, kw) if what[0] == "k" else (qs, P)
                        for ch in range(HEADS // 2):
                            last = nc.tensor.transpose(
                                f_bank_h[:, ch * turned_w(m):ch * turned_w(m) + m],
                                st[0:m, t, 2 * ch:2 * ch + 2, :, :].rearrange("p h f d -> p (h f d)"),
                                c.ident_h[0:m, 0:m])
                    elif what[0] == "q":
                        for j in range(2):
                            ch = 2 * int(what[1]) + j
                            for d in range(DC):
                                last = three_products(nc, f_bank[:, j * SEQ:(j + 1) * SEQ],
                                                      weight(d * qn + ch * P, P), [x[:, d, :] for x in xt],
                                                      first=d == 0, last=d == DC - 1)
                    elif what[0] == "k":
                        kk = keys()
                        for j in range(4):
                            ch = 4 * int(what[1]) + j
                            for d in range(DC):
                                last = three_products(nc, f_bank[:, j * KEYS:(j + 1) * KEYS],
                                                      weight(k_off + d * kn + ch * P, P), [x[d] for x in kk],
                                                      first=d == 0, last=d == DC - 1)
                    else:
                        last = project_rows(f_bank[0:KEYS, :], keys(), v_off + 512 * int(what[1]), 512, vn)
                    last.then_inc(f_full, 1)

            def early_front(b, s):
                front(b, s, 0.5)

            over_steps(pe, nu, (scores, early_front, turn_probs, front, times_v, output))

        @block.scalar
        def _(act):
            if a.affine:
                act.wait_ge(loaded, 16 * a.loads)

            def probs_hi(b, s):
                u = s - 1
                if not 0 <= u < nu:
                    return
                wait(act, t_full, b.count(nu, u + 1))
                wait(act, pv_full, b.count(nu, u - 1))
                nc.scalar.copy(pt[u % 2][0][0:kw, :], c.bank[2 + u % 2][0:kw, :]).then_inc(p_hi, 1)

            def exps(b, s):
                if not 0 <= s < nu:
                    return
                t, h0, nh, kts = units[s]
                wait(act, shift_done, b.count(nu, s + 1))
                wait(act, t_full, b.count(nu, s - 1))
                w = kw * len(kts)
                src = clipped[:, s % 2, :] if a.clip_mask is not None else c.bank[s % 2]
                for i in range(nh):
                    last = nc.scalar.activation(e[s % 2][:, i * w:(i + 1) * w], src[:, i * w:(i + 1) * w], ACT.Exp,
                                                bias=shift[:, s % 2, i:i + 1], scale=a.scale)
                last.then_inc(exp_done, 1)

            def output(b, s):
                for n, (what, t, k, at) in enumerate(a.outs):
                    if at == s and what == "turn":
                        act.wait_ge(o_full, b.count(no, n + 1))
                        m = min(4, a.o_chunks)
                        nc.scalar.copy(ot[0][:, 4 * k:4 * k + m, :].rearrange("p c n -> p (c n)"),
                                       o_bank[:, 0:m * P]).then_inc(o_hi, 1)

            def front(b, s, half=0):
                par = b.off % 2
                for n, (what, at) in enumerate(a.fronts):
                    if at != s - half or what in ("qT1", "kT1"):
                        continue
                    act.wait_ge(f_full, b.count(nf, n + 1))
                    if what == "xT":
                        if a.affine:
                            for d in range(DC):
                                last = nc.scalar.activation(xf[:, d, :], f_bank[:, d * SEQ:(d + 1) * SEQ], ACT.Identity,
                                                            bias=norm_b[:, d:d + 1], scale=norm_g[:, d:d + 1])
                        else:
                            last = nc.scalar.copy(xt[0][:].rearrange("p d n -> p (d n)"), f_bank[:])
                        last.then_inc(f_hi, 1)
                    elif a.causal and what in ("q", "k"):
                        i = "qk".index(what)
                        nc.scalar.copy(raw[i][:].rearrange("p t h d -> p (t h d)"), f_bank[:]).then_inc(f_free, 1)
                    elif a.causal and what == "v":
                        nc.scalar.copy(v[par][0][:, :, :, 0:dh],
                                       f_bank[:].rearrange("p (t h d) -> p t h d", t=2, h=HEADS)).then_inc(f_hi, 1)
                    elif what == "q":
                        for blk in (0, 2):
                            last = nc.scalar.copy(qs[:, :, :, blk, :],
                                                  f_bank[:].rearrange("p (t h d) -> p t h d", t=2, h=HEADS))
                        last.then_inc(f_hi, 1)
                    elif what == "kv" and not wide:
                        kf = f_bank[0:KEYS, 0:256].rearrange("p (h d) -> p h d", h=HEADS)
                        vf = f_bank[0:KEYS, 256:512].rearrange("p (h d) -> p h d", h=HEADS)
                        nc.scalar.copy(ks[0:KEYS, 0, :, 0, :], kf)
                        nc.scalar.copy(ks[0:KEYS, 0, :, 1, :], kf)
                        nc.scalar.copy(v[par][0][0:KEYS, 0, :, 0:dh], vf).then_inc(f_hi, 1)
                    elif what == "kv":
                        nc.scalar.copy(kt[par][0][:, 0, :], f_bank[:, 0:KEYS])
                        nc.scalar.copy(v[par][0][0:KEYS, 0, 0, 0:dh], f_bank[0:KEYS, 128:192]).then_inc(f_hi, 1)
                    elif what[:2] == "qT":
                        nc.scalar.copy(qt[par][0][:, :, 0:P], f_bank_h.rearrange("p (c n) -> p c n", n=P)).then_inc(f_free, 1)
                    elif what == "kT0":
                        nc.scalar.copy(kt[par][0][:, :, 0:P], f_bank_h.rearrange("p (c n) -> p c n", n=P)).then_inc(f_free, 1)
                    elif what == "kT":
                        nc.scalar.copy(kt[par][0][:, :, :],
                                       f_bank_h[:, 0:8 * turned_w(KEYS)].rearrange("p (c n) -> p c n", c=8)[:, :, 0:KEYS]).then_inc(f_free, 1)
                    elif what[0] == "q":
                        ch = 2 * int(what[1])
                        nc.scalar.copy(qt[par][0][:, ch:ch + 2, :].rearrange("p c n -> p (c n)"), f_bank[:]).then_inc(f_hi, 1)
                    elif what[0] == "k":
                        ch = 4 * int(what[1])
                        nc.scalar.copy(kt[par][0][:, ch:ch + 4, :].rearrange("p c n -> p (c n)"),
                                       f_bank[:, 0:4 * KEYS]).then_inc(f_hi, 1)
                    else:
                        h = 8 * int(what[1])
                        nc.scalar.copy(v[par][0][0:KEYS, 0, h:h + 8, 0:dh],
                                       f_bank[0:KEYS, :].rearrange("p (h d) -> p h d", h=8)).then_inc(f_hi, 1)
                if a.causal and not half:
                    for i, at in enumerate((-8, -6)):
                        if at == s:
                            act.wait_ge(rot_step, b.count(8, 4 * i + 4))
                            st, blks = ((qs, (0, 2)), (ks, (0, 1)))[i]
                            for blk in blks:
                                last = nc.scalar.copy(st[:, :, :, blk, :], rot[i][:])
                            last.then_inc(stack_hi, 1)

            def early_front(b, s):
                front(b, s, 0.5)

            over_steps(act, nu, (exps, early_front, front, probs_hi, output))

        @block.vector
        def _(dve):
            dve.wait_ge(const_ready, a.consts)

            def maxima(b, s):
                u = s + 1
                if not 0 <= u < nu:
                    return
                t, h0, nh, kts = units[u]
                w = kw * len(kts)
                src = c.bank[u % 2][:, 0:nh * w].rearrange("p (h k) -> p h k", h=nh)
                wait(dve, s_full, b.count(nu, u + 1))
                if a.clip_mask is not None:
                    if u == 0:
                        wait(dve, cm_ready, b.count(1, 1))
                    wait(dve, exp_done, b.count(nu, u - 1))
                    dst = clipped[:, u % 2, :].rearrange("p (h k) -> p h k", h=nh)
                    bound = CLIP / a.scale
                    upper = cm_u[:, b.off % 2, t, :].unsqueeze(1).broadcast_to([P, nh, KEYS])
                    nc.vector.scalar_tensor_tensor(out=dst, in0=src, scalar=-bound, in1=upper,
                                                   op0=ALU.max, op1=ALU.min).then_inc(clip_done, 1)
                    dve.wait_ge(clip_done, b.count(nu, u + 1))
                    src = dst
                nc.vector.tensor_reduce(top[:, u % 2, 0:nh], src, AX.X, ALU.max).then_inc(top_done, 1)

            def reciprocals(b, s):
                u = s - 3
                if not 0 <= u < nu:
                    return
                nh = units[u][2]
                sums = c.bank[4 + u % 2][:, 0:nh * (dh + 1)].rearrange("p (h d) -> p h d", h=nh)[:, :, dh]
                wait(dve, pv_full, b.count(nu, u + 1))
                nc.vector.reciprocal(rden[:, u % 2, 0:nh], sums).then_inc(rden_done, 1)

            def shifts(b, s):
                u = s + 1
                if not 0 <= u < nu:
                    return
                nh = units[u][2]
                dve.wait_ge(top_done, b.count(nu, u + 1))
                nc.vector.tensor_scalar(shift[:, u % 2, 0:nh], top[:, u % 2, 0:nh], -a.scale, None,
                                        ALU.mult).then_inc(shift_done, 1)

            def normalise(b, s):
                u = s - 3
                if not 0 <= u < nu:
                    return
                t, h0, nh, kts = units[u]
                heads = c.bank[4 + u % 2][:, 0:nh * (dh + 1)].rearrange("p (h d) -> p h d", h=nh)[:, :, 0:dh]
                dve.wait_ge(rden_done, b.count(nu, u + 1))
                nc.vector.tensor_tensor(o[t][:].rearrange("p (h d) -> p h d", d=dh)[:, h0:h0 + 2 * nh - 1:2, :], heads,
                                        rden[:, u % 2, 0:nh].unsqueeze(2).broadcast_to([P, nh, dh]),
                                        ALU.mult).then_inc(norm_done, 1)

            def probs_lo(b, s):
                u = s - 1
                if not 0 <= u < nu:
                    return
                dve.wait_ge(p_hi, b.count(nu, u + 1))
                nc.vector.tensor_tensor(pt[u % 2][1][0:kw, :], c.bank[2 + u % 2][0:kw, :], pt[u % 2][0][0:kw, :],
                                        ALU.subtract).then_inc(p_lo, 1)

            def output(b, s):
                for n, (what, t, k, at) in enumerate(a.outs):
                    if at != s:
                        continue
                    if what == "turn":
                        i = [x for x in turns].index((what, t, k, at))
                        m = min(4, a.o_chunks)
                        dve.wait_ge(o_hi, b.count(len(turns), i + 1))
                        nc.vector.tensor_tensor(ot[1][:, 4 * k:4 * k + m, :].rearrange("p c n -> p (c n)"),
                                                o_bank[:, 0:m * P],
                                                ot[0][:, 4 * k:4 * k + m, :].rearrange("p c n -> p (c n)"),
                                                ALU.subtract).then_inc(o_free, 1)
                        continue
                    tile = b.count(2, t)
                    dve.wait_ge(o_full, b.count(no, n + 1))
                    if a.store == "x":
                        nc.vector.scalar_tensor_tensor(out=c.x[:, tile, :], in0=o_bank[:, 0:DIM],
                                                       scalar=c.gates_w[:, a.gate:a.gate + 1], in1=c.x[:, tile, :],
                                                       op0=ALU.mult, op1=ALU.add).then_inc(o_free, 1)
                    elif a.store == "h+":
                        nc.vector.scalar_tensor_tensor(out=c.h[:, tile, :], in0=o_bank[:, 0:DIM],
                                                       scalar=1.0 / W_SCALE ** 2, in1=c.h[:, tile, :],
                                                       op0=ALU.mult, op1=ALU.add).then_inc(o_free, 1)
                    else:
                        nc.vector.tensor_scalar(c.h[:, tile, :], o_bank[:, 0:DIM], 1.0 / W_SCALE ** 2, None,
                                                ALU.mult).then_inc(o_free, 1)

            def front(b, s, half=0):
                par = b.off % 2
                if s == -nu - 1 and not half:
                    for t in range(2):
                        tile = b.count(2, t)
                        args = (c.mv[:, tile, 0:1], c.rstd[:, bass.ds(tile, 1)])
                        last = nc.vector.tensor_scalar(xn[:, t, :], c.x[:, tile, :], *args, ALU.subtract, ALU.mult)
                        if t == 1:
                            last.then_inc(xn_ready, 1)
                        if a.store == "h+":
                            r1 = c.rstd1[:, bass.ds(tile, 1)]
                            nc.vector.tensor_scalar(c.h[:, tile, :], c.x[:, tile, :], args[0], r1,
                                                    ALU.subtract, ALU.mult)
                for n, (what, at) in enumerate(a.fronts):
                    if at != s - half:
                        continue
                    if what in ("qT0", "kT0", "kT") or (a.causal and what in ("q", "k")):
                        continue
                    if what in ("qT1", "kT1"):
                        dve.wait_ge(f_full, b.count(nf, n + 1))
                        dst = (qt if what[0] == "q" else kt)[par][0]
                        nc.vector.tensor_copy(dst[:, :, P:2 * P], f_bank_h.rearrange("p (c n) -> p c n", n=P)).then_inc(f_free, 1)
                        continue
                    dve.wait_ge(f_hi, b.count(len(both), both.index(what) + 1))
                    if what == "xT" and a.affine:
                        flat = xf[:].rearrange("p d n -> p (d n)")
                        nc.vector.tensor_copy(xt[0][:].rearrange("p d n -> p (d n)"), flat).then_inc(setup_step, 1)
                        dve.wait_ge(setup_step, b.count(1, 1))
                        nc.vector.tensor_tensor(xt[1][:].rearrange("p d n -> p (d n)"), flat,
                                                xt[0][:].rearrange("p d n -> p (d n)"), ALU.subtract).then_inc(f_free, 1)
                    elif what == "xT":
                        nc.vector.tensor_tensor(xt[1][:].rearrange("p d n -> p (d n)"), f_bank[:],
                                                xt[0][:].rearrange("p d n -> p (d n)"), ALU.subtract).then_inc(f_free, 1)
                    elif what == "v" and a.causal:
                        nc.vector.tensor_tensor(v[par][1][:, :, :, 0:dh],
                                                f_bank[:].rearrange("p (t h d) -> p t h d", t=2, h=HEADS),
                                                v[par][0][:, :, :, 0:dh], ALU.subtract).then_inc(f_free, 1)
                    elif what == "q":
                        nc.vector.tensor_tensor(qs[:, :, :, 1, :],
                                                f_bank[:].rearrange("p (t h d) -> p t h d", t=2, h=HEADS),
                                                qs[:, :, :, 0, :], ALU.subtract).then_inc(f_free, 1)
                    elif what == "kv" and not wide:
                        kf = f_bank[0:KEYS, 0:256].rearrange("p (h d) -> p h d", h=HEADS)
                        vf = f_bank[0:KEYS, 256:512].rearrange("p (h d) -> p h d", h=HEADS)
                        nc.vector.tensor_tensor(ks[0:KEYS, 0, :, 2, :], kf, ks[0:KEYS, 0, :, 0, :], ALU.subtract)
                        if a.add_mask is not None:
                            col = mask_h[:, bass.ds(b.count(1, 0), 1)]
                            nc.vector.tensor_copy(ks[0:KEYS, 0, :, 3, 0], col.broadcast_to([KEYS, HEADS]))
                        nc.vector.tensor_tensor(v[par][1][0:KEYS, 0, :, 0:dh], vf, v[par][0][0:KEYS, 0, :, 0:dh],
                                                ALU.subtract).then_inc(f_free, 1)
                    elif what == "kv":
                        nc.vector.tensor_tensor(kt[par][1][:, 0, :], f_bank[:, 0:KEYS], kt[par][0][:, 0, :], ALU.subtract)
                        nc.vector.tensor_tensor(v[par][1][0:KEYS, 0, 0, 0:dh], f_bank[0:KEYS, 128:192],
                                                v[par][0][0:KEYS, 0, 0, 0:dh], ALU.subtract).then_inc(f_free, 1)
                    elif what[0] == "q":
                        ch = 2 * int(what[1])
                        hi, lo = (x[:, ch:ch + 2, :].rearrange("p c n -> p (c n)") for x in qt[par])
                        nc.vector.tensor_tensor(lo, f_bank[:], hi, ALU.subtract).then_inc(f_free, 1)
                    elif what[0] == "k":
                        ch = 4 * int(what[1])
                        hi, lo = (x[:, ch:ch + 4, :].rearrange("p c n -> p (c n)") for x in kt[par])
                        nc.vector.tensor_tensor(lo, f_bank[:, 0:4 * KEYS], hi, ALU.subtract).then_inc(f_free, 1)
                    else:
                        h = 8 * int(what[1])
                        hi, lo = (x[0:KEYS, 0, h:h + 8, 0:dh] for x in v[par])
                        nc.vector.tensor_tensor(lo, f_bank[0:KEYS, :].rearrange("p (h d) -> p h d", h=8), hi,
                                                ALU.subtract).then_inc(f_free, 1)

            def clip_bounds(b, s):
                if a.clip_mask is None or s != -nu:
                    return
                i = b.off % 2
                dve.wait_ge(cm_landed[i], b.count(8, 16 - 8 * i))
                nc.vector.tensor_scalar(cm_t[:, i], cm_i[:, i], 0, NEG_BIG, ALU.is_equal, ALU.mult).then_inc(cm_step, 1)
                dve.wait_ge(cm_step, b.count(1, 1))
                nc.vector.tensor_scalar(cm_u[:, i], cm_t[:, i], CLIP / a.scale, None, ALU.add).then_inc(cm_ready, 1)

            def early_front(b, s):
                front(b, s, 0.5)

            over_steps(dve, nu, (maxima, reciprocals, shifts, normalise, early_front, front, probs_lo, output, clip_bounds))


def quantized_linear(nc, c, tag, gate, next_weights):
    ROUND = 12582912.0
    with ExitStack() as ctx:
        sb = lambda n, sh, dt: ctx.enter_context(nc.sbuf_tensor(f"{tag}_{n}", sh, dt))
        sem = ctx.enter_context(stage_semaphores(nc, tag))
        w8 = sb("w_int8", [P, DC, DIM // 4], I32)
        w = sb("w_f16", [P, DC, DIM], F16)
        w_row, b_row = sb("w_scale_row", [P, DIM], F32), sb("bias_row", [P, DIM], F32)
        xn = sb("xn", [P, 2, DIM], F32)
        amax, xs, inv = (sb(n, [P, 2, 2], F32) for n in ("amax", "x_scale", "x_inv"))
        qa, qb = sb("q_a", [P, 2, DIM], F32), sb("q_b", [P, 2, DIM], F32)
        xq = [sb(f"xq{i}", [P, 2, DIM], F16) for i in range(2)]
        xqt = [sb(f"xqT{i}", [P, DC, SEQ], F16) for i in range(2)]
        ya, yb = sb("y_a", [P, 2, DIM], F32), sb("y_b", [P, 2, DIM], F32)
        loaded, w_ready = sem("loaded"), sem("w_ready")
        step, quantised = sem("quant_step"), sem("quantised")
        turned, copied, product, out_step, updated = sem("turned"), sem("copied"), sem("product"), sem("out_step"), sem("updated")
        block = ctx.enter_context(nc.Block())

        @block.sync
        def _(sp):
            sp.dma_start(w8[:], c.dram["l1f_w"]).then_inc(loaded, 16)
            sp.dma_start(w_row[:], c.dram["l1f_scale"].partition_broadcast(P)).then_inc(loaded, 16)
            sp.dma_start(b_row[:], c.dram["l1f_bias"].partition_broadcast(P)).then_inc(loaded, 16)
            sp.wait_ge(loaded, 48)

        @block.gpsimd
        def _(pool):
            prep_weights(nc, c, pool, next_weights)

        @block.vector
        def _(dve):
            def quantise(b, s):
                if s != -2:
                    return
                i = b.off % 2
                n = lambda k: b.count(7, k)
                for t in range(2):
                    tile = b.count(2, t)
                    last = nc.vector.tensor_scalar(xn[:, t, :], c.x[:, tile, :], c.mv[:, tile, 0:1],
                                                   c.rstd[:, bass.ds(tile, 1)], ALU.subtract, ALU.mult)
                last.then_inc(step, 1)
                dve.wait_ge(step, n(1))
                nc.vector.tensor_reduce(amax[:, i, :], xn[:], AX.X, ALU.max, apply_absolute_value=True).then_inc(step, 1)
                dve.wait_ge(step, n(2))
                nc.vector.tensor_scalar(xs[:, i, :], amax[:, i, :], 1e-6, 1.0 / 127.0, ALU.max, ALU.mult).then_inc(step, 1)
                dve.wait_ge(step, n(3))
                nc.vector.reciprocal(inv[:, i, :], xs[:, i, :]).then_inc(step, 1)
                dve.wait_ge(step, n(4))
                for t in range(2):
                    last = nc.vector.tensor_scalar(qa[:, t, :], xn[:, t, :], inv[:, i, t:t + 1], 127.0, ALU.mult, ALU.min)
                last.then_inc(step, 1)
                dve.wait_ge(step, n(5))
                nc.vector.tensor_scalar(qb[:], qa[:], -128.0, ROUND, ALU.max, ALU.add).then_inc(step, 1)
                dve.wait_ge(step, n(6))
                wait(dve, turned, b.count(1, -1))
                nc.vector.tensor_scalar(xq[i][:], qb[:], ROUND, None, ALU.subtract).then_inc(step, 1)

            def finish(b, s):
                if s != 0:
                    return
                i = b.off % 2
                dve.wait_ge(product, b.count(1, 1))
                for t in range(2):
                    last = nc.vector.scalar_tensor_tensor(out=ya[:, t, :], in0=c.bank[2 + i][:, t * DIM:(t + 1) * DIM],
                                                          scalar=xs[:, i, t:t + 1], in1=w_row[:],
                                                          op0=ALU.mult, op1=ALU.mult)
                last.then_inc(out_step, 1)
                dve.wait_ge(out_step, b.count(2, 1))
                nc.vector.tensor_tensor(yb[:], ya[:], b_row[:].unsqueeze(1).broadcast_to([P, 2, DIM]),
                                        ALU.add).then_inc(out_step, 1)
                dve.wait_ge(out_step, b.count(2, 2))
                tile = b.count(2, 0)
                rows = c.x[:, bass.ds(tile, 2), :]
                nc.vector.scalar_tensor_tensor(out=rows, in0=yb[:], scalar=c.gates[:, gate:gate + 1], in1=rows,
                                               op0=ALU.mult, op1=ALU.add).then_inc(updated, 1)

            dve.wait_ge(loaded, 48)
            nc.vector.tensor_copy(w[:], w8[:].bitcast(mybir.dt.int8)).then_inc(w_ready, 1)
            over_steps(dve, 1, (finish, quantise))

        @block.tensor
        def _(pe):
            pe.wait_ge(w_ready, 1)

            def multiply(b, s):
                if s != 0:
                    return
                i = b.off % 2
                pe.wait_ge(copied, b.count(1, 1))
                wait(pe, updated, b.count(1, -1))
                for t in range(2):
                    for d in range(DC):
                        last = nc.tensor.matmul(c.bank[2 + i][:, t * DIM:(t + 1) * DIM],
                                                xqt[i][:, d, t * P:(t + 1) * P], w[:, d, :], start=d == 0, stop=d == 1)
                last.then_inc(product, 1)

            def turn(b, s):
                if s != -1:
                    return
                i = b.off % 2
                pe.wait_ge(step, b.count(7, 7))
                wait(pe, copied, b.count(1, -1))
                out = c.bank[i][:].bitcast(F16)
                for d in range(DC):
                    for t in range(2):
                        last = nc.tensor.transpose(out[:, d * SEQ + t * P:d * SEQ + (t + 1) * P],
                                                   xq[i][:, t, d * P:(d + 1) * P], c.ident_h[:])
                last.then_inc(turned, 1)

            over_steps(pe, 1, (multiply, turn))

        @block.scalar
        def _(act):
            def copy(b, s):
                if s != -1:
                    return
                i = b.off % 2
                act.wait_ge(turned, b.count(1, 1))
                wait(act, product, b.count(1, -1))
                nc.scalar.copy(xqt[i][:].rearrange("p d n -> p (d n)"),
                               c.bank[i][:].bitcast(F16)[:, 0:2 * SEQ]).then_inc(copied, 1)

            over_steps(act, 1, (copy,))


def scaled_linear(nc, c, tag, gate, weights):
    with ExitStack() as ctx:
        sb = lambda n, sh, dt: ctx.enter_context(nc.sbuf_tensor(f"{tag}_{n}", sh, dt))
        sem = ctx.enter_context(stage_semaphores(nc, tag))
        s_row, b_row = sb("scale_row", [P, DIM], F32), sb("bias_row", [P, DIM], F32)
        xn = [sb(f"xn{i}", [P, 2, DIM], F32) for i in range(2)]
        xt = [[sb(f"xT_{p}{i}", [P, DC, SEQ], F16) for p in ("hi", "lo")] for i in range(2)]
        ya = sb("y_a", [P, 2, DIM], F32)
        yb = sb("y_b", [P, 2, DIM], F32)
        loaded, rows_ready = sem("loaded"), sem("rows_ready")
        normed, turned, hi_done, lo_done = sem("normed"), sem("turned"), sem("hi_done"), sem("lo_done")
        product, out_step, updated = sem("product"), sem("out_step"), sem("updated")
        block = ctx.enter_context(nc.Block())

        @block.sync
        def _(sp):
            sp.dma_start(s_row[:], c.dram["l3f_scale"].partition_broadcast(P)).then_inc(loaded, 16)
            sp.dma_start(b_row[:], c.dram["l3f_bias"].partition_broadcast(P)).then_inc(loaded, 16)
            sp.wait_ge(loaded, 32)

        @block.vector
        def _(dve):
            def norm(b, s):
                if s != -2:
                    return
                wait(dve, turned, b.count(1, -1))
                for t in range(2):
                    tile = b.count(2, t)
                    last = nc.vector.tensor_scalar(xn[b.off % 2][:, t, :], c.x[:, tile, :], c.mv[:, tile, 0:1],
                                                   c.rstd[:, bass.ds(tile, 1)], ALU.subtract, ALU.mult)
                last.then_inc(normed, 1)

            def split(b, s):
                if s != -1:
                    return
                i = b.off % 2
                hi, lo = (x[:].rearrange("p d n -> p (d n)") for x in xt[i])
                dve.wait_ge(hi_done, b.count(1, 1))
                nc.vector.tensor_tensor(lo, c.bank[i][:], hi, ALU.subtract).then_inc(lo_done, 1)

            def finish(b, s):
                if s != 0:
                    return
                dve.wait_ge(product, b.count(1, 1))
                nc.vector.tensor_tensor(ya[:], c.bank[2 + b.off % 2][:].rearrange("p (t d) -> p t d", t=2),
                                        s_row[:].unsqueeze(1).broadcast_to([P, 2, DIM]), ALU.mult).then_inc(out_step, 1)
                dve.wait_ge(out_step, b.count(2, 1))
                nc.vector.tensor_tensor(yb[:], ya[:], b_row[:].unsqueeze(1).broadcast_to([P, 2, DIM]),
                                        ALU.add).then_inc(out_step, 1)
                dve.wait_ge(out_step, b.count(2, 2))
                rows = c.x[:, bass.ds(b.count(2, 0), 2), :]
                nc.vector.tensor_tensor(rows, yb[:], rows, ALU.add).then_inc(updated, 1)

            dve.wait_ge(loaded, 32)
            g = c.gates[:, gate:gate + 1]
            nc.vector.tensor_scalar(s_row[:], s_row[:], 1.0 / 127.0 / W_SCALE, g, ALU.mult, ALU.mult).then_inc(rows_ready, 1)
            nc.vector.tensor_scalar(b_row[:], b_row[:], g, None, ALU.mult).then_inc(rows_ready, 1)
            dve.wait_ge(rows_ready, 2)
            over_steps(dve, 1, (norm, split, finish))

        @block.scalar
        def _(act):
            def copy(b, s):
                if s != -1:
                    return
                i = b.off % 2
                act.wait_ge(turned, b.count(1, 1))
                nc.scalar.copy(xt[i][0][:].rearrange("p d n -> p (d n)"), c.bank[i][:]).then_inc(hi_done, 1)

            over_steps(act, 1, (copy,))

        @block.tensor
        def _(pe):
            w = lambda d: tuple(c.arena[weights.slot][:, k, d * DIM:(d + 1) * DIM] for k in range(2))

            def multiply(b, s):
                if s != 0:
                    return
                i = b.off % 2
                pe.wait_ge(lo_done, b.count(1, 1))
                wait(pe, updated, b.count(1, -1))
                for t in range(2):
                    for d in range(DC):
                        last = three_products(nc, c.bank[2 + i][:, t * DIM:(t + 1) * DIM],
                                              [x[:, d, t * P:(t + 1) * P] for x in xt[i]], w(d), d == 0, d == DC - 1)
                last.then_inc(product, 1)

            def turn(b, s):
                if s != -1:
                    return
                i = b.off % 2
                pe.wait_ge(normed, b.count(1, 1))
                wait(pe, lo_done, b.count(1, -1))
                for d in range(DC):
                    for t in range(2):
                        last = nc.tensor.transpose(c.bank[i][:, d * SEQ + t * P:d * SEQ + (t + 1) * P],
                                                   xn[i][:, t, d * P:(d + 1) * P], c.ident[:])
                last.then_inc(turned, 1)

            over_steps(pe, 1, (turn, multiply))


def norm_context(nc, c, tag, gain, shift):
    with ExitStack() as ctx:
        sb = lambda n, sh, dt: ctx.enter_context(nc.sbuf_tensor(f"{tag}_{n}", sh, dt))
        sem = ctx.enter_context(stage_semaphores(nc, tag))
        cx = sb("rows", [KEYS, BATCH, DIM], F32)
        stats, mv = sb("stats", [KEYS, BATCH, 6], F32), sb("mv", [KEYS, BATCH, 2], F32)
        var_eps, rstd = sb("var_eps", [KEYS, BATCH], F32), sb("rstd", [KEYS, BATCH], F32)
        g, b = sb("gain", [P, DC], F32), sb("shift", [P, DC], F32)
        scaled = sb("scaled", [P, 2, 4 * KEYS], F32)
        loaded, stat_done, var_done, pow_done = sem("loaded"), sem("stat_done"), sem("var_done"), sem("pow_done")
        normed, full, affine, hi_done, lo_done = (sem(n) for n in ("normed", "full", "affine", "hi_done", "lo_done"))
        block = ctx.enter_context(nc.Block())
        groups = DC * BATCH // 4

        def cut(grp):
            return grp % DC, grp // DC * 4

        @block.sync
        def _(sp):
            sp.dma_start(cx[:], c.dram["ctx_1024"].rearrange("b k d -> k b d")).then_inc(loaded, 16)
            sp.dma_start(g[:], gain).then_inc(loaded, 16)
            sp.dma_start(b[:], shift).then_inc(loaded, 16)

        @block.vector
        def _(dve):
            dve.wait_ge(loaded, 48)
            for k in range(BATCH):
                nc.vector.bn_stats(stats[:, k, :], cx[:, k, :]).then_inc(stat_done, 1)
            for k in range(BATCH):
                dve.wait_ge(stat_done, k + 1)
                nc.vector.bn_aggr(mv[:, k, :], stats[:, k, :]).then_inc(var_done, 1)
            dve.wait_ge(pow_done, 2)
            for k in range(BATCH):
                nc.vector.tensor_scalar(cx[:, k, :], cx[:, k, :], mv[:, k, 0:1], rstd[:, k:k + 1],
                                        ALU.subtract, ALU.mult).then_inc(normed, 1)
            for grp in range(groups):
                d, b0 = cut(grp)
                cols = slice(b0 * KEYS, (b0 + 4) * KEYS)
                dve.wait_ge(affine, grp + 1)
                nc.vector.tensor_copy(c.ct[0][:, d, cols], scaled[:, grp % 2, :]).then_inc(hi_done, 1)
                dve.wait_ge(hi_done, grp + 1)
                nc.vector.tensor_tensor(c.ct[1][:, d, cols], scaled[:, grp % 2, :], c.ct[0][:, d, cols],
                                        ALU.subtract).then_inc(lo_done, 1)

        @block.gpsimd
        def _(pool):
            col = lambda i: c.consts[0:KEYS, i:i + 1].broadcast_to([KEYS, BATCH])
            pool.wait_ge(var_done, BATCH)
            nc.gpsimd.tensor_tensor(var_eps[:], mv[:, :, 1], col(0), ALU.add).then_inc(pow_done, 1)
            pool.wait_ge(pow_done, 1)
            nc.gpsimd.tensor_tensor(rstd[:], var_eps[:], col(1), ALU.pow).then_inc(pow_done, 1)

        @block.tensor
        def _(pe):
            for grp in range(groups):
                d, b0 = cut(grp)
                pe.wait_ge(normed, b0 + 4)
                wait(pe, affine, grp - 1)
                for j in range(4):
                    last = nc.tensor.transpose(c.bank[grp % 2][:, j * KEYS:(j + 1) * KEYS],
                                               cx[:, b0 + j, d * P:(d + 1) * P], c.ident[0:KEYS, 0:KEYS])
                last.then_inc(full, 1)

        @block.scalar
        def _(act):
            act.wait_ge(loaded, 48)
            for grp in range(groups):
                d, b0 = cut(grp)
                wait(act, lo_done, grp - 1)
                act.wait_ge(full, grp + 1)
                nc.scalar.activation(scaled[:, grp % 2, :], c.bank[grp % 2][:, 0:4 * KEYS], ACT.Identity,
                                     bias=b[:, d:d + 1], scale=g[:, d:d + 1]).then_inc(affine, 1)


class GatedFf:

    def __init__(self, tag, hidden, weights=None, gate=None, norm_g=None, norm_b=None, experts=None, steps=BATCH,
                 dynamic=False):
        self.tag, self.weights, self.nh, self.gate = tag, weights, hidden, gate
        self.norm_g, self.norm_b, self.experts, self.steps, self.dynamic = norm_g, norm_b, experts, steps, dynamic


def gated_ff(nc, c, f, next_weights=None, r=None):
    nh, n_steps, routed = f.nh, f.steps, f.experts is not None
    with ExitStack() as ctx:
        sb = lambda n, sh, dt: ctx.enter_context(nc.sbuf_tensor(f"{f.tag}_{n}", sh, dt))
        sem = ctx.enter_context(stage_semaphores(nc, f.tag))
        xn = [sb(f"rows{i}", [P, 2, DIM], F32) for i in range(2)]
        xt = [[sb(f"xT_{p}{i}", [P, DC, SEQ], F16) for p in ("hi", "lo")] for i in range(2)]
        silu = [sb(f"silu{i}", [P, SEQ], F32) for i in range(UP_BANKS)]
        prod = [sb(f"prod{i}", [P, SEQ], F32) for i in range(UP_BANKS)]
        g = [[sb(f"g_{p}{i}", [P, nh, SEQ], F16) for p in ("hi", "lo")] for i in range(2)]
        if f.norm_g is not None:
            gain, shift = sb("gain", [P, DC], F32), sb("shift", [P, DC], F32)
            xf = sb("xT_f32", [P, DC, SEQ], F32)
        y = [sb(f"y{i}", [P, 2, DIM], F32) for i in range(2)]
        loaded = sem("loaded")
        rows_ready, x_full, x_hi, x_split, x_free = (sem(n) for n in ("rows_ready", "x_full", "x_hi", "x_split", "x_free"))
        up_full, silu_done, prod_done, g_hi, g_lo = (sem(n) for n in ("up_full", "silu_done", "prod_done", "g_hi", "g_lo"))
        down_full, y_done, bank_free = sem("down_full"), sem("y_done"), sem("bank_free")
        if routed:
            gathered = [sem("gathered0"), sem("gathered1")]
            up_landed, down_landed = ([sem(f"{n}_landed{i}") for i in range(2)] for n in ("up", "down"))
            added, index_ready, passed = (sem(n) for n in ("added", "index_ready", "passed"))
            reloaded, stat_done = [sem(f"reloaded{k}") for k in range(X_LOADS)], sem("stat_done")
            from_rows = [sb(f"from_rows{i}", [P, 2], I32) for i in range(2)]
            to_rows = [sb(f"to_rows{i}", [P, 2], I32) for i in range(2)]
        block = ctx.enter_context(nc.Block())

        hid = nh * P
        up_off, gate_off, down_off = 0, hid, DC * 2 * hid
        if routed:
            e = f.experts
            used_cols = down_off + nh * DIM
            h_flat = c.h[:].rearrange("p t d -> p (t d)").bitcast(F16)
            halves = lambda x: x.rearrange("p (k n) -> p k n", k=2)
            w_buf = [halves(h_flat[:, 0:2 * used_cols])]
            if 4 * used_cols <= 2 * TILES * DIM:
                w_buf.append(halves(h_flat[:, 2 * used_cols:4 * used_cols]))
            else:
                w_buf.append(c.arena[1][:, :, 0:used_cols])
        else:
            w_buf = [c.arena[f.weights.slot][:]] * 2

        def ring(b, j):
            return (nh * (b.off % 2) + j) % UP_BANKS

        def weight(b, off, n):
            return tuple(w_buf[b.off % 2][:, k, off:off + n] for k in range(2))

        def every_second(b, per_step):
            return b.count(per_step // 2, per_step - per_step // 2 * (b.off % 2))

        @block.gpsimd
        def _(pool):
            if not routed:
                prep_weights(nc, c, pool, next_weights)
                return

            def gather(b, s):
                if s != -7:
                    return
                i = b.off % 2
                wait(pool, x_full, b.count(1, -1))
                pool.wait_ge(index_ready, b.count(1, 1))
                pool.sem_inc(passed, 1)
                for t in range(2):
                    nc.gpsimd.indirect_dma_start(out=xn[i][:, t, :], out_offset=None, in_=r.rows,
                                                 in_offset=bass.IndirectOffsetOnAxis(ap=from_rows[i][:, t:t + 1], axis=0)
                                                 ).then_inc(gathered[i], 16)

            def scatter(b, s):
                if s != nh + 3:
                    return
                pool.wait_ge(bank_free, b.count(1, 2))
                for t in range(2):
                    wait(pool, added, b.count(32, 16 * t))
                    pool.sem_inc(passed, 1)
                    nc.gpsimd.indirect_dma_start(out=r.total_rows, out_offset=bass.IndirectOffsetOnAxis(ap=to_rows[b.off % 2][:, t:t + 1], axis=0),
                                                 in_=y[b.off % 2][:, t, :], in_offset=None,
                                                 compute_op=ALU.add).then_inc(added, 16)

            def split_weights(b, s):
                if next_weights is None or b.i is not None or s != 1:
                    return
                steps = (0, 1, n_steps - 2, n_steps - 1)
                if b.off in steps:
                    prep_weights(nc, c, pool, next_weights, WEIGHT_PARTS // 2 + steps.index(b.off), WEIGHT_PARTS)

            over_steps(pool, nh, (gather, scatter, split_weights), n_steps)
            pool.wait_ge(added, 32 * n_steps)

        @block.sync
        def _(sp):
            if f.norm_g is not None:
                sp.dma_start(gain[:], f.norm_g).then_inc(loaded, 16)
                sp.dma_start(shift[:], f.norm_b).then_inc(loaded, 16)
                sp.wait_ge(loaded, 32)
            if routed:
                per = n_steps // EXPERTS

                def expert_columns(b, off, n):
                    if f.dynamic:
                        expert = sp.value_load(r.step_expert[0:1, bass.ds(b.count(1, 0), 1)], min_val=0, max_val=EXPERTS - 1)
                    else:
                        expert = b.off // per if b.i is None else b.i + b.off // per
                    return bass.ds(expert * e.cols + off, n)

                def load_up(b, s):
                    if s != -nh:
                        return
                    i = b.off % 2
                    columns = expert_columns(b, 0, down_off)
                    wait(sp, up_full, b.count(nh, -nh))
                    sp.dma_start(w_buf[i][:, :, 0:down_off], e.split[:, :, columns]
                                 ).then_inc(up_landed[i], 16)

                def load_down(b, s):
                    if s != 4 - nh:
                        return
                    i = b.off % 2
                    columns = expert_columns(b, down_off, used_cols - down_off)
                    wait(sp, down_full, b.count(1, -1))
                    sp.dma_start(w_buf[i][:, :, down_off:used_cols],
                                 e.split[:, :, columns]
                                 ).then_inc(down_landed[i], 16)

                over_steps(sp, nh, (load_up, load_down), n_steps)
                sp.wait_ge(added, 32 * n_steps)
                load_x(sp, c, r.total_rows[0:TOKENS, :].rearrange("(t p) d -> p t d", p=P), reloaded)
        @block.tensor
        def _(pe):
            def up(b, s):
                if not 0 <= s < nh:
                    return
                if s == 0:
                    pe.wait_ge(x_free, b.count(1, 1))
                    if routed:
                        pe.wait_ge(up_landed[b.off % 2], every_second(b, 16))
                wait(pe, g_lo, b.count(nh, s + 1 - UP_BANKS))
                for i, off in enumerate((gate_off, up_off)):
                    for d in range(DC):
                        last = three_products(nc, c.bank[ring(b, s)][:, i * SEQ:(i + 1) * SEQ],
                                              weight(b, d * 2 * hid + off + s * P, P),
                                              [x[:, d, :] for x in xt[b.off % 2]], d == 0, d == DC - 1)
                last.then_inc(up_full, 1)

            def down(b, s):
                t = s - nh - 1
                if not 0 <= t < 2:
                    return
                if t == 0:
                    pe.wait_ge(g_lo, b.count(nh, nh))
                    if routed:
                        pe.wait_ge(down_landed[b.off % 2], every_second(b, 16))
                    wait(pe, bank_free, b.count(1, 0))
                for j in range(nh):
                    last = three_products(nc, c.bank[4 + b.off % 2][:, t * DIM:(t + 1) * DIM],
                                          [x[:, j, t * P:(t + 1) * P] for x in g[b.off % 2]],
                                          weight(b, down_off + j * DIM, DIM), j == 0, j == nh - 1)
                if t == 1:
                    last.then_inc(down_full, 1)

            def turn(b, s):
                if s != -3:
                    return
                if routed:
                    pe.wait_ge(gathered[b.off % 2], every_second(b, 32))
                else:
                    pe.wait_ge(rows_ready, b.count(1, 1))
                wait(pe, x_free, b.count(1, 0))
                for d in range(DC):
                    for t in range(2):
                        last = nc.tensor.transpose(c.bank[6][:, d * SEQ + t * P:d * SEQ + (t + 1) * P],
                                                   xn[b.off % 2][:, t, d * P:(d + 1) * P], c.ident[:])
                last.then_inc(x_full, 1)

            over_steps(pe, nh, (up, down, turn), n_steps)

        @block.scalar
        def _(act):
            if f.norm_g is not None:
                act.wait_ge(loaded, 32)

            def silus(b, s):
                if not 0 <= s < nh:
                    return
                act.wait_ge(up_full, b.count(nh, s + 1))
                nc.scalar.activation(silu[ring(b, s)][:], c.bank[ring(b, s)][:, 0:SEQ], ACT.Silu,
                                     scale=1.0 / W_SCALE).then_inc(silu_done, 1)

            def hi(b, s):
                j = s - 1
                if not 0 <= j < nh:
                    return
                act.wait_ge(prod_done, b.count(nh, j + 1))
                if j == 0:
                    wait(act, down_full, b.count(1, -1))
                nc.scalar.copy(g[b.off % 2][0][:, j, :], prod[ring(b, j)][:]).then_inc(g_hi, 1)

            def rows_hi(b, s):
                if s != -3:
                    return
                act.wait_ge(x_full, b.count(1, 1))
                if f.norm_g is not None:
                    wait(act, x_free, b.count(1, 0))
                    for d in range(DC):
                        last = nc.scalar.activation(xf[:, d, :], c.bank[6][:, d * SEQ:(d + 1) * SEQ], ACT.Identity,
                                                    bias=shift[:, d:d + 1], scale=gain[:, d:d + 1])
                else:
                    last = nc.scalar.copy(xt[b.off % 2][0][:].rearrange("p d n -> p (d n)"), c.bank[6][:])
                last.then_inc(x_hi, 1)

            over_steps(act, nh, (silus, hi, rows_hi), n_steps)

        @block.vector
        def _(dve):
            def products(b, s):
                if not 0 <= s < nh:
                    return
                dve.wait_ge(silu_done, b.count(nh, s + 1))
                nc.vector.scalar_tensor_tensor(out=prod[ring(b, s)][:], in0=c.bank[ring(b, s)][:, SEQ:2 * SEQ],
                                               scalar=1.0 / W_SCALE, in1=silu[ring(b, s)][:],
                                               op0=ALU.mult, op1=ALU.mult).then_inc(prod_done, 1)

            def lo(b, s):
                j = s - 1
                if not 0 <= j < nh:
                    return
                dve.wait_ge(g_hi, b.count(nh, j + 1))
                hi_part, lo_part = (x[:, j, :] for x in g[b.off % 2])
                nc.vector.tensor_tensor(lo_part, prod[ring(b, j)][:], hi_part, ALU.subtract).then_inc(g_lo, 1)

            def rows(b, s):
                if s != -4 or routed:
                    return
                wait(dve, x_full, b.count(1, -1))
                for t in range(2):
                    tile = b.count(2, t)
                    last = nc.vector.tensor_scalar(xn[b.off % 2][:, t, :], c.x[:, tile, :], c.mv[:, tile, 0:1],
                                                   c.rstd[:, bass.ds(tile, 1)], ALU.subtract, ALU.mult)
                last.then_inc(rows_ready, 1)

            def index(b, s):
                if s != -8 or not routed:
                    return
                i = b.off % 2
                wait(dve, gathered[i], b.count(16, -16 * i))
                nc.vector.tensor_copy(from_rows[i][:], r.slot_token[:, bass.ds(b.count(2, 0), 2)]).then_inc(index_ready, 1)

            def rows_lo(b, s):
                if s != -3:
                    return
                dve.wait_ge(x_hi, b.count(1, 1))
                hi_part, lo_part = (x[:].rearrange("p d n -> p (d n)") for x in xt[b.off % 2])
                src = c.bank[6][:]
                if f.norm_g is not None:
                    src = xf[:].rearrange("p d n -> p (d n)")
                    nc.vector.tensor_copy(hi_part, src).then_inc(x_split, 1)
                    dve.wait_ge(x_split, b.count(1, 1))
                nc.vector.tensor_tensor(lo_part, src, hi_part, ALU.subtract).then_inc(x_free, 1)

            def update(b, s):
                if s != nh + 3:
                    return
                dve.wait_ge(down_full, b.count(1, 1))
                bank = c.bank[4 + b.off % 2]
                two = bass.ds(b.count(2, 0), 2)
                if not routed:
                    nc.vector.scalar_tensor_tensor(out=y[b.off % 2][:], in0=bank[:].rearrange("p (t d) -> p t d", t=2),
                                                   scalar=1.0 / W_SCALE, in1=c.h[:, two, :],
                                                   op0=ALU.mult, op1=ALU.add).then_inc(y_done, 1)
                    dve.wait_ge(y_done, b.count(1, 1))
                    nc.vector.scalar_tensor_tensor(out=c.x[:, two, :], in0=y[b.off % 2][:], scalar=c.gates[:, f.gate:f.gate + 1],
                                                   in1=c.x[:, two, :], op0=ALU.mult, op1=ALU.add).then_inc(bank_free, 1)
                else:
                    wait(dve, added, b.count(32, -16))
                    nc.vector.tensor_copy(to_rows[b.off % 2][:], r.slot_token[:, bass.ds(b.count(2, 0), 2)])
                    for t in range(2):
                        last = nc.vector.tensor_scalar(y[b.off % 2][:, t, :], bank[:, t * DIM:(t + 1) * DIM],
                                                       r.slot_weight[:, bass.ds(b.count(2, t), 1)], None, ALU.mult)
                    last.then_inc(bank_free, 1)

            dve.sem_inc(bank_free, 1)
            over_steps(dve, nh, (update, products, lo, rows_lo, rows, index), n_steps)
            if routed:
                stats_of_loads(nc, c, dve, reloaded, stat_done)


def by_expert(x):
    return x.rearrange("p (t e) -> p e t", e=EXPERTS)


def over_tiles(x):
    return x.unsqueeze(1).broadcast_to([P, TILES, EXPERTS])


def tiled(x):
    return x.rearrange("p (t e) -> p t e", e=EXPERTS)


def over_experts(x):
    return x.unsqueeze(2).broadcast_to([P, TILES, EXPERTS])


def norm_rows_of_h(nc, c, tag):
    with ExitStack() as ctx:
        sem = ctx.enter_context(stage_semaphores(nc, tag))
        stat_done, var_done, pow_done = sem("stat_done"), sem("var_done"), sem("pow_done")
        block = ctx.enter_context(nc.Block())

        @block.vector
        def _(dve):
            for t in range(TILES):
                nc.vector.bn_stats(c.stats[:, t, :], c.h[:, t, :]).then_inc(stat_done, 1)
            for t in range(TILES):
                dve.wait_ge(stat_done, t + 1)
                nc.vector.bn_aggr(c.mv[:, t, :], c.stats[:, t, :]).then_inc(var_done, 1)

        @block.gpsimd
        def _(pool):
            def col(i):
                return c.consts[:, i:i + 1].broadcast_to([P, TILES])
            pool.wait_ge(var_done, TILES)
            mean, var = c.mv[:, :, 0], c.mv[:, :, 1]
            nc.gpsimd.tensor_tensor(c.tmp_a[:], mean, mean, ALU.mult).then_inc(pow_done, 1)
            pool.wait_ge(pow_done, 1)
            nc.gpsimd.tensor_tensor(c.tmp_a[:], c.tmp_a[:], var, ALU.add).then_inc(pow_done, 1)
            pool.wait_ge(pow_done, 2)
            nc.gpsimd.tensor_tensor(c.tmp_a[:], c.tmp_a[:], col(2), ALU.add).then_inc(pow_done, 1)
            pool.wait_ge(pow_done, 3)
            nc.gpsimd.tensor_tensor(c.rstd[:], c.tmp_a[:], col(1), ALU.pow).then_inc(pow_done, 1)


WEIGHT_PARTS = 8


def router_scores(nc, c, r, tag, source, weight_off, slot, norm_g, norm_b, next_weights, parts=(0,)):
    with ExitStack() as ctx:
        sb = lambda n, sh, dt: ctx.enter_context(nc.sbuf_tensor(f"{tag}_{n}", sh, dt))
        sem = ctx.enter_context(stage_semaphores(nc, tag))
        xn = [sb(f"xn{i}", [P, 2, DIM], F32) for i in range(2)]
        xf = [sb(f"xT_f32{i}", [P, DC, SEQ], F32) for i in range(2)]
        xt = [[sb(f"xT_{p}{i}", [P, DC, SEQ], F16) for p in ("hi", "lo")] for i in range(2)]
        gain, shift = sb("gain", [P, DC], F32), sb("shift", [P, DC], F32)
        loaded, rows_ready, turned, copied = sem("loaded"), sem("rows_ready"), sem("turned"), sem("copied")
        hi_done, lo_done, product, stored = sem("hi_done"), sem("lo_done"), sem("product"), sem("stored")
        dumped, rows_stored = sem("dumped"), [sem("rows_stored0"), sem("rows_stored1")]
        block = ctx.enter_context(nc.Block())

        @block.sync
        def _(sp):
            sp.dma_start(gain[:], norm_g).then_inc(loaded, 16)
            sp.dma_start(shift[:], norm_b).then_inc(loaded, 16)
            by_tile = lambda dram: dram.rearrange("(t p) d -> p t d", p=P)
            sp.dma_start(by_tile(r.total_rows[0:TOKENS, :]), c.x[:]).then_inc(dumped, 16)
            sp.dma_start(r.total_rows[TOKENS:, :], c.x[:, 0, :]).then_inc(dumped, 16)
            sp.dma_start(r.rows[TOKENS:, :], c.x[:, 0, :]).then_inc(dumped, 16)

            def store_rows(b, s):
                if s != -1:
                    return
                i = b.off % 2
                sp.wait_ge(rows_ready, b.count(1, 1))
                sp.dma_start(by_tile(r.rows[bass.ds(b.count(STEP_ROWS, 0), STEP_ROWS), :]), xn[i][:]).then_inc(rows_stored[i], 16)

            over_steps(sp, 1, (store_rows,))
            for i in range(2):
                sp.wait_ge(rows_stored[i], 16 * BATCH // 2)
            sp.wait_ge(dumped, 48)
            sp.wait_ge(loaded, 32)

        @block.gpsimd
        def _(pool):
            for part in parts:
                prep_weights(nc, c, pool, next_weights, part, 1 if len(parts) == 1 else WEIGHT_PARTS)

        @block.vector
        def _(dve):
            def rows(b, s):
                if s != -2:
                    return
                wait(dve, turned, b.count(1, -1))
                if b.i is not None or b.off >= 2:
                    dve.wait_ge(rows_stored[b.off % 2], b.count(8, -8 * (b.off % 2)))
                for t in range(2):
                    tile = b.count(2, t)
                    rstd = c.rstd[:, bass.ds(tile, 1)]
                    if source == "x":
                        last = nc.vector.tensor_scalar(xn[b.off % 2][:, t, :], c.x[:, tile, :], c.mv[:, tile, 0:1], rstd,
                                                       ALU.subtract, ALU.mult)
                    else:
                        last = nc.vector.tensor_scalar(xn[b.off % 2][:, t, :], c.h[:, tile, :], rstd, None, ALU.mult)
                last.then_inc(rows_ready, 1)

            def split(b, s):
                if s != -1:
                    return
                i = b.off % 2
                src = xf[i][:].rearrange("p d n -> p (d n)")
                hi, lo = (x[:].rearrange("p d n -> p (d n)") for x in xt[i])
                dve.wait_ge(copied, b.count(1, 1))
                wait(dve, product, b.count(1, -1))
                nc.vector.tensor_copy(hi, src).then_inc(hi_done, 1)
                dve.wait_ge(hi_done, b.count(1, 1))
                nc.vector.tensor_tensor(lo, src, hi, ALU.subtract).then_inc(lo_done, 1)

            def finish(b, s):
                if s != 0:
                    return
                dve.wait_ge(product, b.count(1, 1))
                nc.vector.tensor_scalar(r.scores[:, bass.ds(b.count(2 * EXPERTS, 0), 2 * EXPERTS)],
                                        c.bank[2 + b.off % 2][:, 0:2 * EXPERTS], 1.0 / W_SCALE, None,
                                        ALU.mult).then_inc(stored, 1)

            over_steps(dve, 1, (rows, split, finish))

        @block.scalar
        def _(act):
            def affine(b, s):
                if s != -1:
                    return
                i = b.off % 2
                act.wait_ge(turned, b.count(1, 1))
                wait(act, lo_done, b.count(1, -1))
                for d in range(DC):
                    last = nc.scalar.activation(xf[i][:, d, :], c.bank[i][:, d * SEQ:(d + 1) * SEQ], ACT.Identity,
                                                bias=shift[:, d:d + 1], scale=gain[:, d:d + 1])
                last.then_inc(copied, 1)

            act.wait_ge(loaded, 32)
            over_steps(act, 1, (affine,))

        @block.tensor
        def _(pe):
            w = lambda d: tuple(c.arena[slot][:, k, weight_off + d * EXPERTS:weight_off + (d + 1) * EXPERTS]
                                for k in range(2))

            def multiply(b, s):
                if s != 0:
                    return
                i = b.off % 2
                pe.wait_ge(lo_done, b.count(1, 1))
                wait(pe, stored, b.count(1, -1))
                for t in range(2):
                    for d in range(DC):
                        last = three_products(nc, c.bank[2 + i][:, t * EXPERTS:(t + 1) * EXPERTS],
                                              [x[:, d, t * P:(t + 1) * P] for x in xt[i]], w(d), d == 0, d == DC - 1)
                last.then_inc(product, 1)

            def turn(b, s):
                if s != -1:
                    return
                i = b.off % 2
                pe.wait_ge(rows_ready, b.count(1, 1))
                wait(pe, copied, b.count(1, -1))
                for d in range(DC):
                    for t in range(2):
                        last = nc.tensor.transpose(c.bank[i][:, d * SEQ + t * P:d * SEQ + (t + 1) * P],
                                                   xn[i][:, t, d * P:(d + 1) * P], c.ident[:])
                last.then_inc(turned, 1)

            over_steps(pe, 1, (turn, multiply))


class Steps:

    def __init__(self, eng, sem):
        self.eng, self.sem, self.n = eng, sem, 0

    def __call__(self, ins):
        ins.then_inc(self.sem, 1)
        self.n += 1
        self.eng.wait_ge(self.sem, self.n)


class Routing:

    def __init__(self, nc, ctx, tag):
        sb = lambda n, sh, dt: ctx.enter_context(nc.sbuf_tensor(f"{tag}_{n}", sh, dt))
        self.scores = sb("scores", [P, FLAGS], F32)
        self.flags = sb("flags", [P, FLAGS], F32)
        self.flags_h = sb("flags_h", [P, FLAGS], F16)
        self.prefix = sb("prefix", [P, FLAGS], F32)
        self.total = sb("total", [P, EXPERTS], F32)
        self.t = [sb(f"route_tmp{i}", [P, FLAGS], F32) for i in range(4)]
        self.s = [sb(f"route_small{i}", [P, TILES], F32) for i in range(4)]
        self.low, self.high, self.top = (sb(n, [P, EXPERTS], F32) for n in ("low", "high", "top_score"))
        self.slot_of = sb("slot_of", [P, FLAGS], F32)
        self.weight_of = sb("weight_of", [P, FLAGS], F32)
        self.slots = 2 * PICK_STEPS
        self.slot_token = sb("slot_token", [P, self.slots], I32)
        self.slot_weight = sb("slot_weight", [P, self.slots], F32)
        self.step_expert = sb("step_expert", [P, PICK_STEPS], I32)
        self.order = sb("order", [P, EXPERTS], F32)
        self.ones = sb("route_ones", [P, P], F16)
        self.before = sb("before", [P, P], F16)
        self.count = sb("count", [P, P], F32)
        self.lane = sb("lane", [P, 1], F32)
        self.pad_token = sb("pad_token", [P, 1], F32)
        self.rows = nc.dram_tensor(f"{tag}_rows_to_gather", (TOKENS + P, DIM), F32, kind="Internal").ap()
        self.total_rows = nc.dram_tensor(f"{tag}_rows_to_add_to", (TOKENS + P, DIM), F32, kind="Internal").ap()


def make_routing(nc, c, ctx, tag):
    r = Routing(nc, ctx, tag)
    with ExitStack() as inner:
        sem = inner.enter_context(stage_semaphores(nc, f"{tag}_constants"))
        step, loaded, padded = sem("step"), sem("loaded"), sem("padded")
        block = inner.enter_context(nc.Block())

        @block.sync
        def _(sp):
            sp.dma_start(r.count[:], c.dram["count"].partition_broadcast(P)).then_inc(loaded, 16)
            sp.dma_start(r.lane[:], c.dram["lane"]).then_inc(loaded, 16)

        @block.vector
        def _(dve):
            dve.wait_ge(loaded, 32)
            nc.vector.tensor_scalar(r.pad_token[:], r.lane[:], float(TOKENS + P), None, ALU.add).then_inc(padded, 1)

        @block.gpsimd
        def _(pool):
            did = Steps(pool, step)
            for e in range(EXPERTS):
                did(nc.gpsimd.memset(r.order[:, e:e + 1], float(EXPERTS - e)))
            did(nc.gpsimd.memset(r.ones[:], 1.0))
            did(nc.gpsimd.memset(r.before[:], 1.0))
            did(nc.gpsimd.affine_select(out=r.before[:], in_=r.before[:], compare_op=ALU.is_ge, fill=0.0,
                                        base=-1, pattern=[[1, P]], channel_multiplier=-1))
    return r


FLOOR = 1.5 * 2.0 ** 23


def floor_over(nc, did, out, x, n, add=0):
    did(nc.vector.tensor_scalar(out, x, 1.0 / n, (add - (n - 1) / 2) / n, ALU.mult, ALU.add))
    did(nc.vector.tensor_scalar(out, out, FLOOR, None, ALU.add))
    did(nc.vector.tensor_scalar(out, out, FLOOR, None, ALU.subtract))


def place_picked(nc, c, r, tag):
    with ExitStack() as ctx:
        sb = lambda n: ctx.enter_context(nc.sbuf_tensor(f"{tag}_{n}", [P, EXPERTS], F32))
        steps, end, more = sb("steps"), sb("end"), sb("more")
        reached = ctx.enter_context(nc.sbuf_tensor(f"{tag}_reached", [P, PICK_STEPS, EXPERTS], F32))
        passed = ctx.enter_context(nc.sbuf_tensor(f"{tag}_passed", [P, PICK_STEPS], F32))
        step = ctx.enter_context(stage_semaphores(nc, tag))("step")
        block = ctx.enter_context(nc.Block())

        @block.vector
        def _(dve):
            did = Steps(dve, step)
            tt = lambda out, a, b, op: did(nc.vector.tensor_tensor(out, a, b, op))
            floor_over(nc, did, steps[:], r.total[:], STEP_ROWS, STEP_ROWS - 1)
            a, b = end, more
            did(nc.vector.tensor_copy(a[:], steps[:]))
            for k in (1, 2, 4):
                tt(b[:, k:], a[:, k:], a[:, 0:EXPERTS - k], ALU.add)
                did(nc.vector.tensor_copy(b[:, 0:k], a[:, 0:k]))
                a, b = b, a
            tt(reached[:], r.count[:, 0:PICK_STEPS].unsqueeze(2).broadcast_to([P, PICK_STEPS, EXPERTS]),
               a[:].unsqueeze(1).broadcast_to([P, PICK_STEPS, EXPERTS]), ALU.is_ge)
            did(nc.vector.tensor_reduce(passed[:], reached[:], AX.X, ALU.add))
            did(nc.vector.tensor_scalar(r.step_expert[:], passed[:], float(EXPERTS - 1), None, ALU.min))
            tt(steps[:], a[:], steps[:], ALU.subtract)
            did(nc.vector.tensor_scalar(steps[:], steps[:], float(STEP_ROWS), None, ALU.mult))
            tt(tiled(r.prefix[:]), tiled(r.prefix[:]), over_tiles(steps[:]), ALU.add)
            for k in range(PICKED):
                tt(r.t[0][:], r.prefix[:], r.t[2 + k][:], ALU.mult)
                did(nc.vector.tensor_reduce(r.slot_of[:, k * TILES:(k + 1) * TILES], tiled(r.t[0][:]), AX.X, ALU.add))


def place_top(nc, c, r, tag):
    with ExitStack() as ctx:
        step = ctx.enter_context(stage_semaphores(nc, tag))("step")
        block = ctx.enter_context(nc.Block())

        @block.vector
        def _(dve):
            did = Steps(dve, step)
            did(nc.vector.tensor_scalar(r.t[0][:], r.prefix[:], 1.0, None, ALU.add))
            did(nc.vector.tensor_tensor(r.t[1][:], r.t[0][:], r.flags[:], ALU.mult))
            did(nc.vector.tensor_scalar(r.slot_of[:].rearrange("p (e t) -> p e t", e=EXPERTS), by_expert(r.t[1][:]),
                                        -1.0, None, ALU.add))


def slot_tables(nc, c, r, tag, choices, columns, spread, gate):
    group = 8
    values = 4
    n_groups = choices * TILES // group
    n = choices * TILES
    regions = choices if spread else 1
    width = values * columns
    with ExitStack() as ctx:
        sb = lambda nm, sh, dt: ctx.enter_context(nc.sbuf_tensor(f"{tag}_{nm}", sh, dt))
        sem = ctx.enter_context(stage_semaphores(nc, tag))
        col, lane = sb("col", [P, n], F32), sb("slot_lane", [P, n], F32)
        value = sb("value", [P, n, values], F32)
        half = sb("half", [P, n], F16)
        hit_col = [sb(f"hit_col{i}", [P, group, columns], F32) for i in range(2)]
        moving = [sb(f"moving{i}", [P, group, values, columns], F16) for i in range(2)]
        hit_lane = [sb(f"hit_lane{i}", [P, group, P], F16) for i in range(2)]
        table = sb("table", [P, regions * width], F32)
        tok, pad = sb("tok", [P, regions * columns], F32), sb("pad", [P, regions * columns], F32)
        step, ready, used = sem("step"), sem("ready"), sem("used")
        block = ctx.enter_context(nc.Block())

        @block.vector
        def _(dve):
            did = Steps(dve, step)
            tt = lambda out, a, b, op: did(nc.vector.tensor_tensor(out, a, b, op))
            slot, weight = r.slot_of[:, 0:n], r.weight_of[:, 0:n]
            floor_over(nc, did, col[:], slot, P)
            did(nc.vector.scalar_tensor_tensor(out=lane[:], in0=col[:], scalar=-float(P), in1=slot, op0=ALU.mult, op1=ALU.add))
            tiles = r.count[:, 1:TILES + 1].unsqueeze(1).broadcast_to([P, choices, TILES])
            did(nc.vector.tensor_copy(value[:, :, 0].rearrange("p (k t) -> p k t", t=TILES), tiles))
            did(nc.vector.tensor_copy(value[:, :, 1], r.lane[:].broadcast_to([P, n])))
            did(nc.vector.tensor_scalar(value[:, :, 3], weight, WEIGHT_UP, None, ALU.mult))
            did(nc.vector.tensor_copy(half[:], value[:, :, 3]))
            did(nc.vector.tensor_copy(value[:, :, 2], half[:]))
            tt(value[:, :, 3], value[:, :, 3], value[:, :, 2], ALU.subtract)
            for g in range(n_groups):
                i, at = g % 2, slice(g * group, (g + 1) * group)
                wait(dve, used, g - 1)
                over = lambda x, w: x[:, at].unsqueeze(2).broadcast_to([P, group, w])
                counting = lambda w: r.count[:, 0:w].unsqueeze(1).broadcast_to([P, group, w])
                tt(hit_col[i][:], counting(columns), over(col, columns), ALU.is_equal)
                nc.vector.tensor_tensor(hit_lane[i][:], counting(P), over(lane, P), ALU.is_equal).then_inc(ready, 1)
                nc.vector.tensor_tensor(moving[i][:], hit_col[i][:].unsqueeze(2).broadcast_to([P, group, values, columns]),
                                        value[:, at, :].unsqueeze(3).broadcast_to([P, group, values, columns]),
                                        ALU.mult).then_inc(ready, 1)
            dve.wait_ge(used, n_groups)
            did(nc.vector.tensor_copy(table[:], c.bank[0][:, 0:regions * width]))
            part = lambda v: table[:].rearrange("p (k v c) -> p k v c", k=regions, v=values)[:, :, v, :]
            flat = lambda x: x.rearrange("p (k c) -> p k c", k=regions)
            m = regions * columns
            did(nc.vector.scalar_tensor_tensor(out=flat(tok[:]), in0=part(0), scalar=float(P), in1=part(1),
                                               op0=ALU.mult, op1=ALU.add))
            did(nc.vector.tensor_scalar(flat(pad[:]), part(0), 0.0, r.pad_token[:, 0:1], ALU.is_equal, ALU.mult))
            did(nc.vector.scalar_tensor_tensor(out=r.slot_token[:, 0:m], in0=tok[:], scalar=-float(P), in1=pad[:],
                                               op0=ALU.add, op1=ALU.add))
            tt(flat(tok[:]), part(2), part(3), ALU.add)
            did(nc.vector.tensor_scalar(r.slot_weight[:, 0:m], tok[:], 1.0 / WEIGHT_UP / W_SCALE,
                                        c.gates[:, gate:gate + 1], ALU.mult, ALU.mult))

        @block.tensor
        def _(pe):
            for g in range(n_groups):
                i = g % 2
                pe.wait_ge(ready, 2 * g + 2)
                for j in range(group):
                    t = g * group + j
                    k = t // TILES if spread else 0
                    first, final = (t % TILES == 0, t % TILES == TILES - 1) if spread else (t == 0, t == n - 1)
                    last = nc.tensor.matmul(c.bank[0][:, k * width:(k + 1) * width], hit_lane[i][:, j, :],
                                            moving[i][:, j].rearrange("p v c -> p (v c)"), start=first, stop=final)
                last.then_inc(used, 1)


def prefix_counts(nc, r, c, tag):
    with ExitStack() as ctx:
        sem = ctx.enter_context(stage_semaphores(nc, tag))
        halved, counted, step = sem("halved"), sem("counted"), sem("step")
        block = ctx.enter_context(nc.Block())
        within, totals = c.bank[0][:, 0:FLAGS], c.bank[1][:, 0:FLAGS]

        @block.vector
        def _(dve):
            did = Steps(dve, step)
            nc.vector.tensor_copy(r.flags_h[:], r.flags[:]).then_inc(halved, 1)
            dve.wait_ge(counted, 2)
            a, b = r.t[0], r.t[1]
            did(nc.vector.tensor_copy(a[:], totals))
            for k in (1, 2, 4, 8, 16):
                w = k * EXPERTS
                did(nc.vector.tensor_tensor(b[:, w:], a[:, w:], a[:, 0:FLAGS - w], ALU.add))
                did(nc.vector.tensor_copy(b[:, 0:w], a[:, 0:w]))
                a, b = b, a
            did(nc.vector.tensor_copy(r.total[:], a[:, FLAGS - EXPERTS:]))
            did(nc.vector.tensor_tensor(b[:], a[:], totals, ALU.subtract))
            did(nc.vector.tensor_tensor(r.prefix[:], b[:], within, ALU.add))

        @block.tensor
        def _(pe):
            pe.wait_ge(halved, 1)
            nc.tensor.matmul(within, r.before[:], r.flags_h[:], start=True, stop=True).then_inc(counted, 1)
            nc.tensor.matmul(totals, r.ones[:], r.flags_h[:], start=True, stop=True).then_inc(counted, 1)


def pick_two(nc, c, r, tag):
    with ExitStack() as ctx:
        sem = ctx.enter_context(stage_semaphores(nc, tag))
        step, gap_ready, exp_done = sem("step"), sem("gap_ready"), sem("exp_done")
        block = ctx.enter_context(nc.Block())

        @block.vector
        def _(dve):
            did = Steps(dve, step)
            tt = lambda out, a, b, op: did(nc.vector.tensor_tensor(out, a, b, op))
            left, one = r.t[0], r.t[1]
            for k in range(PICKED):
                src, flag, top = (r.scores, left)[k], r.t[2 + k], r.s[k]
                did(nc.vector.tensor_reduce(top[:], tiled(src[:]), AX.X, ALU.max))
                tt(tiled(one[:]), tiled(src[:]), over_experts(top[:]), ALU.is_equal)
                tt(tiled(one[:]), tiled(one[:]), over_tiles(r.order[:]), ALU.mult)
                did(nc.vector.tensor_reduce(r.s[2][:], tiled(one[:]), AX.X, ALU.max))
                tt(tiled(flag[:]), tiled(one[:]), over_experts(r.s[2][:]), ALU.is_equal)
                if k == 0:
                    did(nc.vector.scalar_tensor_tensor(out=left[:], in0=flag[:], scalar=NEG_BIG, in1=r.scores[:],
                                                       op0=ALU.mult, op1=ALU.add))
            nc.vector.tensor_tensor(r.s[2][:], r.s[1][:], r.s[0][:], ALU.subtract).then_inc(gap_ready, 1)
            dve.wait_ge(exp_done, 1)
            did(nc.vector.tensor_scalar(r.s[2][:], r.s[3][:], 1.0, None, ALU.add))
            did(nc.vector.reciprocal(r.s[0][:], r.s[2][:]))
            tt(r.s[1][:], r.s[0][:], r.s[3][:], ALU.mult)
            did(nc.vector.tensor_copy(r.weight_of[:, 0:TILES], r.s[0][:]))
            did(nc.vector.tensor_copy(r.weight_of[:, TILES:2 * TILES], r.s[1][:]))
            tt(r.flags[:], r.t[2][:], r.t[3][:], ALU.add)

        @block.scalar
        def _(act):
            act.wait_ge(gap_ready, 1)
            nc.scalar.activation(r.s[3][:], r.s[2][:], ACT.Exp).then_inc(exp_done, 1)


def find_thresholds(nc, c, r, tag):
    with ExitStack() as ctx:
        sb = lambda n: ctx.enter_context(nc.sbuf_tensor(f"{tag}_{n}", [P, EXPERTS], F32))
        sem = ctx.enter_context(stage_semaphores(nc, tag))
        bound, middle, stride, over, big, out_of_reach, raised = (
            sb(n) for n in ("bound", "middle", "stride", "over", "big", "out_of_reach", "raised"))
        counts = ctx.enter_context(nc.sbuf_tensor(f"{tag}_counts", [P, EXPERTS], F16))
        step, reduced, prepared, bisect, counted, summed = (
            sem(n) for n in ("step", "reduced", "prepared", "bisect", "counted", "summed"))
        block = ctx.enter_context(nc.Block())
        chain = 8

        @block.gpsimd
        def _(pool):
            nc.gpsimd.partition_all_reduce(r.t[0][:], r.scores[:], P, bass.bass_isa.ReduceOp.absmax).then_inc(reduced, 1)
            nc.gpsimd.partition_all_reduce(r.t[1][:], r.scores[:], P, bass.bass_isa.ReduceOp.max).then_inc(reduced, 1)

        @block.vector
        def _(dve):
            did = Steps(dve, step)
            dve.wait_ge(reduced, 2)
            did(nc.vector.tensor_reduce(bound[:], by_expert(r.t[0][:]), AX.X, ALU.max))
            did(nc.vector.tensor_reduce(r.top[:], by_expert(r.t[1][:]), AX.X, ALU.max))
            did(nc.vector.tensor_scalar(r.low[:], bound[:], -1.0, None, ALU.mult))
            did(nc.vector.tensor_scalar(r.high[:], bound[:], 0.0, -NEG_BIG, ALU.mult, ALU.add))
            did(nc.vector.tensor_scalar(big[:], bound[:], 0.0, -NEG_BIG, ALU.mult, ALU.add))
            did(nc.vector.tensor_copy(raised[:], big[:]))
            did(nc.vector.tensor_copy(stride[:], bound[:]))
            with dve.Fori(0, BISECTIONS) as i:
                n = 0

                def then(ins, hold=True):
                    nonlocal n
                    n += 1
                    ins.then_inc(bisect, 1)
                    if hold:
                        dve.wait_ge(bisect, i * chain + n)

                then(nc.vector.tensor_tensor(middle[:], r.low[:], stride[:], ALU.add))
                then(nc.vector.tensor_tensor(tiled(r.flags[:]), tiled(r.scores[:]), over_tiles(middle[:]), ALU.is_ge))
                with nc.allow_low_precision(reason="counts up to 32 are exact in float16"):
                    nc.vector.tensor_reduce(counts[:], by_expert(r.flags[:]), AX.X, ALU.add).then_inc(counted, 1)
                then(nc.vector.tensor_tensor(r.high[:], r.high[:], raised[:], ALU.min), hold=False)
                dve.wait_ge(summed, i + 1)
                total = c.bank[0][:, 0:EXPERTS]
                then(nc.vector.scalar_tensor_tensor(out=over[:], in0=total, scalar=float(CAPACITY), in1=stride[:],
                                                    op0=ALU.is_ge, op1=ALU.mult), hold=False)
                then(nc.vector.scalar_tensor_tensor(out=out_of_reach[:], in0=total, scalar=float(CAPACITY), in1=big[:],
                                                    op0=ALU.is_ge, op1=ALU.mult))
                then(nc.vector.tensor_tensor(r.low[:], r.low[:], over[:], ALU.add), hold=False)
                then(nc.vector.tensor_scalar(stride[:], stride[:], 0.5, None, ALU.mult), hold=False)
                then(nc.vector.tensor_tensor(raised[:], out_of_reach[:], middle[:], ALU.add))
            did(nc.vector.tensor_tensor(r.high[:], r.high[:], raised[:], ALU.min))

        @block.tensor
        def _(pe):
            with pe.Fori(0, BISECTIONS) as i:
                pe.wait_ge(counted, i + 1)
                nc.tensor.matmul(c.bank[0][:, 0:EXPERTS], r.ones[:], counts[:], start=True, stop=True).then_inc(summed, 1)


def flag_ties(nc, c, r, tag):
    with ExitStack() as ctx:
        step = ctx.enter_context(stage_semaphores(nc, tag))("step")
        block = ctx.enter_context(nc.Block())

        @block.vector
        def _(dve):
            did = Steps(dve, step)
            did(nc.vector.tensor_tensor(tiled(r.t[0][:]), tiled(r.scores[:]), over_tiles(r.low[:]), ALU.is_ge))
            did(nc.vector.tensor_tensor(tiled(r.t[2][:]), tiled(r.scores[:]), over_tiles(r.high[:]), ALU.is_ge))
            did(nc.vector.tensor_tensor(r.flags[:], r.t[0][:], r.t[2][:], ALU.subtract))


def take_top(nc, c, r, tag):
    with ExitStack() as ctx:
        sb = lambda n: ctx.enter_context(nc.sbuf_tensor(f"{tag}_{n}", [P, EXPERTS], F32))
        sem = ctx.enter_context(stage_semaphores(nc, tag))
        above, room, sums, total = sb("above"), sb("room"), sb("sums"), sb("sums_all")
        above_all = sb("above_all")
        step, above_ready, above_summed = sem("step"), sem("above_ready"), sem("above_summed")
        gap_ready, exp_done, sums_ready, sums_done = sem("gap_ready"), sem("exp_done"), sem("sums_ready"), sem("sums_done")
        block = ctx.enter_context(nc.Block())

        @block.vector
        def _(dve):
            did = Steps(dve, step)
            tt = lambda out, a, b, op: did(nc.vector.tensor_tensor(out, a, b, op))
            nc.vector.tensor_reduce(above[:], by_expert(r.t[2][:]), AX.X, ALU.add).then_inc(above_ready, 1)
            nc.vector.tensor_tensor(tiled(r.t[0][:]), tiled(r.scores[:]), over_tiles(r.top[:]),
                                    ALU.subtract).then_inc(gap_ready, 1)
            dve.wait_ge(above_summed, 1)
            did(nc.vector.tensor_scalar(room[:], above_all[:], -1.0, float(CAPACITY), ALU.mult, ALU.add))
            tt(tiled(r.t[3][:]), tiled(r.prefix[:]), over_tiles(room[:]), ALU.is_lt)
            tt(r.t[3][:], r.t[3][:], r.flags[:], ALU.mult)
            tt(r.flags[:], r.t[3][:], r.t[2][:], ALU.add)
            dve.wait_ge(exp_done, 1)
            tt(r.t[0][:], r.t[1][:], r.flags[:], ALU.mult)
            nc.vector.tensor_reduce(sums[:], by_expert(r.t[0][:]), AX.X, ALU.add).then_inc(sums_ready, 1)
            dve.wait_ge(sums_done, 1)
            did(nc.vector.reciprocal(room[:], total[:]))
            tt(r.weight_of[:].rearrange("p (e t) -> p e t", e=EXPERTS), by_expert(r.t[0][:]),
               room[:].unsqueeze(2).broadcast_to([P, EXPERTS, TILES]), ALU.mult)

        @block.gpsimd
        def _(pool):
            pool.wait_ge(above_ready, 1)
            nc.gpsimd.partition_all_reduce(above_all[:], above[:], P, bass.bass_isa.ReduceOp.add).then_inc(above_summed, 1)
            pool.wait_ge(sums_ready, 1)
            nc.gpsimd.partition_all_reduce(total[:], sums[:], P, bass.bass_isa.ReduceOp.add).then_inc(sums_done, 1)

        @block.scalar
        def _(act):
            act.wait_ge(gap_ready, 1)
            nc.scalar.activation(r.t[1][:], r.t[0][:], ACT.Exp).then_inc(exp_done, 1)


def add_h(nc, c, tag, gate):
    with ExitStack() as ctx:
        added = ctx.enter_context(stage_semaphores(nc, tag))("added")
        block = ctx.enter_context(nc.Block())

        @block.vector
        def _(dve):
            for t in range(0, TILES, 8):
                nc.vector.scalar_tensor_tensor(out=c.x[:, t:t + 8, :], in0=c.h[:, t:t + 8, :],
                                               scalar=c.gates[:, gate:gate + 1], in1=c.x[:, t:t + 8, :],
                                               op0=ALU.mult, op1=ALU.add).then_inc(added, 1)


def store_result(nc, c, out):
    with ExitStack() as ctx:
        stored = ctx.enter_context(nc.semaphore("stored"))
        block = ctx.enter_context(nc.Block())

        @block.sync
        def _(sp):
            sp.dma_start(out.rearrange("b (t p) d -> p (b t) d", p=P), c.x[:]).then_inc(stored, 16)
            sp.wait_ge(stored, 16)


def build_program(nc, dram, out, first=0, last=8):
    with ExitStack() as ctx:
        c = setup_core(nc, ctx, dram)
        w = {}
        for name, slot in (("l0x", 0), ("l0s", 1), ("l1x", 0), ("l2x", 0), ("l3x", 1), ("l3g", 0), ("l3f", 1)):
            rows = dram.get(f"r_{name}")
            w[name] = Weights(nc, ctx, c, name, slot, dram[f"w_{name}"], rows, (W_SCALE,) * 3 + (W_SCALE ** 2,))
        e0 = ExpertWeights(nc, ctx, "l0e", dram["w_l0e"], 6)
        e2 = ExpertWeights(nc, ctx, "l2e", dram["w_l2e"], 4)
        c.first_weights = {0: w["l0x"], 1: w["l0s"], 2: w["l1x"], 3: None, 4: w["l2x"], 5: w["l2x"], 6: w["l3x"], 7: w["l3f"]}[first]
        prepare(nc, c)
        for stage in range(first, last):
            if stage == 0:
                norm_stats(nc, c, "n0", have_stats=True)
                attention(nc, c, Attention("a0", "cross16", w["l0x"], gate=0, add_mask=dram["mask_t"], biased=True), w["l0s"], e0)
            if stage == 1:
                norm_stats(nc, c, "n1", second=2)
                a1 = Attention("a1", "self16", w["l0s"], affine=True, store="h+")
                a1.norm_g, a1.norm_b = dram["l0_g1"], dram["zeros"]
                attention(nc, c, a1, None)
                with ExitStack() as stage_ctx:
                    r = make_routing(nc, c, stage_ctx, "m1")
                    norm_rows_of_h(nc, c, "m1n")
                    add_h(nc, c, "m1a", 4)
                    gain = dict(norm_g=dram["l0_g2"], norm_b=dram["zeros"])
                    router_scores(nc, c, r, "m1s", "h", 2048, 1, next_weights=w["l1x"], parts=range(WEIGHT_PARTS // 2), **gain)
                    pick_two(nc, c, r, "m1p")
                    prefix_counts(nc, r, c, "m1c")
                    place_picked(nc, c, r, "m1l")
                    slot_tables(nc, c, r, "m1t", PICKED, 2 * PICK_STEPS, False, 4)
                    gated_ff(nc, c, GatedFf("m1", 6, experts=e0, steps=PICK_STEPS, dynamic=True, **gain),
                             next_weights=w["l1x"], r=r)
            if stage == 2:
                norm_stats(nc, c, "n2", have_stats=first <= 2)
                attention(nc, c, Attention("a2", "cross64", w["l1x"], gate=1, biased=True), None, e2)
            if stage == 3:
                norm_stats(nc, c, "n3")
                quantized_linear(nc, c, "q3", 5, w["l2x"])
            if stage == 4:
                norm_stats(nc, c, "n4")
                attention(nc, c, Attention("a4", "cross16", w["l2x"], gate=2, clip_mask=dram["mask_rows"], biased=True), None)
            if stage == 5:
                norm_stats(nc, c, "n5")
                with ExitStack() as stage_ctx:
                    r = make_routing(nc, c, stage_ctx, "m5")
                    gain = dict(norm_g=dram["ones"], norm_b=dram["zeros"])
                    router_scores(nc, c, r, "m5s", "x", 2048, 0, next_weights=w["l3x"], **gain)
                    find_thresholds(nc, c, r, "m5t")
                    flag_ties(nc, c, r, "m5f")
                    prefix_counts(nc, r, c, "m5c")
                    take_top(nc, c, r, "m5p")
                    prefix_counts(nc, r, c, "m5d")
                    place_top(nc, c, r, "m5l")
                    slot_tables(nc, c, r, "m5u", EXPERTS, CAPACITY // P, True, 6)
                    gated_ff(nc, c, GatedFf("m5", 4, experts=e2, steps=TOP_STEPS), r=r)
            if stage == 6:
                l3 = [dram["l3_" + k] for k in ("ln_g", "ln_b", "cln_g", "cln_b")]
                norm_context(nc, c, "c6", l3[2], l3[3])
                norm_stats(nc, c, "n6", second=0, have_stats=True)
                a6 = Attention("a6", "cross64", w["l3x"], shared_kv=True, affine=True, store="h")
                a6.norm_g, a6.norm_b = l3[0], l3[1]
                attention(nc, c, a6, w["l3g"])
                gated_ff(nc, c, GatedFf("g6", 8, weights=w["l3g"], gate=3, norm_g=l3[0], norm_b=l3[1]), w["l3f"])
            if stage == 7:
                norm_stats(nc, c, "n7")
                scaled_linear(nc, c, "f7", 7, w["l3f"])
        store_result(nc, c, out)


def _by_chunk(w):
    k, n = w.shape
    return w.reshape(k // P, P, n).transpose(1, 0, 2).reshape(P, -1)


def _rotary_tables(length, dim):
    inv_freq = 1.0 / 10000.0 ** (np.arange(0, dim, 2, dtype=np.float32) / dim)
    freqs = np.einsum("i,j->ij", np.arange(length, dtype=np.float32), inv_freq)
    cos, sin = np.cos(freqs), np.sin(freqs)
    return np.concatenate([cos, cos], -1).astype(np.float32), np.concatenate([-sin, sin], -1).astype(np.float32)


def _layout(i):
    cat = lambda *w: np.ascontiguousarray(np.concatenate([_by_chunk(x) for x in w], axis=1))
    d = {k: i[k] for k in ("x", "ctx_1024", "g_xattn", "g_ffn")}
    d["w_l0x"] = cat(*(i["L0_xattn_W" + k].T for k in "qkvo"))
    d["r_l0x"] = np.concatenate([i["L0_xattn_b" + k] for k in "qkvo"]).reshape(1, -1)
    d["w_l0s"] = cat(*(i["L0_ffn_w" + k] for k in ("q", "k", "v", "o", "_router")))
    columns = lambda v: np.ascontiguousarray(v.reshape(DC, P).T)
    d["l0_g1"], d["l0_g2"] = columns(i["L0_ffn_g1"]), columns(i["L0_ffn_g2"])
    for k in ("ln_g", "ln_b", "cln_g", "cln_b"):
        d["l3_" + k] = columns(i["L3_xattn_" + k])
    pad = lambda a, axis: np.concatenate([a, np.zeros([6 * P - a.shape[axis] if k == axis else n for k, n in enumerate(a.shape)],
                                                      a.dtype)], axis=axis)
    d["w_l0e"] = np.concatenate([cat(np.concatenate([pad(i["L0_ffn_wu"][e], 1), pad(i["L0_ffn_wg"][e], 1)], 1),
                                     pad(i["L0_ffn_wd"][e], 0)) for e in range(EXPERTS)], 1)
    d["w_l2e"] = np.concatenate([cat(np.concatenate([i["L2_ffn_W3"][e].T, i["L2_ffn_W1"][e].T], 1),
                                     i["L2_ffn_W2"][e].T) for e in range(EXPERTS)], 1)
    d["count"], d["lane"] = np.arange(P, dtype=np.float32), np.arange(P, dtype=np.float32).reshape(P, 1)
    d["ones"] = np.ones((P, DC), np.float32)
    d["zeros"] = np.zeros((P, DC), np.float32)
    cos, sin = _rotary_tables(SEQ, DIM // HEADS)
    rows = lambda t: np.ascontiguousarray(t.reshape(2, P, -1).transpose(1, 0, 2))
    d["rope_cos"], d["rope_sin"] = rows(cos), rows(sin)
    d["w_l1x"] = cat(*(i["L1_xattn_W" + k] for k in "qkvo"))
    d["r_l1x"] = np.concatenate([np.zeros(3 * DIM, np.float32), i["L1_xattn_bo"]]).reshape(1, -1)
    d["l1f_w"] = np.ascontiguousarray(i["L1_ffn_weight_q"].T.reshape(DC, P, DIM).transpose(1, 0, 2)).view(np.int32)
    d["l1f_scale"], d["l1f_bias"] = i["L1_ffn_weight_scale"], i["L1_ffn_bias"]
    d["w_l2x"] = cat(*(i["L2_xattn_w" + k].T for k in "qkvo"), i["L2_ffn_Wg"].T)
    d["r_l2x"] = np.concatenate([i["L2_xattn_b" + k] for k in "qkvo"]).reshape(1, -1)
    k_w, v_w = i["L3_xattn_Wkv"][:, :64], i["L3_xattn_Wkv"][:, 64:]
    d["w_l3x"] = cat(i["L3_xattn_Wq"], np.concatenate([k_w, k_w], axis=1), v_w, i["L3_xattn_Wo"])
    d["w_l3g"] = cat(i["L3_xattn_Wff1"], i["L3_xattn_Wff2"])
    d["w_l3f"] = cat(i["L3_ffn_CB"].T)
    d["l3f_scale"], d["l3f_bias"] = i["L3_ffn_SCB"], i["L3_ffn_bias"]
    d["mask_rows"] = np.ascontiguousarray(i["mask_Bx1xSxS2_ik1"].reshape(BATCH, 2, P, KEYS).transpose(0, 2, 1, 3))
    d["mask_t"] = np.ascontiguousarray(i["mask_BxS2_ik1"].T)
    return d


def kernel(**inputs):
    import concourse.bacc as _bacc
    from concourse.bass_utils import run_bass_kernel_spmd as _run

    nc = _bacc.Bacc("TRN2", target_bir_lowering=False, num_devices=1)
    arrays = _layout({k: np.asarray(v) for k, v in inputs.items()})
    dram = {k: nc.dram_tensor(f"in_{k}", a.shape, mybir.dt.from_np(a.dtype), kind="ExternalInput").ap()
            for k, a in arrays.items()}
    out = nc.dram_tensor("out_x", (BATCH, SEQ, DIM), F32, kind="ExternalOutput").ap()
    build_program(nc, dram, out)
    r = _run(nc, [{f"in_{k}": a for k, a in arrays.items()}], core_ids=[0])
    return r.results[0]["out_x"]
```
